# Optimizing a Trainium2 kernel written in Bass

```python
import numpy as np
import jax
import jax.numpy as jnp

def _softmax(x, axis=-1):
    return jax.nn.softmax(x, axis=axis)

def _gelu(x):
    return jax.nn.gelu(x, approximate=True)

def _silu(x):
    return jax.nn.silu(x)

def _sigmoid(x):
    return jax.nn.sigmoid(x)

def _layernorm(x, axis=-1, eps=1e-05):
    m = jnp.mean(x, axis=axis, keepdims=True)
    v = jnp.var(x, axis=axis, keepdims=True)
    return (x - m) / jnp.sqrt(v + eps)

def _scatter_add(tgt, idx, src, axis=0):
    return tgt.at[idx].add(src)

def _segment_sum(src, seg, n):
    return jax.ops.segment_sum(src, seg, n)
kernel_name = 'mk_flamingo_gated_d2_seqx_r8_5e9747'

def setup_inputs(seed: int=0):
    np.random.seed(seed)
    _w = jnp.asarray

    def _rec_inputs():
        import jax
        import jax.numpy as jnp
        _rk = jax.random.key(seed)
        x = -0.0002928 + 1 * jax.random.normal(jax.random.fold_in(_rk, 1), (8, 100, 128), jnp.float32)
        _lenS = 100 - jax.random.randint(jax.random.fold_in(_rk, 7), (8,), 0, max(1, 100 // 4) + 1, jnp.int32)
        _lenS2 = 1444 - jax.random.randint(jax.random.fold_in(_rk, 8), (8,), 0, max(1, 1444 // 4) + 1, jnp.int32)
        _ctx_1024P = jax.random.normal(jax.random.fold_in(_rk, 11), (8, 16, 128), jnp.float32)
        _ctx_1024c = jax.random.dirichlet(jax.random.fold_in(_rk, 511), 0.3 * jnp.ones((16,), jnp.float32), (8, 1444))
        _ctx_1024t = jnp.einsum('bsk,bkd->bsd', _ctx_1024c, _ctx_1024P)
        _ctx_1024t = _ctx_1024t * jax.lax.rsqrt(jnp.mean(jnp.square(_ctx_1024t)) + 1e-12) * 0.953939
        ctx_1024 = -1.39393e-06 + 0.999914 * (_ctx_1024t + 0.3 * jax.random.normal(jax.random.fold_in(_rk, 611), (8, 1444, 128), jnp.float32))
        _validS = jnp.arange(100)[None, :] < _lenS[:, None]
        _validS2 = jnp.arange(1444)[None, :] < _lenS2[:, None]
        _causal = jnp.tril(jnp.ones((100, 100), dtype=bool))
        mask_BxSxS2_bf1 = jnp.ones((8, 100, 1444), dtype=bool)
        _g = jax.random.normal(jax.random.fold_in(_rk, 9001), (2, 2), jnp.float32)
        _g = jnp.sign(_g) * jnp.maximum(jnp.abs(_g), 1.0) + (_g == 0) * 1.0
        g_xattn = _g[0]
        g_ffn = _g[1]
        return (x, ctx_1024, mask_BxSxS2_bf1, g_xattn, g_ffn)
    x, ctx_1024, mask_BxSxS2_bf1, g_xattn, g_ffn = _rec_inputs()

    def _L0_xattn_setup():
        import jax, jax.numpy as jnp
        import numpy as np
        D_MODEL = 128
        N_HEADS = 16
        HEAD = D_MODEL // N_HEADS
        D_FF = 512
        LN_EPS = 1e-05

        def _layernorm(x, g, b):
            mu = jnp.mean(x, axis=-1, keepdims=True)
            var = jnp.mean(jnp.square(x - mu), axis=-1, keepdims=True)
            return (x - mu) * jax.lax.rsqrt(var + LN_EPS) * g + b

        def _mha(q_in, k_in, v_in, Wq, Wk, Wv, bv, causal):
            q = jnp.einsum('bsd,hde->bhse', q_in, Wq)
            k = jnp.einsum('btd,hde->bhte', k_in, Wk)
            v = jnp.einsum('btd,hde->bhte', v_in, Wv) + bv[None, :, None, :]
            scale = HEAD ** (-0.5)
            scores = jnp.einsum('bhse,bhte->bhst', q, k) * scale
            if causal:
                S, T = (scores.shape[-2], scores.shape[-1])
                mask = jnp.tril(jnp.ones((S, T), dtype=bool))
                scores = jnp.where(mask, scores, -jnp.inf)
            p = jax.nn.softmax(scores, axis=-1)
            o = jnp.einsum('bhst,bhte->bhse', p, v)
            B, H, S, E = o.shape
            return o.transpose(0, 2, 1, 3).reshape(B, S, H * E)
        key = jax.random.key(seed)
        ks = jax.random.split(key, 20)
        B, S, T = (2, 256, 256)
        sd = D_MODEL ** (-0.5)
        inp = {'input_tensor': jax.random.normal(ks[0], (B, S, D_MODEL), jnp.float32), 'encoder_output': jax.random.normal(ks[1], (B, T, D_MODEL), jnp.float32), 'Wq1': jax.random.normal(ks[2], (N_HEADS, D_MODEL, HEAD), jnp.float32) * sd, 'Wk1': jax.random.normal(ks[3], (N_HEADS, D_MODEL, HEAD), jnp.float32) * sd, 'Wv1': jax.random.normal(ks[4], (N_HEADS, D_MODEL, HEAD), jnp.float32) * sd, 'bv1': jnp.zeros((N_HEADS, HEAD), jnp.float32), 'Wq2': jax.random.normal(ks[5], (N_HEADS, D_MODEL, HEAD), jnp.float32) * sd, 'Wk2': jax.random.normal(ks[6], (N_HEADS, D_MODEL, HEAD), jnp.float32) * sd, 'Wv2': jax.random.normal(ks[7], (N_HEADS, D_MODEL, HEAD), jnp.float32) * sd, 'bv2': jnp.zeros((N_HEADS, HEAD), jnp.float32), 'g1': jnp.ones((D_MODEL,), jnp.float32), 'be1': jnp.zeros((D_MODEL,), jnp.float32), 'g2': jnp.ones((D_MODEL,), jnp.float32), 'be2': jnp.zeros((D_MODEL,), jnp.float32), 'g3': jnp.ones((D_MODEL,), jnp.float32), 'be3': jnp.zeros((D_MODEL,), jnp.float32), 'Wf1': jax.random.normal(ks[8], (D_MODEL, D_FF), jnp.float32) * sd, 'bf1': jnp.zeros((D_FF,), jnp.float32), 'Wf2': jax.random.normal(ks[9], (D_FF, D_MODEL), jnp.float32) * D_FF ** (-0.5), 'bf2': jnp.zeros((D_MODEL,), jnp.float32)}
        return inp
    _L0_xattn_all = _L0_xattn_setup()
    _L0_xattn_in = {k: v for k, v in _L0_xattn_all.items() if k in ('Wq1', 'Wk1', 'Wv1', 'bv1', 'Wq2', 'Wk2', 'Wv2', 'bv2', 'g1', 'be1', 'g2', 'be2', 'g3', 'be3', 'Wf1', 'bf1', 'Wf2', 'bf2')}
    del _L0_xattn_all

    def _L0_ffn_setup():
        import jax, jax.numpy as jnp
        import numpy as np
        B, S, D, F, E = (2, 256, 128, 512, 8)
        LN_EPS = 1e-05

        def _xavier(key, shape, fan_in, fan_out):
            a = np.sqrt(6.0 / (fan_in + fan_out))
            return jax.random.uniform(key, shape, jnp.float32, -a, a)
        key = jax.random.key(seed)
        ks = jax.random.split(key, 8)
        tgt = jax.random.normal(ks[0], (B, S, D), jnp.float32)
        router_w = _xavier(ks[1], (E, D), D, E)
        router_b = jnp.zeros((E,), jnp.float32)
        w1 = _xavier(ks[2], (E, D, F), D, F)
        b1 = jnp.zeros((E, F), jnp.float32)
        w2 = _xavier(ks[3], (E, F, D), F, D)
        b2 = jnp.zeros((E, D), jnp.float32)
        gamma = jnp.ones((D,), jnp.float32)
        beta = jnp.zeros((D,), jnp.float32)
        return {'tgt': tgt, 'router_w': router_w, 'router_b': router_b, 'w1': w1, 'b1': b1, 'w2': w2, 'b2': b2, 'gamma': gamma, 'beta': beta}
    _L0_ffn_all = _L0_ffn_setup()
    _L0_ffn_in = {k: v for k, v in _L0_ffn_all.items() if k in ('router_w', 'router_b', 'w1', 'b1', 'w2', 'b2', 'gamma', 'beta')}
    del _L0_ffn_all

    def _L1_xattn_setup():
        import jax, jax.numpy as jnp
        import numpy as np
        B, S, D = (2, 256, 128)
        H, DQK, DV, DOUT = (16, 64, 64, 128)
        key = jax.random.key(seed)
        ks = jax.random.split(key, 8)
        query = jax.random.normal(ks[0], (B, S, D), dtype=jnp.float32)
        k_in = jax.random.normal(ks[1], (B, S, D), dtype=jnp.float32)
        value = jax.random.normal(ks[2], (B, S, D), dtype=jnp.float32)
        mask = jnp.ones((B, S, S), dtype=bool)
        Wq = jax.random.normal(ks[3], (H, D, DQK), dtype=jnp.float32) * np.sqrt(2.0 / (D + DQK))
        Wk = jax.random.normal(ks[4], (H, D, DQK), dtype=jnp.float32) * np.sqrt(2.0 / (D + DQK))
        Wv = jax.random.normal(ks[5], (H, D, DV), dtype=jnp.float32) * np.sqrt(2.0 / (D + DV))
        Wo = jax.random.normal(ks[6], (H * DV, DOUT), dtype=jnp.float32) * np.sqrt(2.0 / (H * DV + DOUT))
        return {'query': query, 'key': k_in, 'value': value, 'mask': mask, 'Wq': Wq, 'Wk': Wk, 'Wv': Wv, 'Wo': Wo}
    _L1_xattn_all = _L1_xattn_setup()
    _L1_xattn_in = {k: v for k, v in _L1_xattn_all.items() if k in ('Wq', 'Wk', 'Wv', 'Wo')}
    del _L1_xattn_all

    def _L1_ffn_setup():
        import jax, jax.numpy as jnp
        import numpy as np
        N_EXPERTS = 8
        TOP_K = 2
        W_SCALE = 0.02
        key = jax.random.key(seed)
        ks = jax.random.split(key, 4)
        S, B, D, F = (256, 2, 128, 512)
        x = jax.random.normal(ks[0], (S, B, D), dtype=jnp.float32)
        gate_w = jax.random.normal(ks[1], (D, N_EXPERTS), dtype=jnp.float32) * W_SCALE
        gate_b = jnp.zeros((N_EXPERTS,), dtype=jnp.float32)
        w1 = jax.random.normal(ks[2], (N_EXPERTS, D, F), dtype=jnp.float32) * W_SCALE
        b1 = jnp.zeros((N_EXPERTS, F), dtype=jnp.float32)
        w2 = jax.random.normal(ks[3], (N_EXPERTS, F, D), dtype=jnp.float32) * W_SCALE
        b2 = jnp.zeros((N_EXPERTS, D), dtype=jnp.float32)
        return {'x': x, 'gate_w': gate_w, 'gate_b': gate_b, 'w1': w1, 'b1': b1, 'w2': w2, 'b2': b2}
    _L1_ffn_all = _L1_ffn_setup()
    _L1_ffn_in = {k: v for k, v in _L1_ffn_all.items() if k in ('gate_w', 'gate_b', 'w1', 'b1', 'w2', 'b2')}
    del _L1_ffn_all
    return {'x': x, 'ctx_1024': ctx_1024, 'mask_BxSxS2_bf1': mask_BxSxS2_bf1, 'g_xattn': g_xattn, 'g_ffn': g_ffn, 'L0_xattn_Wq1': _L0_xattn_in['Wq1'], 'L0_xattn_Wk1': _L0_xattn_in['Wk1'], 'L0_xattn_Wv1': _L0_xattn_in['Wv1'], 'L0_xattn_bv1': _L0_xattn_in['bv1'], 'L0_xattn_Wq2': _L0_xattn_in['Wq2'], 'L0_xattn_Wk2': _L0_xattn_in['Wk2'], 'L0_xattn_Wv2': _L0_xattn_in['Wv2'], 'L0_xattn_bv2': _L0_xattn_in['bv2'], 'L0_xattn_g1': _L0_xattn_in['g1'], 'L0_xattn_be1': _L0_xattn_in['be1'], 'L0_xattn_g2': _L0_xattn_in['g2'], 'L0_xattn_be2': _L0_xattn_in['be2'], 'L0_xattn_g3': _L0_xattn_in['g3'], 'L0_xattn_be3': _L0_xattn_in['be3'], 'L0_xattn_Wf1': _L0_xattn_in['Wf1'], 'L0_xattn_bf1': _L0_xattn_in['bf1'], 'L0_xattn_Wf2': _L0_xattn_in['Wf2'], 'L0_xattn_bf2': _L0_xattn_in['bf2'], 'L0_ffn_router_w': _L0_ffn_in['router_w'], 'L0_ffn_router_b': _L0_ffn_in['router_b'], 'L0_ffn_w1': _L0_ffn_in['w1'], 'L0_ffn_b1': _L0_ffn_in['b1'], 'L0_ffn_w2': _L0_ffn_in['w2'], 'L0_ffn_b2': _L0_ffn_in['b2'], 'L0_ffn_gamma': _L0_ffn_in['gamma'], 'L0_ffn_beta': _L0_ffn_in['beta'], 'L1_xattn_Wq': _L1_xattn_in['Wq'], 'L1_xattn_Wk': _L1_xattn_in['Wk'], 'L1_xattn_Wv': _L1_xattn_in['Wv'], 'L1_xattn_Wo': _L1_xattn_in['Wo'], 'L1_ffn_gate_w': _L1_ffn_in['gate_w'], 'L1_ffn_gate_b': _L1_ffn_in['gate_b'], 'L1_ffn_w1': _L1_ffn_in['w1'], 'L1_ffn_b1': _L1_ffn_in['b1'], 'L1_ffn_w2': _L1_ffn_in['w2'], 'L1_ffn_b2': _L1_ffn_in['b2']}

def reference(x, ctx_1024, mask_BxSxS2_bf1, g_xattn, g_ffn, L0_xattn_Wq1, L0_xattn_Wk1, L0_xattn_Wv1, L0_xattn_bv1, L0_xattn_Wq2, L0_xattn_Wk2, L0_xattn_Wv2, L0_xattn_bv2, L0_xattn_g1, L0_xattn_be1, L0_xattn_g2, L0_xattn_be2, L0_xattn_g3, L0_xattn_be3, L0_xattn_Wf1, L0_xattn_bf1, L0_xattn_Wf2, L0_xattn_bf2, L0_ffn_router_w, L0_ffn_router_b, L0_ffn_w1, L0_ffn_b1, L0_ffn_w2, L0_ffn_b2, L0_ffn_gamma, L0_ffn_beta, L1_xattn_Wq, L1_xattn_Wk, L1_xattn_Wv, L1_xattn_Wo, L1_ffn_gate_w, L1_ffn_gate_b, L1_ffn_w1, L1_ffn_b1, L1_ffn_w2, L1_ffn_b2):
    import jax
    import jax.numpy as jnp

    def _L0_xattn_ref(input_tensor, encoder_output, Wq1, Wk1, Wv1, bv1, Wq2, Wk2, Wv2, bv2, g1, be1, g2, be2, g3, be3, Wf1, bf1, Wf2, bf2):
        import jax, jax.numpy as jnp
        import numpy as np
        D_MODEL = 128
        N_HEADS = 16
        HEAD = D_MODEL // N_HEADS
        D_FF = 512
        LN_EPS = 1e-05

        def _layernorm(x, g, b):
            mu = jnp.mean(x, axis=-1, keepdims=True)
            var = jnp.mean(jnp.square(x - mu), axis=-1, keepdims=True)
            return (x - mu) * jax.lax.rsqrt(var + LN_EPS) * g + b

        def _mha(q_in, k_in, v_in, Wq, Wk, Wv, bv, causal):
            q = jnp.einsum('bsd,hde->bhse', q_in, Wq)
            k = jnp.einsum('btd,hde->bhte', k_in, Wk)
            v = jnp.einsum('btd,hde->bhte', v_in, Wv) + bv[None, :, None, :]
            scale = HEAD ** (-0.5)
            scores = jnp.einsum('bhse,bhte->bhst', q, k) * scale
            if causal:
                S, T = (scores.shape[-2], scores.shape[-1])
                mask = jnp.tril(jnp.ones((S, T), dtype=bool))
                scores = jnp.where(mask, scores, -jnp.inf)
            p = jax.nn.softmax(scores, axis=-1)
            o = jnp.einsum('bhst,bhte->bhse', p, v)
            B, H, S, E = o.shape
            return o.transpose(0, 2, 1, 3).reshape(B, S, H * E)
        x = input_tensor
        sa = _mha(x, x, x, Wq1, Wk1, Wv1, bv1, causal=True)
        x = _layernorm(sa + input_tensor, g1, be1)
        ca = _mha(x, encoder_output, encoder_output, Wq2, Wk2, Wv2, bv2, causal=False)
        x = _layernorm(x + ca, g2, be2)
        ffn = jax.nn.relu(x @ Wf1 + bf1) @ Wf2 + bf2
        x = _layernorm(x + ffn, g3, be3)
        return x

    def _L0_ffn_ref(tgt, router_w, router_b, w1, b1, w2, b2, gamma, beta):
        import jax, jax.numpy as jnp
        import numpy as np
        B, S, D, F, E = (2, 256, 128, 512, 8)
        LN_EPS = 1e-05

        def _xavier(key, shape, fan_in, fan_out):
            a = np.sqrt(6.0 / (fan_in + fan_out))
            return jax.random.uniform(key, shape, jnp.float32, -a, a)
        logits = jnp.einsum('bsd,ed->bse', tgt, router_w) + router_b
        rw = jax.nn.softmax(logits, axis=-1)
        rw = jnp.zeros_like(rw).at[..., 0].set(1.0)
        h = jax.nn.relu(jnp.einsum('bsd,edf->besf', tgt, w1) + b1[None, :, None, :])
        eo = jnp.einsum('besf,efd->besd', h, w2) + b2[None, :, None, :]
        tgt2 = jnp.einsum('besd,bse->bsd', eo, rw)
        x = tgt + tgt2
        mean = jnp.mean(x, axis=-1, keepdims=True)
        var = jnp.mean(jnp.square(x - mean), axis=-1, keepdims=True)
        return (x - mean) * jax.lax.rsqrt(var + LN_EPS) * gamma + beta

    def _L1_xattn_ref(query, key, value, mask, Wq, Wk, Wv, Wo):
        import jax, jax.numpy as jnp
        import numpy as np
        B, S, D = (2, 256, 128)
        H, DQK, DV, DOUT = (16, 64, 64, 128)
        n_seq = query.shape[-2]
        q = jnp.einsum('...i,hio->...ho', query, Wq)
        k = jnp.einsum('...i,hio->...ho', key, Wk)
        v = jnp.einsum('...i,hio->...ho', value, Wv)
        scale = 1.0 / np.sqrt(n_seq).astype(np.float32)
        logits = jnp.einsum('...ihj,...khj->...hik', q, k) * scale
        neg_inf = jnp.where(mask, jnp.float32(0.0), -jnp.inf)
        logits = logits + neg_inf[..., None, :, :]
        probs = jax.nn.softmax(logits, axis=-1)
        out = jnp.einsum('...hij,...jhk->...ihk', probs, v)
        out = out.reshape(out.shape[:-2] + (H * DV,))
        return out @ Wo

    def _L1_ffn_ref(x, gate_w, gate_b, w1, b1, w2, b2):
        import jax, jax.numpy as jnp
        import numpy as np
        N_EXPERTS = 8
        TOP_K = 2
        W_SCALE = 0.02
        logits = jnp.einsum('sbd,de->sbe', x, gate_w) + gate_b
        top_w, top_idx = jax.lax.top_k(logits, TOP_K)
        probs = jax.nn.softmax(top_w.astype(jnp.float32), axis=-1)
        comb = jnp.sum(jax.nn.one_hot(top_idx, N_EXPERTS, dtype=probs.dtype) * probs[..., None], axis=-2)
        out = jnp.zeros_like(x)
        for e in range(N_EXPERTS):
            h = jax.nn.relu(jnp.einsum('sbd,df->sbf', x, w1[e]) + b1[e])
            y = jnp.einsum('sbf,fd->sbd', h, w2[e]) + b2[e]
            out = out + comb[..., e:e + 1].astype(x.dtype) * y
        return out
    x = x + jnp.tanh(g_xattn[0]) * _L0_xattn_ref(_layernorm(x, axis=-1), ctx_1024, L0_xattn_Wq1, L0_xattn_Wk1, L0_xattn_Wv1, L0_xattn_bv1, L0_xattn_Wq2, L0_xattn_Wk2, L0_xattn_Wv2, L0_xattn_bv2, L0_xattn_g1, L0_xattn_be1, L0_xattn_g2, L0_xattn_be2, L0_xattn_g3, L0_xattn_be3, L0_xattn_Wf1, L0_xattn_bf1, L0_xattn_Wf2, L0_xattn_bf2)
    x = x + jnp.tanh(g_ffn[0]) * _L0_ffn_ref(_layernorm(x, axis=-1), L0_ffn_router_w, L0_ffn_router_b, L0_ffn_w1, L0_ffn_b1, L0_ffn_w2, L0_ffn_b2, L0_ffn_gamma, L0_ffn_beta)
    x = x + jnp.tanh(g_xattn[1]) * _L1_xattn_ref(_layernorm(x, axis=-1), ctx_1024, ctx_1024, mask_BxSxS2_bf1, L1_xattn_Wq, L1_xattn_Wk, L1_xattn_Wv, L1_xattn_Wo)
    x = x + jnp.tanh(g_ffn[1]) * _L1_ffn_ref(_layernorm(x, axis=-1), L1_ffn_gate_w, L1_ffn_gate_b, L1_ffn_w1, L1_ffn_b1, L1_ffn_w2, L1_ffn_b2)
    return x

_drawn_inputs = setup_inputs


def setup_inputs(seed=0):
    import zlib

    import numpy as np

    out = dict(_drawn_inputs(seed))
    spreads = {'g_ffn': (-1.0, 0.6),
     'L0_xattn_bv1': (0.0, 0.1),
     'L0_xattn_bv2': (0.0, 0.1),
     'L0_xattn_g1': (1.0, 0.2),
     'L0_xattn_be1': (0.0, 0.1),
     'L0_xattn_g2': (1.0, 0.2),
     'L0_xattn_be2': (0.0, 0.1),
     'L0_xattn_g3': (1.0, 0.2),
     'L0_xattn_be3': (0.0, 0.1),
     'L0_xattn_bf1': (0.0, 0.339),
     'L0_xattn_bf2': (0.0, 0.1),
     'L0_ffn_router_b': (0.0, 0.1),
     'L0_ffn_b1': (0.0, 0.1),
     'L0_ffn_b2': (0.0, 0.1),
     'L0_ffn_gamma': (1.0, 0.2),
     'L0_ffn_beta': (0.0, 0.1),
     'L1_ffn_gate_b': (0.0, 0.1),
     'L1_ffn_b1': (0.0, 0.575),
     'L1_ffn_b2': (0.0, 0.1)}
    factors = {}
    for name, (base, spread) in spreads.items():
        noise = np.random.default_rng([zlib.crc32(name.encode()), seed]).standard_normal(out[name].shape)
        drawn = base * np.exp(spread * noise) if base else spread * noise
        out[name] = jnp.asarray(drawn.astype(out[name].dtype))
    for name, factor in factors.items():
        out[name] = (out[name] * factor).astype(out[name].dtype)
    return out
```

```python
from contextlib import ExitStack

import concourse.bass as bass
from concourse import mybir

F32 = mybir.dt.float32
F16 = mybir.dt.float16
U8 = mybir.dt.uint8
I32 = mybir.dt.int32
ALU = mybir.AluOpType
ACT = mybir.ActivationFunctionType
AX_X = mybir.AxisListType.X

NB, S, D, T, H = 8, 100, 128, 1444, 16
NTOK = NB * S
HALF = NTOK // 2
G, J = 4, 4
E0 = D // H
STACK = 3 * E0
SHIFT = 3
E1 = 64
FF = 512
FT = FF // D
NE = 8
EPS = 1e-5

HC = 4
UNIT = H // 2
MASKED = -60000.0
TT = -(-T // 128)
ROWS = [T // TT + (t < T % TT) for t in range(TT)]
OFF = [sum(ROWS[:t]) for t in range(TT)]
NG = 3
GT = TT // NG
CHUNKS = [(OFF[GT * q], sum(ROWS[GT * q:GT * q + GT])) for q in range(NG)]
NC = NG
TALL = T % TT
assert TT == NG * GT and TALL == GT and max(w for _, w in CHUNKS) <= 512
SCALE0 = float(E0) ** -0.5
SCALE1 = float(S) ** -0.5
STEPS = 2 * TT
LAG = 2
RING = 4
FIRST_JOB_STEP, LAST_JOB_STEP = 2, 21
ACC, SIDE = 4, 6


MARKS = [(E0, 2 * E0, -1.0), (STACK, STACK + SHIFT, 1.0), (2 * E0, STACK, -1.0), (STACK, STACK + SHIFT, 1.0)]


def job_range(n, s):
    s, steps = s - FIRST_JOB_STEP, LAST_JOB_STEP - FIRST_JOB_STEP
    return range(n * s // steps, n * (s + 1) // steps) if 0 <= s < steps else range(0)


JOBS0 = ([("q", 0, 0)] + [("tr", q, 0) for q in range(NG)]
         + [("k", c, j) for c in range(NC) for j in range(J)]
         + [("v", q, 0) for q in range(NG)]
         + [("n", h, c) for h in range(H) for c in range(NC)] + [("m", 0, 0)])
JOBS0 = JOBS0 + [("pad", 0, 0)] * (len(JOBS0) % 2)
JOBS1 = ([("q", q, 0) for q in range(H // HC)] + [("tr", q, 0) for q in range(NG)]
         + [("n", h, c) for h in range(H) for c in range(NC)] + [("m", 0, 0)])
assert len(JOBS0) % 2 == 0 and len(JOBS1) % 2 == 0


def count(jobs, kinds, k=None):
    return sum(job[0] in kinds for job in jobs[:k])


class Core:

    def __init__(self, nc, stack, dram, out):
        self.nc, self.stack, self.dram, self.out = nc, stack, dram, out
        self.sems = {}

    def sem(self, name):
        if name not in self.sems:
            self.sems[name] = self.stack.enter_context(self.nc.semaphore(name))
        return self.sems[name]

    def sb(self, name, shape, dt=F32, stack=None):
        return (stack or self.stack).enter_context(self.nc.sbuf_tensor(name, shape, dt))


def chain(core, eng, name):
    done, n = core.sem(name), [0]

    def link(ins):
        n[0] += 1
        ins.then_inc(done, 1)
        eng.wait_ge(done, n[0])

    return link


def inverse_root(core, link, root, var):
    nc, half, t = core.nc, core.ln_half[:, :], core.ln_t[:, :]
    link(nc.vector.tensor_scalar(root, var, EPS, None, ALU.add))
    link(nc.vector.tensor_scalar(half, root, -0.5, None, ALU.mult))
    link(nc.vector.tensor_scalar(root.bitcast(I32), root.bitcast(I32), -0.5, float(0x5F3759DF), ALU.mult, ALU.add))
    for _ in range(3):
        link(nc.vector.tensor_tensor(t, root, root, ALU.mult))
        link(nc.vector.tensor_tensor(t, t, half, ALU.mult))
        link(nc.vector.scalar_tensor_tensor(out=root, in0=t, scalar=1.5, in1=root, op0=ALU.add, op1=ALU.mult))


def layer_norm(core, link, dst, src, gain=None, shift=None):
    nc, st, mv, rstd = core.nc, core.ln_stats, core.ln_mv, core.ln_rstd
    for b in range(NB):
        ins = nc.vector.bn_stats(st[:, b, :], src[:, b, :])
    link(ins)
    for b in range(NB):
        ins = nc.vector.bn_aggr(mv[:, b, :], st[:, b, :])
    link(ins)
    inverse_root(core, link, rstd[:, :], mv[:, :, 1])
    for b in range(NB):
        ins = nc.vector.tensor_scalar(dst[:, b, :], src[:, b, :], mv[:, b, 0:1], rstd[:, b:b + 1],
                                      ALU.subtract, ALU.mult)
    link(ins)
    if gain is not None:
        link(nc.vector.tensor_tensor(dst[:, :, :], dst[:, :, :], rows(gain), ALU.mult))
        link(nc.vector.tensor_tensor(dst[:, :, :], dst[:, :, :], rows(shift), ALU.add))


def rows(row):
    return row[0:S, :].unsqueeze(1).broadcast_to([S, NB, D])


def transpose_x(core, pe, src, bank):
    for b in range(NB):
        ins = core.nc.tensor.transpose(core.ps[:, bank + b // 4, (b % 4) * S:(b % 4 + 1) * S],
                                       src[:, b, :], core.ident[0:S, 0:S])
    return ins


def split_stack(core, eng, dst, psum, high, signs):
    return core.nc.vector.scalar_tensor_tensor(out=dst, in0=high, scalar=signs, in1=psum,
                                               op0=ALU.mult, op1=ALU.add)


def shift_parts(core, link, nm3, psum, rest):
    nc = core.nc
    link(nc.vector.tensor_copy(nm3[:, 0, :], psum))
    link(nc.vector.tensor_tensor(rest, psum, nm3[:, 0, :], ALU.subtract))
    link(nc.vector.tensor_copy(nm3[:, 1, :], rest))
    link(nc.vector.tensor_tensor(rest, rest, nm3[:, 1, :], ALU.subtract))
    return nc.vector.tensor_copy(nm3[:, 2, :], rest)


def setup_phase(core):
    nc, dram, sem, sb = core.nc, core.dram, core.sem, core.sb
    core.ps = core.stack.enter_context(nc.psum_tensor("psum", [128, 8, 512], F32))
    core.x = sb("x", [S, NB, D])
    core.xn = sb("normalised", [S, NB, D])
    core.work = sb("work", [S, NB, D])
    core.xT = sb("xT", [D, NTOK])
    core.ident = sb("identity", [128, 128])
    core.ident4 = sb("identity_heads", [S, J, S], F16)
    core.causal4 = sb("causal_heads", [S, J, S], F16)
    core.ln_stats = sb("ln_stats", [S, NB, 6])
    core.ln_mv = sb("ln_mean_var", [S, NB, 2])
    core.ln_rstd = sb("ln_rstd", [S, NB])
    core.ln_half = sb("ln_half", [S, NB])
    core.ln_t = sb("ln_t", [S, NB])
    core.signs_k = sb("signs_keys", [128, 1])
    core.signs_q = sb("signs_queries", [128, 1])
    core.ones_k = sb("ones_keys", [128, 1])
    core.gates = sb("gates", [128, 4])
    core.wstack = {n: sb(f"stack_{n}", [D, J, 128]) for n in ("Wq1", "Wk1", "Wq2", "Wk2")}
    core.wraw = {n: sb(f"raw_{n}", [D, H, E0]) for n in ("Wq1", "Wk1", "Wv1", "Wq2", "Wk2", "Wv2")}
    names = {"bv1": H * E0, "bv2": H * E0, "g1": D, "be1": D, "g2": D, "be2": D, "g3": D, "be3": D,
             "bf2": D}
    core.row = {n: sb(f"row_{n}", [S, w]) for n, w in names.items()}
    core.row_e = {n: sb(f"row_{n}", [S, D]) for n in ("b2", "gamma", "beta")}
    core.dense = {n: (sb(f"{n}_up", [D, FF]), sb(f"{n}_up_bias", [D, FT]), sb(f"{n}_down", [D, FT, D]))
                  for n in ("ffn", "expert0")}
    row_marks = sb("row_marks", [128, len(MARKS), G])

    with nc.Block() as block:
        @block.sync
        def _(sp):
            sp.dma_start(core.x[:, :, :], dram["x"].rearrange("b s d -> s b d")).then_inc(sem("x_loaded"), 16)
            for n in ("Wq1", "Wk1", "Wv1"):
                sp.dma_start(core.wraw[n][:, :, :], dram[f"L0_xattn_{n}"].rearrange("h d e -> d h e")
                             ).then_inc(sem("self_weights_loaded"), 16)
            for n in ("Wq2", "Wk2", "Wv2"):
                sp.dma_start(core.wraw[n][:, :, :], dram[f"L0_xattn_{n}"].rearrange("h d e -> d h e")
                             ).then_inc(sem("cross_weights_loaded"), 16)
            for n, up, up_bias, down in (
                    ("ffn", dram["L0_xattn_Wf1"], dram["L0_xattn_bf1"], dram["L0_xattn_Wf2"]),
                    ("expert0", dram["L0_ffn_w1"][0], dram["L0_ffn_b1"][0], dram["L0_ffn_w2"][0])):
                for dst, src in zip(core.dense[n], (up, up_bias.rearrange("(f p) -> p f", p=D),
                                                    down.rearrange("(f p) d -> p f d", p=D))):
                    sp.dma_start(dst[tuple(slice(None) for _ in dst.shape)], src, allow_slow_non_contiguous=True
                                 ).then_inc(sem(f"{n}_loaded"), 16)

        @block.scalar
        def _(act):
            for n, w in names.items():
                src = dram[f"L0_xattn_{n}"]
                src = src.rearrange("h e -> (h e)") if len(src.shape) == 2 else src
                act.dma_start(core.row[n][:, :], src.rearrange("(o w) -> o w", o=1).broadcast_to([S, w])
                              ).then_inc(sem("rows_loaded"), 16)
            for k, n in enumerate(("g_xattn", "g_ffn")):
                act.dma_start(core.gates[:, 2 * k:2 * k + 2],
                              dram[n].rearrange("(o w) -> o w", o=1).broadcast_to([128, 2])
                              ).then_inc(sem("gates_loaded"), 16)
            for n, src in (("b2", dram["L0_ffn_b2"][0:1, :]),
                           ("gamma", dram["L0_ffn_gamma"].rearrange("(o w) -> o w", o=1)),
                           ("beta", dram["L0_ffn_beta"].rearrange("(o w) -> o w", o=1))):
                act.dma_start(core.row_e[n][:, :], src.broadcast_to([S, D])).then_inc(sem("expert_rows_loaded"), 16)
            act.wait_ge(sem("gates_loaded"), 32)
            nc.scalar.activation(core.gates[:, :], core.gates[:, :], ACT.Tanh).then_inc(sem("gates_ready"), 1)

        @block.gpsimd
        def _(pool):
            link = chain(core, pool, "setup_pool_steps")
            link(nc.gpsimd.memset(core.ident[:, :], 0.0))
            link(nc.gpsimd.affine_select(out=core.ident[:, :], in_=core.ident[:, :], compare_op=ALU.not_equal,
                                         fill=1.0, base=0, pattern=[[-1, 128]], channel_multiplier=1))
            nc.gpsimd.tensor_copy(core.ident4[:, :, :],
                                  core.ident[0:S, 0:S].unsqueeze(1).broadcast_to([S, J, S])
                                  ).then_inc(sem("identity_ready"), 1)
            link(nc.gpsimd.memset(core.causal4[:, :, :], 0.0))
            nc.gpsimd.affine_select(out=core.causal4[:, :, :], in_=core.causal4[:, :, :], compare_op=ALU.is_ge,
                                    fill=MASKED, base=0, pattern=[[0, J], [-1, S]], channel_multiplier=1
                                    ).then_inc(sem("causal_ready"), 1)
            for k, (lo, hi, value) in enumerate(MARKS):
                marks = row_marks[:, k, :]
                link(nc.gpsimd.memset(marks, value))
                link(nc.gpsimd.affine_select(out=marks, in_=marks, compare_op=ALU.is_ge, fill=0.0, base=-lo,
                                             pattern=[[-32, G]], channel_multiplier=1))
                ins = nc.gpsimd.affine_select(out=marks, in_=marks, compare_op=ALU.is_ge, fill=0.0,
                                              base=hi - 1, pattern=[[32, G]], channel_multiplier=-1)
                if k + 1 < len(MARKS):
                    link(ins)
            ins.then_inc(sem("marks_ready"), 1)

        @block.vector
        def _(dve):
            link = chain(core, dve, "setup_vector_steps")
            dve.wait_ge(sem("marks_ready"), 1)
            nc.vector.tensor_reduce(core.signs_k[:, :], row_marks[:, 0:2, :].rearrange("p a g -> p (a g)"),
                                    AX_X, ALU.add)
            nc.vector.tensor_reduce(core.signs_q[:, :], row_marks[:, 2, :], AX_X, ALU.add)
            nc.vector.tensor_reduce(core.ones_k[:, :], row_marks[:, 3, :], AX_X, ALU.add
                                    ).then_inc(sem("signs_ready"), 1)
            for n in core.wstack:
                link(nc.vector.memset(core.wstack[n][:, :, :], 0.0))
            for n, (loaded, k) in {"Wq1": ("self_weights_loaded", 48), "Wk1": ("self_weights_loaded", 48),
                                   "Wq2": ("cross_weights_loaded", 48),
                                   "Wk2": ("cross_weights_loaded", 48)}.items():
                dve.wait_ge(sem(loaded), k)
                for r in range(3):
                    ins = nc.vector.tensor_copy(
                        core.wstack[n][:, :, :].rearrange("d j (g r) -> d g j r", g=G)[:, :, :, E0 * r:E0 * r + E0],
                        core.wraw[n][:, :, :].rearrange("d (g j) e -> d g j e", j=J))
                ins.then_inc(sem("stack_weights_ready"), 1)
            dve.wait_ge(sem("x_loaded"), 16)
            layer_norm(core, link, core.xn, core.x)
            dve.sem_inc(sem("x_normalised"), 1)


def self_attention_phase(core):
    nc, sem, ps = core.nc, core.sem, core.ps
    with ExitStack() as own:
        def sb(name, shape, dt=F32):
            return core.sb(name, shape, dt, own)

        high = sb("self_high", [128, 2, 2, HALF], F16)
        qst = sb("self_queries", [128, J, NTOK], F16)
        kst = sb("self_keys", [128, J, NTOK], F16)
        values = sb("self_values", [S, NB, H, 32])
        probs = sb("self_probs", [S, RING, 2, J * S])
        mx = sb("self_max", [S, G, J, NB])
        nm3 = sb("self_shift", [G * J * NB, SHIFT, S], F16)
        rest = sb("self_shift_rest", [G * J * NB, S])

        with nc.Block() as block:
            @block.sync
            def _(sp):
                sp.wait_ge(sem("self_shift_ready"), 1)
                for g in range(G):
                    for r in range(SHIFT):
                        row = 32 * g + STACK + r
                        sp.dma_start(qst[row:row + 1, :, :].rearrange("o j n -> o (j n)"),
                                     nm3[J * NB * g:J * NB * (g + 1), r, :]).then_inc(sem("self_shift_loaded"), 16)
                sp.wait_ge(sem("self_shift_loaded"), 16 * G * SHIFT)

            @block.gpsimd
            def _(pool):
                link = chain(core, pool, "self_pool_steps")
                link(nc.gpsimd.memset(values[:, :, :, :], 0.0))
                nc.gpsimd.memset(values[:, :, :, E0:E0 + 1], 1.0).then_inc(sem("self_ones_ready"), 1)

            @block.tensor
            def _(pe):
                pe.wait_ge(sem("identity_ready"), 1)
                pe.wait_ge(sem("x_normalised"), 1)
                transpose_x(core, pe, core.xn, 6).then_inc(sem("input_xT_psum"), 1)
                pe.wait_ge(sem("input_xT_ready"), 1)
                pe.wait_ge(sem("stack_weights_ready"), 2)
                for k, n in enumerate(("Wq1", "Wk1")):
                    for j in range(J):
                        i = J * k + j
                        if i >= 2:
                            pe.wait_ge(sem("self_stack_ready"), i - 1)
                        for c in range(2):
                            ins = nc.tensor.matmul(ps[:, 2 * (i % 2) + c, 0:HALF], core.wstack[n][:, j, :],
                                                   core.xT[:, c * HALF:(c + 1) * HALF], start=True, stop=True)
                        ins.then_inc(sem("self_stack_psum"), 1)
                for b in range(NB):
                    ins = nc.tensor.matmul(ps[0:S, 4 + b // 4, 128 * (b % 4):128 * (b % 4 + 1)],
                                           core.xT[:, b * S:(b + 1) * S],
                                           core.wraw["Wv1"][:, :, :].rearrange("d h e -> d (h e)"),
                                           start=True, stop=True)
                ins.then_inc(sem("self_values_psum"), 1)
                pe.wait_ge(sem("self_stack_ready"), 2 * J)
                pe.wait_ge(sem("causal_ready"), 1)
                for b in range(NB):
                    for g in range(G):
                        if b:
                            pe.wait_ge(sem("self_max_ready"), G * (b - 1) + g + 1)
                        bank = ps[0:S, g, 0:HALF]
                        nc.tensor.matmul(bank, core.ident4[:, 0, :],
                                         core.causal4[:, :, :].rearrange("s j t -> s (j t)"),
                                         start=True, stop=False, skip_group_check=True)
                        for j in range(J):
                            ins = nc.tensor.matmul(
                                ps[0:S, g, j * S:(j + 1) * S], qst[32 * g:32 * g + STACK, j, b * S:(b + 1) * S],
                                kst[32 * g:32 * g + STACK, j, b * S:(b + 1) * S],
                                start=False, stop=True, skip_group_check=True)
                        ins.then_inc(sem("self_first_scores"), 1)
                pe.wait_ge(sem("self_negmax_ready"), 1)
                nc.tensor.transpose(ps[:, 6, 0:S], core.negmax[:, :], core.ident[0:S, 0:S]
                                    ).then_inc(sem("self_negmax_psum"), 1)
                pe.wait_ge(sem("self_shift_loaded"), 16 * G * SHIFT)
                pe.wait_ge(sem("self_values_ready"), 2)

                def values_product(n):
                    b, half = n // 2, n % 2
                    pe.wait_ge(sem("self_probs_ready"), n + 1)
                    if half == 0 and b >= 2:
                        pe.wait_ge(sem("self_oT_ready"), b - 1)
                    for gg in range(2):
                        g = 2 * half + gg
                        for j in range(J):
                            ins = nc.tensor.matmul(
                                ps[32 * j:32 * j + 32, ACC + b % 2, g * S:(g + 1) * S], values[:, b, J * g + j, :],
                                probs[:, n % RING, gg, j * S:(j + 1) * S], start=(g == 0), stop=True,
                                skip_group_check=True)
                    ins.then_inc(sem("self_product_done"), 1)

                for n in range(2 * NB):
                    b, half = n // 2, n % 2
                    if n >= 2:
                        pe.wait_ge(sem("self_probs_ready"), n - 1)
                    for gg in range(2):
                        g = 2 * half + gg
                        nc.tensor.matmul(ps[0:S, g, 0:HALF], core.causal4[:, 0, :],
                                         core.ident4[:, :, :].rearrange("s j t -> s (j t)"),
                                         start=True, stop=False, skip_group_check=True)
                        for j in range(J):
                            ins = nc.tensor.matmul(
                                ps[0:S, g, j * S:(j + 1) * S],
                                kst[32 * g:32 * g + STACK + SHIFT, j, b * S:(b + 1) * S],
                                qst[32 * g:32 * g + STACK + SHIFT, j, b * S:(b + 1) * S],
                                start=False, stop=True, skip_group_check=True)
                    ins.then_inc(sem("self_scores_psum"), 1)
                    if n >= 1:
                        values_product(n - 1)
                values_product(2 * NB - 1)

            @block.scalar
            def _(act):
                act.wait_ge(sem("input_xT_psum"), 1)
                nc.scalar.activation(core.xT[:, :].rearrange("d (c n) -> d c n", c=2), ps[:, 6:8, 0:HALF], ACT.Copy
                                     ).then_inc(sem("input_xT_ready"), 1)
                act.wait_ge(sem("signs_ready"), 1)
                for i in range(2 * J):
                    act.wait_ge(sem("self_stack_psum"), i + 1)
                    if i >= 2:
                        act.wait_ge(sem("self_stack_ready"), i - 1)
                    b = 2 * (i % 2)
                    nc.scalar.activation(high[:, i % 2, :, :], ps[:, b:b + 2, 0:HALF], ACT.Identity,
                                         bias=core.ones_k[:, 0:1] if i >= J else 0.0
                                         ).then_inc(sem("self_high_ready"), 1)
                act.wait_ge(sem("self_values_psum"), 1)
                act.wait_ge(sem("self_ones_ready"), 1)
                for c in range(2):
                    nc.scalar.activation(values[:, 4 * c:4 * c + 4, :, 0:E0],
                                         ps[0:S, 4 + c, :].rearrange("s (b h e) -> s b h e", b=4, h=H), ACT.Copy
                                         ).then_inc(sem("self_values_ready"), 1)
                for n in range(2 * NB):
                    half = n % 2
                    act.wait_ge(sem("self_scores_psum"), n + 1)
                    if n >= RING:
                        act.wait_ge(sem("self_product_done"), n - RING + 1)
                    nc.scalar.activation(probs[:, n % RING, :, :], ps[0:S, 2 * half:2 * half + 2, 0:HALF], ACT.Exp,
                                         scale=SCALE0).then_inc(sem("self_probs_ready"), 1)

            @block.vector
            def _(dve):
                link = chain(core, dve, "self_vector_steps")
                for i in range(2 * J):
                    dve.wait_ge(sem("self_high_ready"), i + 1)
                    b = 2 * (i % 2)
                    dst = (qst if i < J else kst)[:, i % J, :].rearrange("p (c n) -> p c n", c=2)
                    split_stack(core, dve, dst, ps[:, b:b + 2, 0:HALF], high[:, i % 2, :, :],
                                core.signs_q[:, 0:1] if i < J else core.signs_k[:, 0:1]
                                ).then_inc(sem("self_stack_ready"), 1)
                for b in range(NB):
                    for g in range(G):
                        dve.wait_ge(sem("self_first_scores"), G * b + g + 1)
                        nc.vector.tensor_reduce(mx[:, g, :, b], ps[0:S, g, 0:HALF].rearrange("s (j t) -> s j t", j=J),
                                                AX_X, ALU.max).then_inc(sem("self_max_ready"), 1)
                dve.wait_ge(sem("self_max_ready"), G * NB)
                nc.vector.tensor_scalar(core.negmax[:, :], mx[:, :, :, :].rearrange("s g j b -> s (g j b)"), -1.0,
                                        None, ALU.mult).then_inc(sem("self_negmax_ready"), 1)
                dve.wait_ge(sem("self_negmax_psum"), 1)
                shift_parts(core, link, nm3, ps[:, 6, 0:S], rest[:, :]).then_inc(sem("self_shift_ready"), 1)
                for b in range(NB):
                    dve.wait_ge(sem("self_product_done"), 2 * b + 2)
                    nc.vector.tensor_copy(core.oT[:, b, :], ps[:, ACC + b % 2, 0:G * S]
                                          ).then_inc(sem("self_oT_ready"), 1)


def finish_attention_phase(core, name):
    nc, sem, ps = core.nc, core.sem, core.ps
    gain, shift, bias = {"self": ("g1", "be1", "bv1"), "cross": ("g2", "be2", "bv2")}[name]
    with nc.Block() as block:
        @block.tensor
        def _(pe):
            for b in range(NB):
                if b >= 4:
                    pe.wait_ge(sem(name + "_normalised"), b - 3)
                for g in range(G):
                    ins = nc.tensor.transpose(ps[0:S, b % 4, 128 * g:128 * (g + 1)], core.oT[:, b, g * S:(g + 1) * S],
                                              core.ident[:, :])
                ins.then_inc(sem(name + "_o_psum"), 1)
            pe.wait_ge(sem(name + "_added"), 1)
            transpose_x(core, pe, core.xn, 6).then_inc(sem(name + "_xT_psum"), 1)

        @block.vector
        def _(dve):
            link = chain(core, dve, name + "_finish_steps")
            for b in range(NB):
                dve.wait_ge(sem(name + "_o_psum"), b + 1)
                o = ps[0:S, b % 4, :].rearrange("s (g j e) -> s g j e", g=G, j=J)
                link(nc.vector.reciprocal(core.row_sums[:, b, :, :], o[:, :, :, E0]))
                nc.vector.tensor_tensor(core.work[:, b, :].rearrange("s (g j e) -> s g j e", g=G, j=J),
                                        o[:, :, :, 0:E0],
                                        core.row_sums[:, b, :, :].unsqueeze(3).broadcast_to([S, G, J, E0]), ALU.mult
                                        ).then_inc(sem(name + "_normalised"), 1)
            dve.wait_ge(sem(name + "_normalised"), NB)
            dve.wait_ge(sem("rows_loaded"), 16 * len(core.row))
            link(nc.vector.tensor_tensor(core.work[:, :, :], core.work[:, :, :], rows(core.row[bias]), ALU.add))
            link(nc.vector.tensor_tensor(core.work[:, :, :], core.work[:, :, :], core.xn[:, :, :], ALU.add))
            layer_norm(core, link, core.xn, core.work, core.row[gain], core.row[shift])
            dve.sem_inc(sem(name + "_added"), 1)

        @block.scalar
        def _(act):
            act.wait_ge(sem(name + "_xT_psum"), 1)
            nc.scalar.activation(core.xT[:, :].rearrange("d (c n) -> d c n", c=2), ps[:, 6:8, 0:HALF], ACT.Copy
                                 ).then_inc(sem(name + "_xT_ready"), 1)


def run_sequences(eng, emit):
    with eng.Fori(0, NB // 2 - 1) as i:
        for u in range(2):
            emit(2 * i + u, u, True)
    emit(NB - 2, 0, True)
    emit(NB - 1, 1, False)


def wait_apart(eng, turns):
    eng.sem_inc(turns, 1)


def load_context_tiles(core, eng, b, u, loaded):
    src = core.dram["ctx_1024"][bass.ds(b, 1), :, :].rearrange("o r d -> (o r) d")
    cut = OFF[TALL]
    eng.dma_start(core.ctx[0:ROWS[0], u, 0:TALL, :], src[0:cut, :].rearrange("(t p) d -> p t d", p=ROWS[0])
                  ).then_inc(loaded, 16)
    eng.dma_start(core.ctx[0:ROWS[-1], u, TALL:TT, :], src[cut:T, :].rearrange("(t p) d -> p t d", p=ROWS[-1])
                  ).then_inc(loaded, 16)


def cross_attention_0_phase(core):
    nc, sem, ps = core.nc, core.sem, core.ps
    jobs, nj = JOBS0, len(JOBS0)
    with ExitStack() as own:
        def sb(name, shape, dt=F32):
            return core.sb(name, shape, dt, own)

        ctx = core.ctx
        ctxT = sb("x0_contextT", [D, T])
        high = sb("x0_high", [128, 2, 512], F16)
        qst = sb("x0_queries", [128, 2, J, S], F16)
        kst = sb("x0_keys", [128, 2, J, T], F16)
        values = sb("x0_values", [128, 2, TT, H, 32])
        probs = sb("x0_probs", [128, RING, 2, J * S])
        mx = sb("x0_max", [S, H, NC])
        negmax = sb("x0_negmax", [S, H])
        nm3 = sb("x0_shift", [H, SHIFT, S], F16)
        rest = sb("x0_shift_rest", [H, S])

        def side(k):
            return ps[:, SIDE + k % 2, :]

        stacks = count(jobs, "qk")

        with nc.Block() as block:
            @block.sync
            def _(sp):
                def load_context(b, u):
                    load_context_tiles(core, sp, b, u, sem("x0_context_loaded"))

                def shift_rows(n, u):
                    sp.wait_ge(sem("x0_shift_ready"), n + 1)
                    for g in range(G):
                        for r in range(SHIFT):
                            row = 32 * g + STACK + r
                            sp.dma_start(qst[row:row + 1, u, :, :].rearrange("o j n -> o (j n)"),
                                         nm3[J * g:J * (g + 1), r, :]).then_inc(sem("x0_shift_loaded"), 16)

                load_context(0, 0)
                shift_rows(0, 0)

                def sequence(b, u, more):
                    if more:
                        load_context(b + 1, 1 - u)
                        shift_rows(b + 1, 1 - u)

                run_sequences(sp, sequence)

            @block.gpsimd
            def _(pool):
                pool.memset(values[:, 0, :, :, :], 0.0).then_inc(sem("x0_zeros_ready"), 1)
                pool.memset(values[:, 1, :, :, :], 0.0).then_inc(sem("x0_zeros_ready"), 1)
                pool.wait_ge(sem("x0_zeros_ready"), 2)
                for u in range(2):
                    pool.memset(values[:, u, :, :, E0:E0 + 1], 1.0).then_inc(sem("x0_ones_ready"), 1)

            @block.tensor
            def _(pe):
                pe.wait_ge(sem("self_xT_ready"), 1)
                pe.wait_ge(sem("stack_weights_ready"), 4)

                def job(k, n, u):
                    kind, a, c = jobs[k]
                    pe.wait_ge(sem(f"x0_side_free{k % 2}"), nj // 2 * n + k // 2 + 1)
                    bank = side(k)
                    if kind == "q":
                        for j in range(J):
                            ins = nc.tensor.matmul(bank[:, j * S:(j + 1) * S], core.wstack["Wq2"][:, j, :],
                                                   core.xT[:, bass.ds(n * S, S)], start=True, stop=True)
                    elif kind == "tr":
                        if a == 0:
                            pe.wait_ge(sem("x0_context_loaded"), 32 * n + 32)
                        for t in range(GT * a, GT * a + GT):
                            o = OFF[t] - CHUNKS[a][0]
                            ins = nc.tensor.transpose(bank[:, o:o + ROWS[t]],
                                                      ctx[0:ROWS[t], u, t, :], core.ident[0:ROWS[t], 0:ROWS[t]])
                    elif kind == "k":
                        if a == 0 and c == 0:
                            pe.wait_ge(sem("x0_contextT_ready"), NG * (n + 1))
                        o, w = CHUNKS[a]
                        ins = nc.tensor.matmul(bank[:, 0:w], core.wstack["Wk2"][:, c, :], ctxT[:, o:o + w],
                                               start=True, stop=True)
                    elif kind == "v":
                        for t in range(GT * a, GT * a + GT):
                            ins = nc.tensor.matmul(bank[0:ROWS[t], D * (t % GT):D * (t % GT + 1)],
                                                   ctxT[:, OFF[t]:OFF[t] + ROWS[t]],
                                                   core.wraw["Wv2"][:, :, :].rearrange("d h e -> d (h e)"),
                                                   start=True, stop=True)
                    elif kind == "n":
                        if a == 0 and c == 0:
                            pe.wait_ge(sem("x0_stack_ready"), stacks * (n + 1))
                        g, j, (o, w) = a // J, a % J, CHUNKS[c]
                        ins = nc.tensor.matmul(bank[0:S, 0:w], qst[32 * g:32 * g + STACK, u, j, :],
                                               kst[32 * g:32 * g + STACK, u, j, o:o + w], start=True, stop=True)
                    elif kind == "m":
                        pe.wait_ge(sem("x0_negmax_ready"), n + 1)
                        ins = nc.tensor.transpose(bank[0:H, 0:S], negmax[:, :], core.ident[0:S, 0:S])
                    else:
                        pe.sem_inc(sem("x0_side_ready"), 1)
                        return
                    ins.then_inc(sem("x0_side_ready"), 1)

                for k in range(nj):
                    job(k, 0, 0)

                def sequence(b, u, more):
                    for s in range(STEPS + LAG):
                        if s < STEPS:
                            t, half = s // 2, s % 2
                            if s == 0:
                                pe.wait_ge(sem("x0_shift_loaded"), 16 * G * SHIFT * (b + 1))
                            pe.wait_ge(sem("x0_probs_ready"), STEPS * b + s + 1)
                            for j in range(J):
                                for g in (2 * half, 2 * half + 1):
                                    ins = nc.tensor.matmul(
                                        ps[0:ROWS[t], g, j * S:(j + 1) * S],
                                        kst[32 * g:32 * g + STACK + SHIFT, u, j, OFF[t]:OFF[t] + ROWS[t]],
                                        qst[32 * g:32 * g + STACK + SHIFT, u, j, :], start=True, stop=True)
                            ins.then_inc(sem("x0_scores_ready"), 1)
                        if more:
                            for k in job_range(nj, s):
                                job(k, b + 1, 1 - u)
                        if s >= LAG:
                            v = s - LAG
                            t, half = v // 2, v % 2
                            if v == 0:
                                pe.wait_ge(sem("x0_values_ready"), NG * (b + 1))
                                pe.wait_ge(sem("x0_oT_ready"), b + 1)
                            pe.wait_ge(sem("x0_probs_ready"), STEPS * b + v + 1 + 2)
                            for g in (2 * half, 2 * half + 1):
                                for j in range(J):
                                    ins = nc.tensor.matmul(
                                        ps[32 * j:32 * j + 32, ACC + u, g * S:(g + 1) * S],
                                        values[0:ROWS[t], u, t, J * g + j, :],
                                        probs[0:ROWS[t], v % RING, g % 2, j * S:(j + 1) * S],
                                        start=(t == 0 and g == 0), stop=(t == TT - 1), skip_group_check=True)
                            ins.then_inc(sem("x0_product_done"), 1)

                run_sequences(pe, sequence)

            @block.scalar
            def _(act):
                act.sem_inc(sem("x0_probs_ready"), 2)
                act.sem_inc(sem("x0_oT_ready"), 1)

                def job(k, n, u):
                    kind, a, c = jobs[k]
                    if kind in ("n", "m", "pad"):
                        return
                    act.wait_ge(sem("x0_side_ready"), nj * n + k + 1)
                    bank = side(k)
                    if kind == "q":
                        nc.scalar.activation(high[:, k % 2, 0:J * S], bank[:, 0:J * S], ACT.Identity
                                             ).then_inc(sem("x0_high_ready"), 1)
                    elif kind == "k":
                        w = CHUNKS[a][1]
                        nc.scalar.activation(high[:, k % 2, 0:w], bank[:, 0:w], ACT.Identity,
                                             bias=core.ones_k[:, 0:1]).then_inc(sem("x0_high_ready"), 1)
                    elif kind == "tr":
                        o, w = CHUNKS[a]
                        nc.scalar.activation(ctxT[:, o:o + w], bank[:, 0:w], ACT.Copy
                                             ).then_inc(sem("x0_contextT_ready"), 1)
                        act.wait_ge(sem("x0_contextT_ready"), NG * n + a + 1)
                        act.sem_inc(sem(f"x0_side_free{k % 2}"), 1)
                    elif kind == "v":
                        if a == 0:
                            act.wait_ge(sem("x0_ones_ready"), 2)
                        r = ROWS[GT * a]
                        nc.scalar.activation(values[0:r, u, GT * a:GT * a + GT, :, 0:E0],
                                             bank[0:r, 0:GT * D].rearrange("p (t h e) -> p t h e", t=GT, h=H), ACT.Copy
                                             ).then_inc(sem("x0_values_ready"), 1)
                        act.wait_ge(sem("x0_values_ready"), NG * n + a + 1)
                        act.sem_inc(sem(f"x0_side_free{k % 2}"), 1)

                for k in range(nj):
                    job(k, 0, 0)

                def sequence(b, u, more):
                    for s in range(STEPS + LAG):
                        if s < STEPS:
                            t, half = s // 2, s % 2
                            act.wait_ge(sem("x0_scores_ready"), STEPS * b + s + 1)
                            act.wait_ge(sem("x0_product_done"), STEPS * b + s + 1)
                            nc.scalar.activation(probs[0:ROWS[t], s % RING, :, :],
                                                 ps[0:ROWS[t], 2 * half:2 * half + 2, 0:J * S], ACT.Exp,
                                                 scale=SCALE0).then_inc(sem("x0_probs_ready"), 1)
                        if more:
                            for k in job_range(nj, s):
                                job(k, b + 1, 1 - u)
                    act.wait_ge(sem("x0_product_done"), STEPS * (b + 1) + RING)
                    nc.scalar.activation(core.oT[:, bass.ds(b, 1), :], ps[:, ACC + u, 0:G * S].unsqueeze(1), ACT.Copy
                                         ).then_inc(sem("x0_oT_ready"), 1)

                run_sequences(act, sequence)

            @block.vector
            def _(dve):
                dve.sem_inc(sem("x0_product_done"), RING)
                dve.sem_inc(sem("x0_side_free0"), 1)
                dve.sem_inc(sem("x0_side_free1"), 1)
                per = 6
                last_n = max(k for k in range(nj) if jobs[k][0] == "n")

                def job(k, n, u):
                    kind, a, c = jobs[k]
                    if kind in ("tr", "v"):
                        return
                    free = sem(f"x0_side_free{k % 2}")
                    if kind == "pad":
                        dve.sem_inc(free, 1)
                        return
                    dve.wait_ge(sem("x0_side_ready"), nj * n + k + 1)
                    bank = side(k)
                    if kind in ("q", "k"):
                        dve.wait_ge(sem("x0_high_ready"), stacks * n + count(jobs, "qk", k) + 1)
                        if kind == "q":
                            dst, w, signs = qst[:, u, :, :].rearrange("p j s -> p (j s)"), J * S, core.signs_q
                        else:
                            o, w = CHUNKS[a]
                            dst, signs = kst[:, u, c, o:o + w], core.signs_k
                        split_stack(core, dve, dst, bank[:, 0:w], high[:, k % 2, 0:w], signs[:, 0:1]
                                    ).then_inc(sem("x0_stack_ready"), 1)
                        dve.wait_ge(sem("x0_stack_ready"), stacks * n + count(jobs, "qk", k) + 1)
                        dve.sem_inc(free, 1)
                    elif kind == "n":
                        w = CHUNKS[c][1]
                        nc.vector.tensor_reduce(mx[:, a, c:c + 1], bank[0:S, 0:w], AX_X, ALU.max).then_inc(free, 1)
                        if k == last_n:
                            steps = sem("x0_shift_steps")
                            dve.wait_ge(free, nj // 2 * n + k // 2 + 2)
                            nc.vector.tensor_reduce(negmax[:, :], mx[:, :, :], AX_X, ALU.max, negate=True
                                                    ).then_inc(sem("x0_negmax_ready"), 1)
                    elif kind == "m":
                        steps = sem("x0_shift_steps")
                        psum = bank[0:H, 0:S]
                        if not isinstance(n, int) or n:
                            dve.wait_ge(sem("x0_shift_loaded"), 16 * G * SHIFT * n)
                        nc.vector.tensor_copy(nm3[:, 0, :], psum).then_inc(steps, 1)
                        dve.wait_ge(steps, 4 * n + 1)
                        nc.vector.tensor_tensor(rest[:, :], psum, nm3[:, 0, :], ALU.subtract).then_inc(steps, 1)
                        dve.wait_ge(steps, 4 * n + 2)
                        nc.vector.tensor_copy(nm3[:, 1, :], rest[:, :]).then_inc(steps, 1)
                        dve.wait_ge(steps, 4 * n + 3)
                        nc.vector.tensor_tensor(rest[:, :], rest[:, :], nm3[:, 1, :], ALU.subtract).then_inc(steps, 1)
                        dve.wait_ge(steps, 4 * n + 4)
                        nc.vector.tensor_copy(nm3[:, 2, :], rest[:, :]).then_inc(sem("x0_shift_ready"), 1)
                        dve.sem_inc(free, 1)

                for k in range(nj):
                    job(k, 0, 0)

                def sequence(b, u, more):
                    if more:
                        for k in range(nj):
                            job(k, b + 1, 1 - u)

                run_sequences(dve, sequence)


def hidden_layer(core, pe, up, hidden_free, hidden_psum, base):
    nc, ps = core.nc, core.ps
    for f in range(FT):
        pe.wait_ge(hidden_free, base + f + 1)
        for c in range(2):
            ins = nc.tensor.matmul(ps[:, 2 * (f % 2) + c, 0:HALF], up[:, D * f:D * f + D],
                                   core.xT[:, c * HALF:(c + 1) * HALF], start=True, stop=True)
        ins.then_inc(hidden_psum, 1)


def output_layer(core, pe, down, hidden, bank):
    nc, ps = core.nc, core.ps
    for b in range(NB):
        for f in range(FT):
            ins = nc.tensor.matmul(ps[0:S, bank + b // 4, D * (b % 4):D * (b % 4 + 1)],
                                   hidden[:, f, b * S:(b + 1) * S], down[:, f, :], start=(f == 0), stop=(f == FT - 1))
    return ins


def halves(ap, w):
    return ap.rearrange("p (c n) -> p c n", n=w)


def token_banks(core, bank):
    return core.ps[0:S, bank:bank + 2, :].rearrange("s c (b d) -> s (c b) d", d=D)


def add_gated(core, link, gate, what):
    link(core.nc.vector.scalar_tensor_tensor(
        out=flat(core.x), in0=flat(what), scalar=core.gates[0:S, gate:gate + 1], in1=flat(core.x),
        op0=ALU.mult, op1=ALU.add))


def flat(t):
    return t[:, :, :].rearrange("s b d -> s (b d)")


def feed_forward_phase(core, name, bias, gain, shift, gate):
    nc, sem, ps = core.nc, core.sem, core.ps
    up, up_bias, down = core.dense[name]
    with ExitStack() as own, nc.Block() as block:
        hidden = core.sb(f"{name}_hidden", [D, FT, NTOK], F32, own)

        @block.tensor
        def _(pe):
            pe.wait_ge(sem(f"{name}_loaded"), 48)
            hidden_layer(core, pe, up, sem(f"{name}_hidden_free"), sem(f"{name}_hidden_psum"), 0)
            pe.wait_ge(sem(f"{name}_hidden_free"), 2 + FT)
            output_layer(core, pe, down, hidden, 4).then_inc(sem(f"{name}_out_psum"), 1)
            pe.wait_ge(sem(f"{name}_added"), 1)
            transpose_x(core, pe, core.xn, 6).then_inc(sem(f"{name}_xT_psum"), 1)

        @block.scalar
        def _(act):
            act.sem_inc(sem(f"{name}_hidden_free"), 2)
            for f in range(FT):
                act.wait_ge(sem(f"{name}_hidden_psum"), f + 1)
                nc.scalar.activation(halves(hidden[:, f, :], HALF), ps[:, 2 * (f % 2):2 * (f % 2) + 2, 0:HALF], ACT.Relu,
                                     bias=up_bias[:, f:f + 1]).then_inc(sem(f"{name}_hidden_free"), 1)
            act.wait_ge(sem(f"{name}_xT_psum"), 1)
            nc.scalar.activation(halves(core.xT[:, :], HALF), ps[:, 6:8, 0:HALF], ACT.Copy
                                 ).then_inc(sem(f"{name}_xT_ready"), 1)

        @block.vector
        def _(dve):
            link = chain(core, dve, f"{name}_vector_steps")
            dve.wait_ge(sem(f"{name}_out_psum"), 1)
            dve.wait_ge(sem("expert_rows_loaded"), 48)
            link(nc.vector.tensor_tensor(core.work[:, :, :], token_banks(core, 4), rows(bias), ALU.add))
            link(nc.vector.tensor_tensor(core.work[:, :, :], core.work[:, :, :], core.xn[:, :, :], ALU.add))
            layer_norm(core, link, core.xn, core.work, gain, shift)
            dve.wait_ge(sem("gates_ready"), 1)
            add_gated(core, link, gate, core.xn)
            layer_norm(core, link, core.xn, core.x)
            dve.sem_inc(sem(f"{name}_added"), 1)


def merge_weights_phase(core):
    nc, sem, ps, dram = core.nc, core.sem, core.ps, core.dram
    with ExitStack() as own, nc.Block() as block:
        raw = {n: core.sb(f"raw1_{n}", [D, H, E1], F32, own) for n in ("Wq", "Wk", "Wv")}
        turned = {n: core.sb(f"turned_{n}", [2 * E1, H // 2, D], F32, own) for n in ("Wq", "Wk", "Wv")}
        wo = core.sb("Wo", [2 * E1, H // 2, D], F32, own)

        @block.sync
        def _(sp):
            for n in raw:
                sp.dma_start(raw[n][:, :, :], dram[f"L1_xattn_{n}"].rearrange("h d e -> d h e")
                             ).then_inc(sem(f"{n}_loaded"), 16)
            sp.dma_start(wo[:, :, :], dram["L1_xattn_Wo"].rearrange("(a p) o -> p a o", p=2 * E1)
                         ).then_inc(sem("Wo_loaded"), 16)

        @block.tensor
        def _(pe):
            for k, n in enumerate(raw):
                pe.wait_ge(sem(f"{n}_loaded"), 16)
                for a in range(H // 2):
                    ins = nc.tensor.transpose(ps[:, 2 * k + a // 4, D * (a % 4):D * (a % 4 + 1)],
                                              raw[n][:, 2 * a:2 * a + 2, :].rearrange("d h e -> d (h e)"),
                                              core.ident[:, :])
                ins.then_inc(sem("turned_psum"), 1)
            pe.wait_ge(sem("Wo_loaded"), 16)
            for k, (left, right) in enumerate(((turned["Wq"], turned["Wk"]), (turned["Wv"], wo))):
                pe.wait_ge(sem("turned_ready"), 2 if k == 0 else 3)
                for quarter in range(2):
                    q = 2 * k + quarter
                    pe.wait_ge(sem("turned_ready"), 3)
                    if q >= 2:
                        pe.wait_ge(sem("merged_ready"), q - 1)
                    for h in range(8 * quarter, 8 * quarter + 8):
                        p, a = E1 * (h % 2), h // 2
                        ins = nc.tensor.matmul(ps[:, 2 * (q % 2) + h % 2, D * (a % 4):D * (a % 4 + 1)],
                                               left[p:p + E1, a, :], right[p:p + E1, a, :], start=True, stop=True)
                    ins.then_inc(sem("merged_psum"), 1)

        @block.scalar
        def _(act):
            for k, n in enumerate(raw):
                act.wait_ge(sem("turned_psum"), k + 1)
                nc.scalar.activation(turned[n][:, :, :].rearrange("p (c a) d -> p c (a d)", c=2),
                                     ps[:, 2 * k:2 * k + 2, :], ACT.Copy).then_inc(sem("turned_ready"), 1)

        @block.vector
        def _(dve):
            for q in range(4):
                dst = (core.merged_qk if q < 2 else core.merged_vo)[:, 8 * (q % 2):8 * (q % 2) + 8, :]
                dve.wait_ge(sem("merged_psum"), q + 1)
                nc.vector.tensor_copy(dst.rearrange("d (a r) o -> d r a o", r=2),
                                      ps[:, 2 * (q % 2):2 * (q % 2) + 2, :].rearrange("d r (a o) -> d r a o", a=4)
                                      ).then_inc(sem("merged_ready"), 1)


def side_order_1(more):
    order = []
    for s in range(STEPS + LAG):
        if s == TT + LAG:
            order += [(s, "sum", 0, 0), (s, "sum", 0, 1)]
        if more:
            order += [(s, *JOBS1[k]) for k in job_range(len(JOBS1), s)]
    return order + [(STEPS + LAG, "sum", 1, 0), (STEPS + LAG, "sum", 1, 1)]


def cross_attention_1_phase(core):
    nc, sem, ps = core.nc, core.sem, core.ps
    jobs, nj = JOBS1, len(JOBS1)
    with ExitStack() as own:
        def sb(name, shape, dt=F32):
            return core.sb(name, shape, dt, own)

        ctx = core.ctx
        chigh = sb("x1_context_high", [D, 2, T], F16)
        clow = sb("x1_context_low", [D, 2, T], F16)
        qhigh = sb("x1_queries_high", [D, 2, H * S], F16)
        qlow = sb("x1_queries_low", [D, 2, H * S], F16)
        mask_raw = sb("x1_mask_raw", [S, 2, T], U8)
        masked = sb("x1_masked", [S + SHIFT, 2, T], F16)
        select = sb("x1_select", [S + SHIFT, 2, H, S], F16)
        probs = sb("x1_probs", [128, RING, UNIT * S])
        sums = sb("x1_sums", [128, 2, UNIT * S])
        inverse = sb("x1_inverse", [128, 2, HALF])
        ones = sb("x1_ones", [128, 128])
        junk = sb("x1_junk", [S, 2, 512], F16)
        mx = sb("x1_max", [S, H, NC])
        negmax = sb("x1_negmax", [S, H])
        nm3 = sb("x1_shift", [H, SHIFT, S], F16)
        rest = sb("x1_shift_rest", [H, S])
        averages = core.averages
        splits = count(jobs, ("q", "tr"))

        def base(b):
            return nj + (nj + 4) * b

        def half_base(b):
            return nj // 2 + (nj + 4) // 2 * b

        with nc.Block() as block:
            @block.sync
            def _(sp):
                def load(b, u):
                    load_context_tiles(core, sp, b, u, sem("x1_context_loaded"))
                    sp.dma_start(mask_raw[:, u, :],
                                 core.dram["mask_BxSxS2_bf1"][bass.ds(b, 1), :, :].rearrange("o s t -> (o s) t")
                                 ).then_inc(sem("x1_mask_loaded"), 16)

                def shift_rows(n, u):
                    sp.wait_ge(sem("x1_shift_ready"), n + 1)
                    for r in range(SHIFT):
                        sp.dma_start(select[S + r:S + r + 1, u, :, :].rearrange("o h s -> o (h s)"), nm3[:, r, :]
                                     ).then_inc(sem("x1_shift_loaded"), 16)

                load(0, 0)
                sp.wait_ge(sem("x1_select_ready"), 1)
                shift_rows(0, 0)

                def sequence(b, u, more):
                    if more:
                        sp.wait_ge(sem("x1_product_done"), STEPS * b + RING)
                        load(b + 1, 1 - u)
                        shift_rows(b + 1, 1 - u)

                run_sequences(sp, sequence)

            @block.gpsimd
            def _(pool):
                pool.memset(ones[:, :], 1.0)
                pool.memset(masked[:, :, :], 1.0).then_inc(sem("x1_ones_ready"), 1)
                for u in range(2):
                    ins = pool.tensor_copy(select[0:S, u, :, :],
                                           core.ident4[:, 0:1, :].broadcast_to([S, H, S]))
                ins.then_inc(sem("x1_select_ready"), 1)
                pool.sem_inc(sem("x1_sums_used"), 2)
                pool.wait_ge(sem("x1_ones_ready"), 1)

                def additive_mask(n, u):
                    pool.wait_ge(sem("x1_mask_loaded"), 16 * (n + 1))
                    wait_apart(pool, sem("pool_waits"))
                    pool.tensor_scalar(masked[0:S, u, :], mask_raw[:, u, :], -MASKED, MASKED, ALU.mult, ALU.add
                                       ).then_inc(sem("x1_mask_ready"), 1)

                additive_mask(0, 0)

                def sequence(b, u, more):
                    for s in range(STEPS):
                        unit, t = s // TT, s % TT
                        if s == 1 and more:
                            additive_mask(b + 1, 1 - u)
                        pool.wait_ge(sem("x1_probs_ready"), STEPS * b + s + 1 + 2)
                        dst, src = sums[0:ROWS[t], unit, :], probs[0:ROWS[t], s % RING, :]
                        if t == 0:
                            pool.wait_ge(sem("x1_sums_used"), 2 * b + unit + 1)
                            wait_apart(pool, sem("pool_waits"))
                            ins = pool.tensor_copy(dst, src)
                        else:
                            pool.wait_ge(sem("x1_sums_done"), STEPS * b + s + RING)
                            ins = pool.tensor_tensor(dst, dst, src, ALU.add)
                        ins.then_inc(sem("x1_sums_done"), 1)

                run_sequences(pool, sequence)

            @block.tensor
            def _(pe):
                def job(kind, a, c, p, n, u, before, half_before):
                    pe.wait_ge(sem(f"x1_side_free{p % 2}"), half_before + p // 2 + 1)
                    bank = ps[:, SIDE + p % 2, :]
                    if kind == "q":
                        for h in range(HC * a, HC * a + HC):
                            ins = nc.tensor.matmul(bank[:, (h % HC) * S:(h % HC + 1) * S], core.merged_qk[:, h, :],
                                                   core.xT[:, bass.ds(n * S, S)], start=True, stop=True)
                    elif kind == "tr":
                        if a == 0:
                            pe.wait_ge(sem("x1_context_loaded"), 32 * n + 32)
                        for t in range(GT * a, GT * a + GT):
                            o = OFF[t] - CHUNKS[a][0]
                            ins = nc.tensor.transpose(bank[:, o:o + ROWS[t]], ctx[0:ROWS[t], u, t, :],
                                                      core.ident[0:ROWS[t], 0:ROWS[t]])
                    elif kind == "n":
                        if a == 0 and c == 0:
                            pe.wait_ge(sem("x1_high_ready"), splits * (n + 1))
                        o, w = CHUNKS[c]
                        ins = nc.tensor.matmul(bank[0:S, 0:w], qhigh[:, u, a * S:(a + 1) * S], chigh[:, u, o:o + w],
                                               start=True, stop=True)
                    elif kind == "m":
                        pe.wait_ge(sem("x1_negmax_ready"), n + 1)
                        ins = nc.tensor.transpose(bank[0:H, 0:S], negmax[:, :], core.ident[0:S, 0:S])
                    else:
                        if c == 0:
                            pe.wait_ge(sem("x1_sums_done"), STEPS * n + TT * (a + 1) + RING)
                        ins = nc.tensor.matmul(bank[:, 0:HALF], ones[0:ROWS[0], :],
                                               sums[0:ROWS[0], a, c * HALF:(c + 1) * HALF], start=True, stop=True)
                        if c == 1:
                            ins.then_inc(sem("x1_side_ready"), 1)
                            return ins
                    ins.then_inc(sem("x1_side_ready"), 1)

                pe.wait_ge(sem("x1_ones_ready"), 1)
                pe.wait_ge(sem("x1_select_ready"), 1)
                for k in range(nj):
                    job(*jobs[k], k, 0, 0, 0, 0)

                def values_product(b, u, v):
                    unit, t = v // TT, v % TT
                    if t == 0:
                        pe.wait_ge(sem("x1_averages_ready"), 4 * b + 2 * unit + 2)
                    pe.wait_ge(sem("x1_probs_ready"), STEPS * b + v + 1 + 2)
                    for c in range(2):
                        ins = nc.tensor.matmul(ps[:, ACC + c, 0:HALF], ctx[0:ROWS[t], u, t, :],
                                               probs[0:ROWS[t], v % RING, c * HALF:(c + 1) * HALF],
                                               start=(t == 0), stop=(t == TT - 1))
                    ins.then_inc(sem("x1_product_done"), 1)

                def sequence(b, u, more):
                    order = side_order_1(more)
                    for s in range(STEPS + LAG + 1):
                        mine = [(p, o) for p, o in enumerate(order) if o[0] == s]
                        for p, (_, kind, a, c) in mine:
                            if kind == "sum":
                                job(kind, a, c, p, b, u, None, half_base(b))
                        if s < STEPS:
                            unit, t = s // TT, s % TT
                            if s == 0:
                                pe.wait_ge(sem("x1_shift_loaded"), 16 * SHIFT * (b + 1))
                                pe.wait_ge(sem("x1_low_ready"), splits * (b + 1))
                                pe.wait_ge(sem("x1_mask_ready"), b + 1)
                            pe.wait_ge(sem("x1_probs_ready"), STEPS * b + s + 1)
                            r, o = ROWS[t], OFF[t]
                            for k, (left, right) in enumerate(((chigh, qhigh), (chigh, qlow), (clow, qhigh))):
                                for c in range(2):
                                    q0 = (UNIT * unit + HC * c) * S
                                    nc.tensor.matmul(ps[0:r, 2 * (s % 2) + c, 0:HALF], left[:, u, o:o + r],
                                                     right[:, u, q0:q0 + HALF], start=(k == 0), stop=False)
                            for c in range(2):
                                h0 = UNIT * unit + HC * c
                                ins = nc.tensor.matmul(ps[0:r, 2 * (s % 2) + c, 0:HALF], masked[:, u, o:o + r],
                                                       select[:, u, h0:h0 + HC, :].rearrange("p h s -> p (h s)"),
                                                       start=False, stop=True)
                            ins.then_inc(sem("x1_scores_ready"), 1)
                        for p, (_, kind, a, c) in mine:
                            if kind != "sum":
                                job(kind, a, c, p, b + 1, 1 - u, None, half_base(b))
                        if LAG <= s < STEPS + LAG:
                            values_product(b, u, s - LAG)

                run_sequences(pe, sequence)

            @block.scalar
            def _(act):
                act.sem_inc(sem("x1_probs_ready"), 2)

                def job(kind, a, c, p, n, u, before):
                    if kind not in ("q", "tr"):
                        return
                    act.wait_ge(sem("x1_side_ready"), before + p + 1)
                    bank = ps[:, SIDE + p % 2, :]
                    if kind == "q":
                        dst, w = qhigh[:, u, HALF * a:HALF * (a + 1)], HALF
                    else:
                        o, w = CHUNKS[a]
                        dst = chigh[:, u, o:o + w]
                    nc.scalar.activation(dst, bank[:, 0:w], ACT.Copy).then_inc(sem("x1_high_ready"), 1)

                for k in range(nj):
                    job(*jobs[k], k, 0, 0, 0)

                def sequence(b, u, more):
                    order = side_order_1(more)
                    for s in range(STEPS + LAG + 1):
                        if s < STEPS:
                            r = ROWS[s % TT]
                            act.wait_ge(sem("x1_scores_ready"), STEPS * b + s + 1)
                            act.wait_ge(sem("x1_product_done"), STEPS * b + s + 1)
                            act.wait_ge(sem("x1_sums_done"), STEPS * b + s + 1)
                            nc.scalar.activation(halves(probs[0:r, s % RING, :], HALF),
                                                 ps[0:r, 2 * (s % 2):2 * (s % 2) + 2, 0:HALF], ACT.Exp, scale=SCALE1
                                                 ).then_inc(sem("x1_probs_ready"), 1)
                        for p, (at, kind, a, c) in enumerate(order):
                            if at == s:
                                job(kind, a, c, p, b + 1, 1 - u, base(b))

                run_sequences(act, sequence)

            @block.vector
            def _(dve):
                dve.sem_inc(sem("x1_product_done"), RING)
                dve.sem_inc(sem("x1_sums_done"), RING)
                dve.sem_inc(sem("x1_averages_ready"), 2)
                dve.sem_inc(sem("x1_side_free0"), 1)
                dve.sem_inc(sem("x1_side_free1"), 1)
                last_n = [j for j in jobs if j[0] == "n"][-1]

                def job(kind, a, c, p, n, u, before, half_before, splits_before):
                    free = sem(f"x1_side_free{p % 2}")
                    dve.wait_ge(sem("x1_side_ready"), before + p + 1)
                    bank = ps[:, SIDE + p % 2, :]
                    if kind in ("q", "tr"):
                        dve.wait_ge(sem("x1_high_ready"), splits * n + splits_before + 1)
                        if kind == "q":
                            high, low, w = qhigh, qlow, HALF
                            o = HALF * a
                        else:
                            high, low, (o, w) = chigh, clow, CHUNKS[a]
                        nc.vector.tensor_tensor(low[:, u, o:o + w], bank[:, 0:w], high[:, u, o:o + w], ALU.subtract
                                                ).then_inc(sem("x1_low_ready"), 1)
                        dve.wait_ge(sem("x1_low_ready"), splits * n + splits_before + 1)
                        dve.sem_inc(free, 1)
                    elif kind == "n":
                        o, w = CHUNKS[c]
                        if a == 0 and c == 0:
                            dve.wait_ge(sem("x1_mask_ready"), n + 1)
                        wait_apart(dve, sem("vector_waits"))
                        nc.vector.tensor_tensor_reduce(junk[:, p % 2, 0:w], bank[0:S, 0:w], masked[0:S, u, o:o + w],
                                                       1.0, -3.0e38, ALU.add, ALU.max, mx[:, a, c:c + 1]
                                                       ).then_inc(free, 1)
                        if (kind, a, c) == last_n:
                            dve.wait_ge(free, half_before + p // 2 + 2)
                            nc.vector.tensor_reduce(negmax[:, :], mx[:, :, :], AX_X, ALU.max, negate=True
                                                    ).then_inc(sem("x1_negmax_ready"), 1)
                    elif kind == "m":
                        steps = sem("x1_shift_steps")
                        psum = bank[0:H, 0:S]
                        if not isinstance(n, int) or n:
                            dve.wait_ge(sem("x1_shift_loaded"), 16 * SHIFT * n)
                        nc.vector.tensor_copy(nm3[:, 0, :], psum).then_inc(steps, 1)
                        dve.wait_ge(steps, 4 * n + 1)
                        nc.vector.tensor_tensor(rest[:, :], psum, nm3[:, 0, :], ALU.subtract).then_inc(steps, 1)
                        dve.wait_ge(steps, 4 * n + 2)
                        nc.vector.tensor_copy(nm3[:, 1, :], rest[:, :]).then_inc(steps, 1)
                        dve.wait_ge(steps, 4 * n + 3)
                        nc.vector.tensor_tensor(rest[:, :], rest[:, :], nm3[:, 1, :], ALU.subtract).then_inc(steps, 1)
                        dve.wait_ge(steps, 4 * n + 4)
                        nc.vector.tensor_copy(nm3[:, 2, :], rest[:, :]).then_inc(sem("x1_shift_ready"), 1)
                        dve.sem_inc(free, 1)
                    else:
                        nc.vector.reciprocal(inverse[:, c, :], bank[:, 0:HALF]).then_inc(free, 1)
                        if c == 1:
                            dve.sem_inc(sem("x1_sums_used"), 1)
                        dve.wait_ge(free, half_before + p // 2 + 2)
                        dve.wait_ge(sem("x1_product_done"), STEPS * n + TT * (a + 1) + RING)
                        h0 = (UNIT * a + HC * c) * S
                        nc.vector.tensor_tensor(averages[:, bass.ds(n, 1), h0:h0 + HALF],
                                                ps[:, ACC + c, 0:HALF].unsqueeze(1), inverse[:, c, :].unsqueeze(1),
                                                ALU.mult).then_inc(sem("x1_averages_ready"), 1)

                for k in range(nj):
                    job(*jobs[k], k, 0, 0, 0, 0, count(jobs, ("q", "tr"), k))

                def sequence(b, u, more):
                    seen = 0
                    for p, (_, kind, a, c) in enumerate(side_order_1(more)):
                        if kind == "sum":
                            job(kind, a, c, p, b, u, base(b), half_base(b), seen)
                        else:
                            job(kind, a, c, p, b + 1, 1 - u, base(b), half_base(b), seen)
                            seen += kind in ("q", "tr")

                run_sequences(dve, sequence)


def project_averages_phase(core):
    nc, sem, ps = core.nc, core.sem, core.ps
    with nc.Block() as block:
        @block.tensor
        def _(pe):
            for b in range(NB):
                for h in range(H):
                    ins = nc.tensor.matmul(ps[0:S, 4 + b // 4, D * (b % 4):D * (b % 4 + 1)],
                                           core.averages[:, b, h * S:(h + 1) * S], core.merged_vo[:, h, :],
                                           start=(h == 0), stop=(h == H - 1))
            ins.then_inc(sem("projected_psum"), 1)
            pe.wait_ge(sem("projected_added"), 1)
            transpose_x(core, pe, core.xn, 6).then_inc(sem("projected_xT_psum"), 1)

        @block.scalar
        def _(act):
            act.wait_ge(sem("projected_xT_psum"), 1)
            nc.scalar.activation(halves(core.xT[:, :], HALF), ps[:, 6:8, 0:HALF], ACT.Copy
                                 ).then_inc(sem("projected_xT_ready"), 1)

        @block.vector
        def _(dve):
            link = chain(core, dve, "projected_vector_steps")
            dve.wait_ge(sem("projected_psum"), 1)
            link(nc.vector.tensor_copy(core.work[:, :, :], token_banks(core, 4)))
            add_gated(core, link, 1, core.work)
            layer_norm(core, link, core.xn, core.x)
            dve.sem_inc(sem("projected_added"), 1)


def experts_phase(core):
    nc, sem, ps, dram = core.nc, core.sem, core.ps, core.dram
    with ExitStack() as own:
        def sb(name, shape, dt=F32):
            return core.sb(name, shape, dt, own)

        gate_w = sb("gate_w", [D, NE])
        gate_b = sb("gate_b", [S, NE])
        up = sb("expert_up", [D, 2, FF])
        up_bias = sb("expert_up_bias", [D, 2, FT])
        down = sb("expert_down", [D, 2, FT, D])
        b2 = sb("expert_b2", [NE, D])
        hidden = sb("expert_hidden", [D, FT, NTOK])
        logits = sb("router_scores", [S, NB, NE])
        best = sb("router_best", [S, NB, NE])
        greater = sb("router_greater", [S, NB, NE, NE])
        equal = sb("router_equal", [S, NB, NE, NE])
        lower = sb("router_lower", [S, NE, NE])
        rank = sb("router_rank", [S, NB, NE])
        e2 = sb("router_second", [S, NB])
        w1 = sb("router_w1", [S, NB])
        w2 = sb("router_w2", [S, NB])
        comb = sb("router_weights", [S, NB, NE])
        second = sb("router_weights_second", [S, NB, NE])
        combT = sb("router_weightsT", [NE, NTOK])
        part = sb("expert_part", [S, NB, D])

        def over_features(ap):
            return ap.broadcast_to([S, NB, D])

        with nc.Block() as block:
            @block.sync
            def _(sp):
                sp.dma_start(gate_w[:, :], dram["L1_ffn_gate_w"]).then_inc(sem("router_loaded"), 16)
                sp.dma_start(gate_b[:, :], dram["L1_ffn_gate_b"].rearrange("(o e) -> o e", o=1).broadcast_to([S, NE])
                             ).then_inc(sem("router_loaded"), 16)
                sp.dma_start(b2[:, :], dram["L1_ffn_b2"]).then_inc(sem("router_loaded"), 16)

                with sp.Fori(0, NE // 2) as i:
                    for u in range(2):
                        e = 2 * i + u
                        sp.wait_ge(sem("expert_used"), e + 1)
                        sp.dma_start(up[:, u, :], dram["L1_ffn_w1"][bass.ds(e, 1), :, :].rearrange("o d f -> (o d) f")
                                     ).then_inc(sem(f"expert_weights_loaded{u}"), 16)
                        sp.dma_start(up_bias[:, u, :], dram["L1_ffn_b1"][bass.ds(e, 1), :].rearrange(
                            "o (f p) -> (o p) f", p=D), allow_slow_non_contiguous=True).then_inc(sem(f"expert_weights_loaded{u}"), 16)
                        sp.dma_start(down[:, u, :, :], dram["L1_ffn_w2"][bass.ds(e, 1), :, :].rearrange(
                            "o (f p) d -> (o p) f d", p=D)).then_inc(sem(f"expert_weights_loaded{u}"), 16)

            @block.gpsimd
            def _(pool):
                pool.memset(lower[:, :, :], 1.0).then_inc(sem("router_lower_ready"), 1)
                pool.wait_ge(sem("router_lower_ready"), 1)
                pool.affine_select(out=lower[:, :, :], in_=lower[:, :, :], compare_op=ALU.is_gt, fill=0.0, base=0,
                                   pattern=[[1, NE], [-1, NE]], channel_multiplier=0
                                   ).then_inc(sem("router_lower_ready"), 1)

            @block.tensor
            def _(pe):
                pe.wait_ge(sem("router_loaded"), 48)
                for b in range(NB):
                    ins = nc.tensor.matmul(ps[0:S, 6, NE * b:NE * (b + 1)], core.xT[:, b * S:(b + 1) * S], gate_w[:, :],
                                           start=True, stop=True)
                ins.then_inc(sem("router_psum"), 1)
                with pe.Fori(0, NE // 2) as i:
                    for u in range(2):
                        e = 2 * i + u
                        pe.wait_ge(sem(f"expert_weights_loaded{u}"), 48 * i + 48)
                        hidden_layer(core, pe, up[:, u, :], sem("expert_hidden_free"), sem("expert_hidden_psum"), FT * e)
                        pe.wait_ge(sem("expert_hidden_free"), FT * e + FT + 2)
                        pe.wait_ge(sem("expert_out_free"), e + 1)
                        output_layer(core, pe, down[:, u, :, :], hidden, 4).then_inc(sem("expert_out_psum"), 1)
                pe.wait_ge(sem("router_weights_ready"), 1)
                for b in range(NB):
                    ins = nc.tensor.transpose(ps[0:NE, 6 + b // 4, (b % 4) * S:(b % 4 + 1) * S], comb[:, b, :],
                                              core.ident[0:S, 0:S])
                ins.then_inc(sem("router_weightsT_psum"), 1)
                pe.wait_ge(sem("router_weightsT_ready"), 1)
                for b in range(NB):
                    ins = nc.tensor.matmul(ps[0:S, b // 4, D * (b % 4):D * (b % 4 + 1)], combT[:, b * S:(b + 1) * S],
                                           b2[:, :], start=True, stop=True)
                ins.then_inc(sem("expert_bias_psum"), 1)

            @block.scalar
            def _(act):
                act.sem_inc(sem("expert_hidden_free"), 2)
                act.wait_ge(sem("router_gap_ready"), 1)
                nc.scalar.activation(e2[:, :], e2[:, :], ACT.Exp).then_inc(sem("router_exp_ready"), 1)
                with act.Fori(0, NE // 2) as i:
                    for u in range(2):
                        e = 2 * i + u
                        act.wait_ge(sem("expert_out_psum"), e + 1)
                        act.wait_ge(sem(f"expert_weights_loaded{u}"), 48 * i + 48)
                        for f in range(FT):
                            act.wait_ge(sem("expert_hidden_psum"), FT * e + f + 1)
                            nc.scalar.activation(halves(hidden[:, f, :], HALF),
                                                 ps[:, 2 * (f % 2):2 * (f % 2) + 2, 0:HALF], ACT.Relu,
                                                 bias=up_bias[:, u, f:f + 1]).then_inc(sem("expert_hidden_free"), 1)
                act.wait_ge(sem("router_weightsT_psum"), 1)
                nc.scalar.activation(halves(combT[:, :], HALF), ps[0:NE, 6:8, 0:HALF], ACT.Copy
                                     ).then_inc(sem("router_weightsT_ready"), 1)

            @block.vector
            def _(dve):
                dve.sem_inc(sem("expert_used"), 2)
                dve.sem_inc(sem("expert_out_free"), 1)
                dve.sem_inc(sem("expert_out_psum"), 1)
                link = chain(core, dve, "router_steps")
                dve.wait_ge(sem("router_psum"), 1)
                link(nc.vector.tensor_tensor(logits[:, :, :], ps[0:S, 6, 0:NB * NE].rearrange("s (b e) -> s b e", e=NE),
                                             gate_b[:, :].unsqueeze(1).broadcast_to([S, NB, NE]), ALU.add))
                for b in range(NB):
                    ins = nc.vector.max(best[:, b, :], logits[:, b, :])
                link(ins)
                nc.vector.tensor_tensor(e2[:, :], best[:, :, 1], best[:, :, 0], ALU.subtract
                                        ).then_inc(sem("router_gap_ready"), 1)
                dve.wait_ge(sem("router_lower_ready"), 2)
                for b in range(NB):
                    other = logits[:, b, :].unsqueeze(1).broadcast_to([S, NE, NE])
                    mine = logits[:, b, :].unsqueeze(2).broadcast_to([S, NE, NE])
                    nc.vector.tensor_tensor(greater[:, b, :, :], other, mine, ALU.is_gt)
                    ins = nc.vector.tensor_tensor(equal[:, b, :, :], other, mine, ALU.is_equal)
                link(ins)
                link(nc.vector.tensor_tensor(
                    equal[:, :, :, :].rearrange("s b e f -> s b (e f)"), equal[:, :, :, :].rearrange("s b e f -> s b (e f)"),
                    lower[:, :, :].rearrange("s e f -> s (e f)").unsqueeze(1).broadcast_to([S, NB, NE * NE]), ALU.mult))
                link(nc.vector.tensor_tensor(greater[:, :, :, :].rearrange("s b e f -> s (b e f)"),
                                             greater[:, :, :, :].rearrange("s b e f -> s (b e f)"),
                                             equal[:, :, :, :].rearrange("s b e f -> s (b e f)"), ALU.add))
                link(nc.vector.tensor_reduce(rank[:, :, :], greater[:, :, :, :], AX_X, ALU.add))
                dve.wait_ge(sem("router_exp_ready"), 1)
                link(nc.vector.tensor_scalar(w1[:, :], e2[:, :], 1.0, None, ALU.add))
                link(nc.vector.reciprocal(w1[:, :], w1[:, :]))
                link(nc.vector.tensor_tensor(w2[:, :], e2[:, :], w1[:, :], ALU.mult))
                nc.vector.tensor_scalar(comb[:, :, :], rank[:, :, :], 0.0, None, ALU.is_equal)
                link(nc.vector.tensor_scalar(second[:, :, :], rank[:, :, :], 1.0, None, ALU.is_equal))
                link(nc.vector.tensor_tensor(comb[:, :, :], comb[:, :, :],
                                             w1[:, :].unsqueeze(2).broadcast_to([S, NB, NE]), ALU.mult))
                link(nc.vector.tensor_tensor(second[:, :, :], second[:, :, :],
                                             w2[:, :].unsqueeze(2).broadcast_to([S, NB, NE]), ALU.mult))
                link(nc.vector.tensor_tensor(comb[:, :, :], comb[:, :, :], second[:, :, :], ALU.add))
                dve.sem_inc(sem("router_weights_ready"), 1)
                link(nc.vector.memset(core.work[:, :, :], 0.0))

                with dve.Fori(0, NE // 2) as i:
                    for u in range(2):
                        e = 2 * i + u
                        dve.wait_ge(sem("expert_out_psum"), e + 2)
                        dve.sem_inc(sem("expert_used"), 1)
                        nc.vector.tensor_tensor(part[:, :, :], token_banks(core, 4), over_features(comb[:, :, bass.ds(e, 1)]),
                                                ALU.mult).then_inc(sem("expert_out_free"), 1)
                        dve.wait_ge(sem("expert_out_free"), e + 2)
                        nc.vector.tensor_tensor(core.work[:, :, :], core.work[:, :, :], part[:, :, :], ALU.add
                                                ).then_inc(sem("expert_added"), 1)
                        dve.wait_ge(sem("expert_added"), e + 1)
                dve.wait_ge(sem("expert_bias_psum"), 1)
                link(nc.vector.tensor_tensor(core.work[:, :, :], core.work[:, :, :], token_banks(core, 0), ALU.add))
                add_gated(core, link, 3, core.work)


INPUTS = ["x", "ctx_1024", "mask_BxSxS2_bf1", "g_xattn", "g_ffn"] + [
    f"L0_xattn_{n}" for n in ("Wq1", "Wk1", "Wv1", "bv1", "Wq2", "Wk2", "Wv2", "bv2", "g1", "be1", "g2", "be2", "g3",
                              "be3", "Wf1", "bf1", "Wf2", "bf2")] + [
    f"L0_ffn_{n}" for n in ("w1", "b1", "w2", "b2", "gamma", "beta")] + [
    f"L1_xattn_{n}" for n in ("Wq", "Wk", "Wv", "Wo")] + [
    f"L1_ffn_{n}" for n in ("gate_w", "gate_b", "w1", "b1", "w2", "b2")]


def store_phase(core, what):
    nc, sem = core.nc, core.sem
    with nc.Block() as block:
        @block.sync
        def _(sp):
            sp.dma_start(core.out.rearrange("b s d -> s b d"), what[:, :, :]).then_inc(sem("out_stored"), 16)
            sp.wait_ge(sem("out_stored"), 16)


def program(nc, dram, out):
    with ExitStack() as stack:
        core = Core(nc, stack, dram, out)
        core.oT = core.sb("oT", [128, NB, G * S])
        core.negmax = core.sb("negmax", [S, G * J * NB])
        core.row_sums = core.sb("row_sums", [S, NB, G, J])
        core.ctx = core.sb("context", [128, 2, TT, D])
        setup_phase(core)
        self_attention_phase(core)
        finish_attention_phase(core, "self")
        cross_attention_0_phase(core)
        finish_attention_phase(core, "cross")
        feed_forward_phase(core, "ffn", core.row["bf2"], core.row["g3"], core.row["be3"], 0)
        feed_forward_phase(core, "expert0", core.row_e["b2"], core.row_e["gamma"], core.row_e["beta"], 2)
        core.averages = core.sb("averages", [D, NB, H * S])
        core.merged_qk = core.sb("merged_qk", [D, H, D])
        core.merged_vo = core.sb("merged_vo", [D, H, D])
        merge_weights_phase(core)
        cross_attention_1_phase(core)
        project_averages_phase(core)
        experts_phase(core)
        store_phase(core, core.x)


def kernel(**inputs):
    import numpy as _np
    import concourse.bacc as _bacc
    from concourse import mybir as _mybir
    from concourse.bass_utils import run_bass_kernel_spmd as _run

    nc = _bacc.Bacc("TRN2", target_bir_lowering=False, num_devices=1)
    arrays, dram = {}, {}
    for name in INPUTS:
        a = _np.ascontiguousarray(inputs[name])
        if a.dtype == _np.bool_:
            a = a.view(_np.uint8)
        arrays[f"in_{name}"] = a
        dram[name] = nc.dram_tensor(f"in_{name}", a.shape, _mybir.dt.from_np(a.dtype), kind="ExternalInput").ap()
    out = nc.dram_tensor("out_x", (NB, S, D), _mybir.dt.float32, kind="ExternalOutput").ap()
    program(nc, dram, out)
    return _run(nc, [arrays], core_ids=[0]).results[0]["out_x"]
```

```python
from contextlib import ExitStack

import concourse.bass as bass
from concourse import mybir

F32 = mybir.dt.float32
F16 = mybir.dt.float16
U8 = mybir.dt.uint8
I32 = mybir.dt.int32
ALU = mybir.AluOpType
ACT = mybir.ActivationFunctionType
AX_X = mybir.AxisListType.X

NB, S, D, T, H = 8, 100, 128, 1444, 16
NTOK = NB * S
HALF = NTOK // 2
G, J = 4, 4
E0 = D // H
STACK = 3 * E0
SHIFT = 3
E1 = 64
FF = 512
FT = FF // D
NE = 8
EPS = 1e-5

HC = 4
UNIT = H // 2
MASKED = -60000.0
TT = -(-T // 128)
ROWS = [T // TT + (t < T % TT) for t in range(TT)]
OFF = [sum(ROWS[:t]) for t in range(TT)]
NG = 3
GT = TT // NG
CHUNKS = [(OFF[GT * q], sum(ROWS[GT * q:GT * q + GT])) for q in range(NG)]
NC = NG
TALL = T % TT
assert TT == NG * GT and TALL == GT and max(w for _, w in CHUNKS) <= 512
SCALE0 = float(E0) ** -0.5
SCALE1 = float(S) ** -0.5
STEPS = 2 * TT
LAG = 2
RING = 4
JOB_STEPS0 = (1, 22)
JOB_STEPS1 = (2, 21)
N_WEIGHT = 2.5
ACC = 4
SIDE0, SIDES0 = 5, 3
SIDE1, SIDES1 = 6, 2


MARKS = [(E0, 2 * E0, -1.0), (STACK, STACK + SHIFT, 1.0), (2 * E0, STACK, -1.0), (STACK, STACK + SHIFT, 1.0)]


def spread(jobs, first, last):
    weights = [N_WEIGHT if job[0] == "n" else 1.0 for job in jobs]
    steps = [[] for _ in range(STEPS)]
    for k in range(len(jobs)):
        steps[first + int((last - first) * sum(weights[:k]) / sum(weights))].append(k)
    return steps


JOBS0 = ([("q", p, 0) for p in range(2)] + [("tr", q, 0) for q in range(NG)]
         + [("k", c, j) for c in range(NC) for j in range(J)]
         + [("v", q, 0) for q in range(NG)]
         + [("n", h, c) for h in range(H) for c in range(NC)] + [("m", 0, 0)])
assert len(JOBS0) % SIDES0 == 0
JOBS1 = ([("q", q, 0) for q in range(H // HC)] + [("tr", q, 0) for q in range(NG)]
         + [("n", h, c) for h in range(H) for c in range(NC)] + [("m", 0, 0)])
assert len(JOBS1) % SIDES1 == 0
AT_STEP0, AT_STEP1 = spread(JOBS0, *JOB_STEPS0), spread(JOBS1, *JOB_STEPS1)


def count(jobs, kinds, k=None):
    return sum(job[0] in kinds for job in jobs[:k])


class Core:

    def __init__(self, nc, stack, dram, out):
        self.nc, self.stack, self.dram, self.out = nc, stack, dram, out
        self.sems = {}

    def sem(self, name):
        if name not in self.sems:
            self.sems[name] = self.stack.enter_context(self.nc.semaphore(name))
        return self.sems[name]

    def sb(self, name, shape, dt=F32, stack=None):
        return (stack or self.stack).enter_context(self.nc.sbuf_tensor(name, shape, dt))


def chain(core, eng, name):
    done, n = core.sem(name), [0]

    def link(ins):
        n[0] += 1
        ins.then_inc(done, 1)
        eng.wait_ge(done, n[0])

    return link


def inverse_root(core, link, root, var):
    nc, half, t = core.nc, core.ln_half[:, :], core.ln_t[:, :]
    link(nc.vector.tensor_scalar(root, var, EPS, None, ALU.add))
    link(nc.vector.tensor_scalar(half, root, -0.5, None, ALU.mult))
    link(nc.vector.tensor_scalar(root.bitcast(I32), root.bitcast(I32), -0.5, float(0x5F3759DF), ALU.mult, ALU.add))
    for _ in range(3):
        link(nc.vector.tensor_tensor(t, root, root, ALU.mult))
        link(nc.vector.tensor_tensor(t, t, half, ALU.mult))
        link(nc.vector.scalar_tensor_tensor(out=root, in0=t, scalar=1.5, in1=root, op0=ALU.add, op1=ALU.mult))


def layer_norm(core, link, dst, src, gain=None, shift=None):
    nc, st, mv, rstd = core.nc, core.ln_stats, core.ln_mv, core.ln_rstd
    for b in range(NB):
        ins = nc.vector.bn_stats(st[:, b, :], src[:, b, :])
    link(ins)
    for b in range(NB):
        ins = nc.vector.bn_aggr(mv[:, b, :], st[:, b, :])
    link(ins)
    inverse_root(core, link, rstd[:, :], mv[:, :, 1])
    for b in range(NB):
        ins = nc.vector.tensor_scalar(dst[:, b, :], src[:, b, :], mv[:, b, 0:1], rstd[:, b:b + 1],
                                      ALU.subtract, ALU.mult)
    link(ins)
    if gain is not None:
        link(nc.vector.tensor_tensor(dst[:, :, :], dst[:, :, :], rows(gain), ALU.mult))
        link(nc.vector.tensor_tensor(dst[:, :, :], dst[:, :, :], rows(shift), ALU.add))


def rows(row):
    return row[0:S, :].unsqueeze(1).broadcast_to([S, NB, D])


def transpose_x(core, pe, src, bank):
    for b in range(NB):
        ins = core.nc.tensor.transpose(core.ps[:, bank + b // 4, (b % 4) * S:(b % 4 + 1) * S],
                                       src[:, b, :], core.ident[0:S, 0:S])
    return ins


def split_stack(core, eng, dst, psum, high, signs):
    return core.nc.vector.scalar_tensor_tensor(out=dst, in0=high, scalar=signs, in1=psum,
                                               op0=ALU.mult, op1=ALU.add)


def shift_parts(core, link, nm3, psum, rest):
    nc = core.nc
    link(nc.vector.tensor_copy(nm3[:, 0, :], psum))
    link(nc.vector.tensor_tensor(rest, psum, nm3[:, 0, :], ALU.subtract))
    link(nc.vector.tensor_copy(nm3[:, 1, :], rest))
    link(nc.vector.tensor_tensor(rest, rest, nm3[:, 1, :], ALU.subtract))
    return nc.vector.tensor_copy(nm3[:, 2, :], rest)


def setup_phase(core):
    nc, dram, sem, sb = core.nc, core.dram, core.sem, core.sb
    core.ps = core.stack.enter_context(nc.psum_tensor("psum", [128, 8, 512], F32))
    core.x = sb("x", [S, NB, D])
    core.xn = sb("normalised", [S, NB, D])
    core.work = sb("work", [S, NB, D])
    core.xT = sb("xT", [D, NTOK])
    core.ident = sb("identity", [128, 128])
    core.ident4 = sb("identity_heads", [S, J, S], F16)
    core.causal4 = sb("causal_heads", [S, J, S], F16)
    core.ln_stats = sb("ln_stats", [S, NB, 6])
    core.ln_mv = sb("ln_mean_var", [S, NB, 2])
    core.ln_rstd = sb("ln_rstd", [S, NB])
    core.ln_half = sb("ln_half", [S, NB])
    core.ln_t = sb("ln_t", [S, NB])
    core.signs_k = sb("signs_keys", [128, 1])
    core.signs_q = sb("signs_queries", [128, 1])
    core.ones_k = sb("ones_keys", [128, 1])
    core.gates = sb("gates", [128, 4])
    core.wstack = {n: sb(f"stack_{n}", [D, J, 128]) for n in ("Wq1", "Wk1", "Wq2", "Wk2")}
    core.wraw = {n: sb(f"raw_{n}", [D, H, E0]) for n in ("Wq1", "Wk1", "Wv1", "Wq2", "Wk2", "Wv2")}
    names = {"bv1": H * E0, "bv2": H * E0, "g1": D, "be1": D, "g2": D, "be2": D, "g3": D, "be3": D,
             "bf2": D}
    core.row = {n: sb(f"row_{n}", [S, w]) for n, w in names.items()}
    core.row_e = {n: sb(f"row_{n}", [S, D]) for n in ("b2", "gamma", "beta")}
    core.dense = {n: (sb(f"{n}_up", [D, FF]), sb(f"{n}_up_bias", [D, FT]), sb(f"{n}_down", [D, FT, D]))
                  for n in ("ffn", "expert0")}
    row_marks = sb("row_marks", [128, len(MARKS), G])

    with nc.Block() as block:
        @block.sync
        def _(sp):
            sp.dma_start(core.x[:, :, :], dram["x"].rearrange("b s d -> s b d")).then_inc(sem("x_loaded"), 16)
            for n in ("Wq1", "Wk1", "Wv1"):
                sp.dma_start(core.wraw[n][:, :, :], dram[f"L0_xattn_{n}"].rearrange("h d e -> d h e")
                             ).then_inc(sem("self_weights_loaded"), 16)
            for n in ("Wq2", "Wk2", "Wv2"):
                sp.dma_start(core.wraw[n][:, :, :], dram[f"L0_xattn_{n}"].rearrange("h d e -> d h e")
                             ).then_inc(sem("cross_weights_loaded"), 16)
            for n, up, up_bias, down in (
                    ("ffn", dram["L0_xattn_Wf1"], dram["L0_xattn_bf1"], dram["L0_xattn_Wf2"]),
                    ("expert0", dram["L0_ffn_w1"][0], dram["L0_ffn_b1"][0], dram["L0_ffn_w2"][0])):
                for dst, src in zip(core.dense[n], (up, up_bias.rearrange("(f p) -> p f", p=D),
                                                    down.rearrange("(f p) d -> p f d", p=D))):
                    sp.dma_start(dst[tuple(slice(None) for _ in dst.shape)], src, allow_slow_non_contiguous=True
                                 ).then_inc(sem(f"{n}_loaded"), 16)

        @block.scalar
        def _(act):
            for n, w in names.items():
                src = dram[f"L0_xattn_{n}"]
                src = src.rearrange("h e -> (h e)") if len(src.shape) == 2 else src
                act.dma_start(core.row[n][:, :], src.rearrange("(o w) -> o w", o=1).broadcast_to([S, w])
                              ).then_inc(sem("rows_loaded"), 16)
            for k, n in enumerate(("g_xattn", "g_ffn")):
                act.dma_start(core.gates[:, 2 * k:2 * k + 2],
                              dram[n].rearrange("(o w) -> o w", o=1).broadcast_to([128, 2])
                              ).then_inc(sem("gates_loaded"), 16)
            for n, src in (("b2", dram["L0_ffn_b2"][0:1, :]),
                           ("gamma", dram["L0_ffn_gamma"].rearrange("(o w) -> o w", o=1)),
                           ("beta", dram["L0_ffn_beta"].rearrange("(o w) -> o w", o=1))):
                act.dma_start(core.row_e[n][:, :], src.broadcast_to([S, D])).then_inc(sem("expert_rows_loaded"), 16)
            act.wait_ge(sem("gates_loaded"), 32)
            nc.scalar.activation(core.gates[:, :], core.gates[:, :], ACT.Tanh).then_inc(sem("gates_ready"), 1)

        @block.gpsimd
        def _(pool):
            link = chain(core, pool, "setup_pool_steps")
            link(nc.gpsimd.memset(core.ident[:, :], 0.0))
            link(nc.gpsimd.affine_select(out=core.ident[:, :], in_=core.ident[:, :], compare_op=ALU.not_equal,
                                         fill=1.0, base=0, pattern=[[-1, 128]], channel_multiplier=1))
            nc.gpsimd.tensor_copy(core.ident4[:, :, :],
                                  core.ident[0:S, 0:S].unsqueeze(1).broadcast_to([S, J, S])
                                  ).then_inc(sem("identity_ready"), 1)
            link(nc.gpsimd.memset(core.causal4[:, :, :], 0.0))
            nc.gpsimd.affine_select(out=core.causal4[:, :, :], in_=core.causal4[:, :, :], compare_op=ALU.is_ge,
                                    fill=MASKED, base=0, pattern=[[0, J], [-1, S]], channel_multiplier=1
                                    ).then_inc(sem("causal_ready"), 1)
            for k, (lo, hi, value) in enumerate(MARKS):
                marks = row_marks[:, k, :]
                link(nc.gpsimd.memset(marks, value))
                link(nc.gpsimd.affine_select(out=marks, in_=marks, compare_op=ALU.is_ge, fill=0.0, base=-lo,
                                             pattern=[[-32, G]], channel_multiplier=1))
                ins = nc.gpsimd.affine_select(out=marks, in_=marks, compare_op=ALU.is_ge, fill=0.0,
                                              base=hi - 1, pattern=[[32, G]], channel_multiplier=-1)
                if k + 1 < len(MARKS):
                    link(ins)
            ins.then_inc(sem("marks_ready"), 1)

        @block.vector
        def _(dve):
            link = chain(core, dve, "setup_vector_steps")
            dve.wait_ge(sem("marks_ready"), 1)
            nc.vector.tensor_reduce(core.signs_k[:, :], row_marks[:, 0:2, :].rearrange("p a g -> p (a g)"),
                                    AX_X, ALU.add)
            nc.vector.tensor_reduce(core.signs_q[:, :], row_marks[:, 2, :], AX_X, ALU.add)
            nc.vector.tensor_reduce(core.ones_k[:, :], row_marks[:, 3, :], AX_X, ALU.add
                                    ).then_inc(sem("signs_ready"), 1)
            for n in core.wstack:
                link(nc.vector.memset(core.wstack[n][:, :, :], 0.0))
            for n, (loaded, k) in {"Wq1": ("self_weights_loaded", 48), "Wk1": ("self_weights_loaded", 48),
                                   "Wq2": ("cross_weights_loaded", 48),
                                   "Wk2": ("cross_weights_loaded", 48)}.items():
                dve.wait_ge(sem(loaded), k)
                order = "d (g j) e -> d g j e" if n in ("Wq1", "Wk1") else "d (j g) e -> d g j e"
                for r in range(3):
                    ins = nc.vector.tensor_copy(
                        core.wstack[n][:, :, :].rearrange("d j (g r) -> d g j r", g=G)[:, :, :, E0 * r:E0 * r + E0],
                        core.wraw[n][:, :, :].rearrange(order, j=J))
                ins.then_inc(sem("stack_weights_ready"), 1)
            dve.wait_ge(sem("x_loaded"), 16)
            layer_norm(core, link, core.xn, core.x)
            dve.sem_inc(sem("x_normalised"), 1)


def self_attention_phase(core):
    nc, sem, ps = core.nc, core.sem, core.ps
    with ExitStack() as own:
        def sb(name, shape, dt=F32):
            return core.sb(name, shape, dt, own)

        high = sb("self_high", [128, 2, 2, HALF], F16)
        qst = sb("self_queries", [128, J, NTOK], F16)
        kst = sb("self_keys", [128, J, NTOK], F16)
        values = sb("self_values", [S, NB, H, 32])
        probs = sb("self_probs", [S, RING, 2, J * S])
        mx = sb("self_max", [S, G, J, NB])
        nm3 = sb("self_shift", [G * J * NB, SHIFT, S], F16)
        rest = sb("self_shift_rest", [G * J * NB, S])

        with nc.Block() as block:
            @block.sync
            def _(sp):
                sp.wait_ge(sem("self_shift_ready"), 1)
                for g in range(G):
                    for r in range(SHIFT):
                        row = 32 * g + STACK + r
                        sp.dma_start(qst[row:row + 1, :, :].rearrange("o j n -> o (j n)"),
                                     nm3[J * NB * g:J * NB * (g + 1), r, :]).then_inc(sem("self_shift_loaded"), 16)
                sp.wait_ge(sem("self_shift_loaded"), 16 * G * SHIFT)

            @block.gpsimd
            def _(pool):
                link = chain(core, pool, "self_pool_steps")
                link(nc.gpsimd.memset(values[:, :, :, :], 0.0))
                nc.gpsimd.memset(values[:, :, :, E0:E0 + 1], 1.0).then_inc(sem("self_ones_ready"), 1)

            @block.tensor
            def _(pe):
                pe.wait_ge(sem("identity_ready"), 1)
                pe.wait_ge(sem("x_normalised"), 1)
                transpose_x(core, pe, core.xn, 6).then_inc(sem("input_xT_psum"), 1)
                pe.wait_ge(sem("input_xT_ready"), 1)
                pe.wait_ge(sem("stack_weights_ready"), 2)
                for k, n in enumerate(("Wq1", "Wk1")):
                    for j in range(J):
                        i = J * k + j
                        if i >= 2:
                            pe.wait_ge(sem("self_stack_ready"), i - 1)
                        for c in range(2):
                            ins = nc.tensor.matmul(ps[:, 2 * (i % 2) + c, 0:HALF], core.wstack[n][:, j, :],
                                                   core.xT[:, c * HALF:(c + 1) * HALF], start=True, stop=True)
                        ins.then_inc(sem("self_stack_psum"), 1)
                for b in range(NB):
                    ins = nc.tensor.matmul(ps[0:S, 4 + b // 4, 128 * (b % 4):128 * (b % 4 + 1)],
                                           core.xT[:, b * S:(b + 1) * S],
                                           core.wraw["Wv1"][:, :, :].rearrange("d h e -> d (h e)"),
                                           start=True, stop=True)
                ins.then_inc(sem("self_values_psum"), 1)
                pe.wait_ge(sem("self_stack_ready"), 2 * J)
                pe.wait_ge(sem("causal_ready"), 1)
                for b in range(NB):
                    for g in range(G):
                        if b:
                            pe.wait_ge(sem("self_max_ready"), G * (b - 1) + g + 1)
                        bank = ps[0:S, g, 0:HALF]
                        nc.tensor.matmul(bank, core.ident4[:, 0, :],
                                         core.causal4[:, :, :].rearrange("s j t -> s (j t)"),
                                         start=True, stop=False, skip_group_check=True)
                        for j in range(J):
                            ins = nc.tensor.matmul(
                                ps[0:S, g, j * S:(j + 1) * S], qst[32 * g:32 * g + STACK, j, b * S:(b + 1) * S],
                                kst[32 * g:32 * g + STACK, j, b * S:(b + 1) * S],
                                start=False, stop=True, skip_group_check=True)
                        ins.then_inc(sem("self_first_scores"), 1)
                pe.wait_ge(sem("self_negmax_ready"), 1)
                nc.tensor.transpose(ps[:, 6, 0:S], core.negmax[:, :], core.ident[0:S, 0:S]
                                    ).then_inc(sem("self_negmax_psum"), 1)
                pe.wait_ge(sem("self_shift_loaded"), 16 * G * SHIFT)
                pe.wait_ge(sem("self_values_ready"), 2)

                def values_product(n):
                    b, half = n // 2, n % 2
                    pe.wait_ge(sem("self_probs_ready"), n + 1)
                    if half == 0 and b >= 2:
                        pe.wait_ge(sem("self_oT_ready"), b - 1)
                    for gg in range(2):
                        g = 2 * half + gg
                        for j in range(J):
                            ins = nc.tensor.matmul(
                                ps[32 * j:32 * j + 32, ACC + b % 2, g * S:(g + 1) * S], values[:, b, J * g + j, :],
                                probs[:, n % RING, gg, j * S:(j + 1) * S], start=(g == 0), stop=True,
                                skip_group_check=True)
                    ins.then_inc(sem("self_product_done"), 1)

                for n in range(2 * NB):
                    b, half = n // 2, n % 2
                    if n >= 2:
                        pe.wait_ge(sem("self_probs_ready"), n - 1)
                    for gg in range(2):
                        g = 2 * half + gg
                        nc.tensor.matmul(ps[0:S, g, 0:HALF], core.causal4[:, 0, :],
                                         core.ident4[:, :, :].rearrange("s j t -> s (j t)"),
                                         start=True, stop=False, skip_group_check=True)
                        for j in range(J):
                            ins = nc.tensor.matmul(
                                ps[0:S, g, j * S:(j + 1) * S],
                                kst[32 * g:32 * g + STACK + SHIFT, j, b * S:(b + 1) * S],
                                qst[32 * g:32 * g + STACK + SHIFT, j, b * S:(b + 1) * S],
                                start=False, stop=True, skip_group_check=True)
                    ins.then_inc(sem("self_scores_psum"), 1)
                    if n >= 1:
                        values_product(n - 1)
                values_product(2 * NB - 1)

            @block.scalar
            def _(act):
                act.wait_ge(sem("input_xT_psum"), 1)
                nc.scalar.activation(core.xT[:, :].rearrange("d (c n) -> d c n", c=2), ps[:, 6:8, 0:HALF], ACT.Copy
                                     ).then_inc(sem("input_xT_ready"), 1)
                act.wait_ge(sem("signs_ready"), 1)
                for i in range(2 * J):
                    act.wait_ge(sem("self_stack_psum"), i + 1)
                    if i >= 2:
                        act.wait_ge(sem("self_stack_ready"), i - 1)
                    b = 2 * (i % 2)
                    nc.scalar.activation(high[:, i % 2, :, :], ps[:, b:b + 2, 0:HALF], ACT.Identity,
                                         bias=core.ones_k[:, 0:1] if i >= J else 0.0
                                         ).then_inc(sem("self_high_ready"), 1)
                act.wait_ge(sem("self_values_psum"), 1)
                act.wait_ge(sem("self_ones_ready"), 1)
                for c in range(2):
                    nc.scalar.activation(values[:, 4 * c:4 * c + 4, :, 0:E0],
                                         ps[0:S, 4 + c, :].rearrange("s (b h e) -> s b h e", b=4, h=H), ACT.Copy
                                         ).then_inc(sem("self_values_ready"), 1)
                for n in range(2 * NB):
                    half = n % 2
                    act.wait_ge(sem("self_scores_psum"), n + 1)
                    if n >= RING:
                        act.wait_ge(sem("self_product_done"), n - RING + 1)
                    nc.scalar.activation(probs[:, n % RING, :, :], ps[0:S, 2 * half:2 * half + 2, 0:HALF], ACT.Exp,
                                         scale=SCALE0).then_inc(sem("self_probs_ready"), 1)

            @block.vector
            def _(dve):
                link = chain(core, dve, "self_vector_steps")
                for i in range(2 * J):
                    dve.wait_ge(sem("self_high_ready"), i + 1)
                    b = 2 * (i % 2)
                    dst = (qst if i < J else kst)[:, i % J, :].rearrange("p (c n) -> p c n", c=2)
                    split_stack(core, dve, dst, ps[:, b:b + 2, 0:HALF], high[:, i % 2, :, :],
                                core.signs_q[:, 0:1] if i < J else core.signs_k[:, 0:1]
                                ).then_inc(sem("self_stack_ready"), 1)
                for b in range(NB):
                    for g in range(G):
                        dve.wait_ge(sem("self_first_scores"), G * b + g + 1)
                        nc.vector.tensor_reduce(mx[:, g, :, b], ps[0:S, g, 0:HALF].rearrange("s (j t) -> s j t", j=J),
                                                AX_X, ALU.max).then_inc(sem("self_max_ready"), 1)
                dve.wait_ge(sem("self_max_ready"), G * NB)
                nc.vector.tensor_scalar(core.negmax[:, :], mx[:, :, :, :].rearrange("s g j b -> s (g j b)"), -1.0,
                                        None, ALU.mult).then_inc(sem("self_negmax_ready"), 1)
                dve.wait_ge(sem("self_negmax_psum"), 1)
                shift_parts(core, link, nm3, ps[:, 6, 0:S], rest[:, :]).then_inc(sem("self_shift_ready"), 1)
                for b in range(NB):
                    dve.wait_ge(sem("self_product_done"), 2 * b + 2)
                    nc.vector.tensor_copy(core.oT[:, b, :], ps[:, ACC + b % 2, 0:G * S]
                                          ).then_inc(sem("self_oT_ready"), 1)


def finish_attention_phase(core, name):
    nc, sem, ps = core.nc, core.sem, core.ps
    gain, shift, bias = {"self": ("g1", "be1", "bv1"), "cross": ("g2", "be2", "bv2")}[name]
    with nc.Block() as block:
        @block.tensor
        def _(pe):
            for b in range(NB):
                if b >= 4:
                    pe.wait_ge(sem(name + "_normalised"), b - 3)
                for g in range(G):
                    ins = nc.tensor.transpose(ps[0:S, b % 4, 128 * g:128 * (g + 1)], core.oT[:, b, g * S:(g + 1) * S],
                                              core.ident[:, :])
                ins.then_inc(sem(name + "_o_psum"), 1)
            pe.wait_ge(sem(name + "_added"), 1)
            transpose_x(core, pe, core.xn, 6).then_inc(sem(name + "_xT_psum"), 1)

        @block.vector
        def _(dve):
            link = chain(core, dve, name + "_finish_steps")
            for b in range(NB):
                dve.wait_ge(sem(name + "_o_psum"), b + 1)
                o = ps[0:S, b % 4, :].rearrange("s (g j e) -> s g j e", g=G, j=J)
                link(nc.vector.reciprocal(core.row_sums[:, b, :, :], o[:, :, :, E0]))
                nc.vector.tensor_tensor(core.work[:, b, :].rearrange("s (g j e) -> s g j e", g=G, j=J),
                                        o[:, :, :, 0:E0],
                                        core.row_sums[:, b, :, :].unsqueeze(3).broadcast_to([S, G, J, E0]), ALU.mult
                                        ).then_inc(sem(name + "_normalised"), 1)
            dve.wait_ge(sem(name + "_normalised"), NB)
            dve.wait_ge(sem("rows_loaded"), 16 * len(core.row))
            link(nc.vector.tensor_tensor(core.work[:, :, :], core.work[:, :, :], rows(core.row[bias]), ALU.add))
            link(nc.vector.tensor_tensor(core.work[:, :, :], core.work[:, :, :], core.xn[:, :, :], ALU.add))
            layer_norm(core, link, core.xn, core.work, core.row[gain], core.row[shift])
            dve.sem_inc(sem(name + "_added"), 1)

        @block.scalar
        def _(act):
            act.wait_ge(sem(name + "_xT_psum"), 1)
            nc.scalar.activation(core.xT[:, :].rearrange("d (c n) -> d c n", c=2), ps[:, 6:8, 0:HALF], ACT.Copy
                                 ).then_inc(sem(name + "_xT_ready"), 1)


def run_sequences(eng, emit):
    emit(0, 0, True, False)
    with eng.Fori(0, NB // 2 - 1) as i:
        for k in range(2):
            emit(2 * i + k + 1, (k + 1) % 2, False, False)
    emit(NB - 1, 1, False, True)


def share(items, k, of):
    return items[len(items) * k // of:len(items) * (k + 1) // of]


def wait_apart(eng, turns):
    eng.sem_inc(turns, 1)


def load_context_tiles(core, eng, b, u, loaded):
    src = core.dram["ctx_1024"][bass.ds(b, 1), :, :].rearrange("o r d -> (o r) d")
    cut = OFF[TALL]
    eng.dma_start(core.ctx[0:ROWS[0], u, 0:TALL, :], src[0:cut, :].rearrange("(t p) d -> p t d", p=ROWS[0])
                  ).then_inc(loaded, 16)
    eng.dma_start(core.ctx[0:ROWS[-1], u, TALL:TT, :], src[cut:T, :].rearrange("(t p) d -> p t d", p=ROWS[-1])
                  ).then_inc(loaded, 16)


def float16_parts(core, dve, phase, n, mx, negmax, parts, rest, whole):
    nc, steps = core.nc, core.sem(phase + "_shift_steps")
    nc.vector.tensor_reduce(negmax, mx, AX_X, ALU.max, negate=True).then_inc(steps, 1)
    dve.wait_ge(steps, 5 * n + 1)
    nc.vector.tensor_copy(parts[0], whole).then_inc(steps, 1)
    dve.wait_ge(steps, 5 * n + 2)
    nc.vector.tensor_tensor(rest, whole, parts[0], ALU.subtract).then_inc(steps, 1)
    dve.wait_ge(steps, 5 * n + 3)
    nc.vector.tensor_copy(parts[1], rest).then_inc(steps, 1)
    dve.wait_ge(steps, 5 * n + 4)
    nc.vector.tensor_tensor(rest, rest, parts[1], ALU.subtract).then_inc(steps, 1)
    dve.wait_ge(steps, 5 * n + 5)
    return nc.vector.tensor_copy(parts[2], rest)


def cross_attention_0_phase(core):
    nc, sem, ps = core.nc, core.sem, core.ps
    jobs, nj = JOBS0, len(JOBS0)
    with ExitStack() as own:
        def sb(name, shape, dt=F32):
            return core.sb(name, shape, dt, own)

        ctx = core.ctx
        ctxT = sb("x0_contextT", [D, T])
        high = sb("x0_high", [128, SIDES0, 512], F16)
        qst = sb("x0_queries", [128, 2, J, G * S], F16)
        kst = sb("x0_keys", [128, 2, J, T], F16)
        values = sb("x0_values", [128, 2, TT, H, 32])
        probs = sb("x0_probs", [128, RING, 2, G * S])
        mx = sb("x0_max", [S, H, NC])
        negmax = sb("x0_negmax", [S, H])
        parts = sb("x0_shift_parts", [S, G, SHIFT, J], F16)
        rest = sb("x0_shift_rest", [S, G, J])
        shift = sb("x0_shift", [G * SHIFT * J, S], F16)

        def side(k):
            return ps[:, SIDE0 + k % SIDES0, :]

        stacks = count(jobs, "qk")

        with nc.Block() as block:
            @block.sync
            def _(sp):
                def load_context(b, u):
                    load_context_tiles(core, sp, b, u, sem(f"x0_context_loaded{u}"))

                def shift_rows(n, u):
                    sp.wait_ge(sem("x0_shift_ready"), n + 1)
                    for g in range(G):
                        row = 32 * g + STACK
                        sp.dma_start(qst[row:row + SHIFT, u, :, g * S:(g + 1) * S],
                                     shift[SHIFT * J * g:SHIFT * J * (g + 1), :]
                                     ).then_inc(sem("x0_shift_loaded"), 16)

                load_context(0, 0)
                load_context(1, 1)
                shift_rows(0, 0)
                load_context(2, 0)
                shift_rows(1, 1)
                with sp.Fori(0, NB // 2 - 2) as i:
                    for k in range(2):
                        load_context(2 * i + k + 3, (k + 1) % 2)
                        shift_rows(2 * i + k + 2, k % 2)
                load_context(NB - 1, 1)
                for n in (NB - 2, NB - 1):
                    shift_rows(n, n % 2)

            @block.gpsimd
            def _(pool):
                pool.memset(qst[:, :, :, :], 0.0).then_inc(sem("x0_zero_queries"), 1)
                pool.memset(values[:, 0, :, :, :], 0.0).then_inc(sem("x0_zeros_ready"), 1)
                pool.memset(values[:, 1, :, :, :], 0.0).then_inc(sem("x0_zeros_ready"), 1)
                pool.wait_ge(sem("x0_zeros_ready"), 2)
                for u in range(2):
                    pool.memset(values[:, u, :, :, E0:E0 + 1], 1.0).then_inc(sem("x0_ones_ready"), 1)

            @block.tensor
            def _(pe):
                pe.wait_ge(sem("self_xT_ready"), 1)
                pe.wait_ge(sem("stack_weights_ready"), 4)

                def job(k, n, u):
                    kind, a, c = jobs[k]
                    pe.wait_ge(sem(f"x0_side_free{k % SIDES0}"), nj // SIDES0 * n + k // SIDES0 + 1)
                    bank = side(k)
                    if kind == "q":
                        for p in range(2):
                            ins = nc.tensor.matmul(bank[:, p * S:(p + 1) * S], core.wstack["Wq2"][:, 2 * a + p, :],
                                                   core.xT[:, bass.ds(n * S, S)], start=True, stop=True)
                    elif kind == "tr":
                        if a == 0:
                            pe.wait_ge(sem(f"x0_context_loaded{u}"), 16 * (n - u) + 32)
                        for t in range(GT * a, GT * a + GT):
                            o = OFF[t] - CHUNKS[a][0]
                            ins = nc.tensor.transpose(bank[:, o:o + ROWS[t]],
                                                      ctx[0:ROWS[t], u, t, :], core.ident[0:ROWS[t], 0:ROWS[t]])
                    elif kind == "k":
                        if a == 0 and c == 0:
                            pe.wait_ge(sem("x0_contextT_ready"), NG * (n + 1))
                        o, w = CHUNKS[a]
                        ins = nc.tensor.matmul(bank[:, 0:w], core.wstack["Wk2"][:, c, :], ctxT[:, o:o + w],
                                               start=True, stop=True)
                    elif kind == "v":
                        for t in range(GT * a, GT * a + GT):
                            ins = nc.tensor.matmul(bank[0:ROWS[t], D * (t % GT):D * (t % GT + 1)],
                                                   ctxT[:, OFF[t]:OFF[t] + ROWS[t]],
                                                   core.wraw["Wv2"][:, :, :].rearrange("d h e -> d (h e)"),
                                                   start=True, stop=True)
                    elif kind == "n":
                        if a == 0 and c == 0:
                            pe.wait_ge(sem("x0_stack_ready"), stacks * (n + 1))
                        g, j, (o, w) = a // J, a % J, CHUNKS[c]
                        ins = nc.tensor.matmul(bank[0:S, 0:w], qst[32 * g:32 * g + STACK, u, j, g * S:(g + 1) * S],
                                               kst[32 * g:32 * g + STACK, u, j, o:o + w], start=True, stop=True)
                    elif kind == "m":
                        pe.wait_ge(sem("x0_parts_ready"), n + 1)
                        ins = nc.tensor.matmul(bank[0:G * SHIFT * J, 0:S],
                                               parts[:, :, :, :].rearrange("s g r j -> s (g r j)"),
                                               core.ident4[:, 0, :], start=True, stop=True)
                    ins.then_inc(sem("x0_side_ready"), 1)

                for k in range(nj):
                    job(k, 0, 0)

                def values_product(b, u, v, j):
                    t = v // 2
                    if v == 0 and j == 0:
                        pe.wait_ge(sem("x0_values_ready"), NG * (b + 1))
                        pe.wait_ge(sem("x0_oT_ready"), b + 1)
                    if j % 2 == 0:
                        pe.wait_ge(sem("x0_probs_ready"), STEPS * b + v + 1 + 2)
                    for g in range(G):
                        ins = nc.tensor.matmul(
                            ps[32 * g:32 * g + 32, ACC, j * S:(j + 1) * S], values[0:ROWS[t], u, t, G * j + g, :],
                            probs[0:ROWS[t], v % RING, j % 2, g * S:(g + 1) * S],
                            start=(t == 0 and j == 0), stop=(t == TT - 1), skip_group_check=True)
                    if j % 2:
                        ins.then_inc(sem("x0_product_done"), 1)

                def sequence(b, u, first, last):
                    for s in range(STEPS + (LAG if last else 0)):
                        if s < STEPS:
                            t, half = s // 2, s % 2
                            if s == 0:
                                pe.wait_ge(sem("x0_shift_loaded"), 16 * G * (b + 1))
                            pe.wait_ge(sem("x0_probs_ready"), STEPS * b + s + 1)
                            for j in (2 * half, 2 * half + 1):
                                ins = nc.tensor.matmul(ps[0:ROWS[t], j, 0:G * S],
                                                       kst[:, u, j, OFF[t]:OFF[t] + ROWS[t]], qst[:, u, j, :],
                                                       start=True, stop=True)
                            ins.then_inc(sem("x0_scores_ready"), 1)
                        mine = [] if last else AT_STEP0[s]
                        v = s - LAG
                        for part in range(3):
                            for k in share(mine, part, 3):
                                job(k, b + 1, 1 - u)
                            if part < 2 and v >= 0:
                                values_product(b, u, v, 2 * (v % 2) + part)
                            elif part < 2 and not first:
                                values_product(b - 1, 1 - u, v + STEPS, 2 * (v % 2) + part)

                run_sequences(pe, sequence)

            @block.scalar
            def _(act):
                act.sem_inc(sem("x0_probs_ready"), 2)
                act.sem_inc(sem("x0_oT_ready"), 1)

                def job(k, n, u):
                    kind, a, c = jobs[k]
                    if kind in ("n", "m"):
                        return
                    act.wait_ge(sem("x0_side_ready"), nj * n + k + 1)
                    bank = side(k)
                    if kind == "q":
                        nc.scalar.activation(high[:, k % SIDES0, 0:2 * S], bank[:, 0:2 * S], ACT.Identity
                                             ).then_inc(sem("x0_high_ready"), 1)
                    elif kind == "k":
                        w = CHUNKS[a][1]
                        nc.scalar.activation(high[:, k % SIDES0, 0:w], bank[:, 0:w], ACT.Identity,
                                             bias=core.ones_k[:, 0:1]).then_inc(sem("x0_high_ready"), 1)
                    elif kind == "tr":
                        o, w = CHUNKS[a]
                        nc.scalar.activation(ctxT[:, o:o + w], bank[:, 0:w], ACT.Copy
                                             ).then_inc(sem("x0_contextT_ready"), 1)
                        act.wait_ge(sem("x0_contextT_ready"), NG * n + a + 1)
                        act.sem_inc(sem(f"x0_side_free{k % SIDES0}"), 1)
                    elif kind == "v":
                        if a == 0:
                            act.wait_ge(sem("x0_ones_ready"), 2)
                        r = ROWS[GT * a]
                        nc.scalar.activation(values[0:r, u, GT * a:GT * a + GT, :, 0:E0],
                                             bank[0:r, 0:GT * D].rearrange("p (t h e) -> p t h e", t=GT, h=H), ACT.Copy
                                             ).then_inc(sem("x0_values_ready"), 1)
                        act.wait_ge(sem("x0_values_ready"), NG * n + a + 1)
                        act.sem_inc(sem(f"x0_side_free{k % SIDES0}"), 1)

                def store_oT(b):
                    act.wait_ge(sem("x0_product_done"), STEPS * (b + 1) + RING)
                    nc.scalar.activation(core.oT[:, bass.ds(b, 1), :], ps[:, ACC, 0:J * S].unsqueeze(1), ACT.Copy
                                         ).then_inc(sem("x0_oT_ready"), 1)

                for k in range(nj):
                    job(k, 0, 0)

                def sequence(b, u, first, last):
                    for s in range(STEPS):
                        if s == LAG and not first:
                            store_oT(b - 1)
                        if s < STEPS:
                            t, half = s // 2, s % 2
                            act.wait_ge(sem("x0_scores_ready"), STEPS * b + s + 1)
                            act.wait_ge(sem("x0_product_done"), STEPS * b + s + 1)
                            nc.scalar.activation(probs[0:ROWS[t], s % RING, :, :],
                                                 ps[0:ROWS[t], 2 * half:2 * half + 2, 0:G * S], ACT.Exp,
                                                 scale=SCALE0).then_inc(sem("x0_probs_ready"), 1)
                        if not last:
                            for k in AT_STEP0[s]:
                                job(k, b + 1, 1 - u)
                    if last:
                        store_oT(b)

                run_sequences(act, sequence)

            @block.vector
            def _(dve):
                dve.sem_inc(sem("x0_product_done"), RING)
                for k in range(SIDES0):
                    dve.sem_inc(sem(f"x0_side_free{k}"), 1)
                last_n = max(k for k in range(nj) if jobs[k][0] == "n")

                def job(k, n, u):
                    kind, a, c = jobs[k]
                    if kind in ("tr", "v"):
                        return
                    free = sem(f"x0_side_free{k % SIDES0}")
                    dve.wait_ge(sem("x0_side_ready"), nj * n + k + 1)
                    bank = side(k)
                    if kind in ("q", "k"):
                        dve.wait_ge(sem("x0_high_ready"), stacks * n + count(jobs, "qk", k) + 1)
                        if kind == "q":
                            if k == 0:
                                dve.wait_ge(sem("x0_zero_queries"), 1)
                            for g in range(G):
                                rows_g = slice(32 * g, 32 * g + 32)
                                ins = split_stack(
                                    core, dve, qst[rows_g, u, 2 * a:2 * a + 2, g * S:(g + 1) * S],
                                    halves(bank[rows_g, 0:2 * S], S), halves(high[rows_g, k % SIDES0, 0:2 * S], S),
                                    core.signs_q[rows_g, 0:1])
                        else:
                            o, w = CHUNKS[a]
                            ins = split_stack(core, dve, kst[:, u, c, o:o + w], bank[:, 0:w],
                                              high[:, k % SIDES0, 0:w], core.signs_k[:, 0:1])
                        ins.then_inc(sem("x0_stack_ready"), 1)
                        dve.wait_ge(sem("x0_stack_ready"), stacks * n + count(jobs, "qk", k) + 1)
                        dve.sem_inc(free, 1)
                    elif kind == "n":
                        w = CHUNKS[c][1]
                        nc.vector.tensor_reduce(mx[:, a, c:c + 1], bank[0:S, 0:w], AX_X, ALU.max).then_inc(free, 1)
                        if k == last_n:
                            dve.wait_ge(free, nj // SIDES0 * n + k // SIDES0 + 2)
                            float16_parts(core, dve, "x0", n, mx[:, :, :], negmax[:, :],
                                          [parts[:, :, r, :] for r in range(SHIFT)], rest[:, :, :],
                                          negmax[:, :].rearrange("s (g j) -> s g j", g=G)
                                          ).then_inc(sem("x0_parts_ready"), 1)
                    elif kind == "m":
                        if not isinstance(n, int) or n:
                            dve.wait_ge(sem("x0_shift_loaded"), 16 * G * n)
                        nc.vector.tensor_copy(shift[:, :], bank[0:G * SHIFT * J, 0:S]
                                              ).then_inc(sem("x0_shift_ready"), 1)
                        dve.wait_ge(sem("x0_shift_ready"), n + 1)
                        dve.sem_inc(free, 1)

                for k in range(nj):
                    job(k, 0, 0)

                def sequence(b, u, first, last):
                    if not last:
                        for k in range(nj):
                            job(k, b + 1, 1 - u)

                run_sequences(dve, sequence)


def hidden_layer(core, pe, up, hidden_free, hidden_psum, base):
    nc, ps = core.nc, core.ps
    for f in range(FT):
        pe.wait_ge(hidden_free, base + f + 1)
        for c in range(2):
            ins = nc.tensor.matmul(ps[:, 2 * (f % 2) + c, 0:HALF], up[:, D * f:D * f + D],
                                   core.xT[:, c * HALF:(c + 1) * HALF], start=True, stop=True)
        ins.then_inc(hidden_psum, 1)


def output_layer(core, pe, down, hidden, bank):
    nc, ps = core.nc, core.ps
    for b in range(NB):
        for f in range(FT):
            ins = nc.tensor.matmul(ps[0:S, bank + b // 4, D * (b % 4):D * (b % 4 + 1)],
                                   hidden[:, f, b * S:(b + 1) * S], down[:, f, :], start=(f == 0), stop=(f == FT - 1))
    return ins


def halves(ap, w):
    return ap.rearrange("p (c n) -> p c n", n=w)


def token_banks(core, bank):
    return core.ps[0:S, bank:bank + 2, :].rearrange("s c (b d) -> s (c b) d", d=D)


def add_gated(core, link, gate, what):
    link(core.nc.vector.scalar_tensor_tensor(
        out=flat(core.x), in0=flat(what), scalar=core.gates[0:S, gate:gate + 1], in1=flat(core.x),
        op0=ALU.mult, op1=ALU.add))


def flat(t):
    return t[:, :, :].rearrange("s b d -> s (b d)")


def feed_forward_phase(core, name, bias, gain, shift, gate):
    nc, sem, ps = core.nc, core.sem, core.ps
    up, up_bias, down = core.dense[name]
    with ExitStack() as own, nc.Block() as block:
        hidden = core.sb(f"{name}_hidden", [D, FT, NTOK], F32, own)

        @block.tensor
        def _(pe):
            pe.wait_ge(sem(f"{name}_loaded"), 48)
            hidden_layer(core, pe, up, sem(f"{name}_hidden_free"), sem(f"{name}_hidden_psum"), 0)
            pe.wait_ge(sem(f"{name}_hidden_free"), 2 + FT)
            output_layer(core, pe, down, hidden, 4).then_inc(sem(f"{name}_out_psum"), 1)
            pe.wait_ge(sem(f"{name}_added"), 1)
            transpose_x(core, pe, core.xn, 6).then_inc(sem(f"{name}_xT_psum"), 1)

        @block.scalar
        def _(act):
            act.sem_inc(sem(f"{name}_hidden_free"), 2)
            for f in range(FT):
                act.wait_ge(sem(f"{name}_hidden_psum"), f + 1)
                nc.scalar.activation(halves(hidden[:, f, :], HALF), ps[:, 2 * (f % 2):2 * (f % 2) + 2, 0:HALF], ACT.Relu,
                                     bias=up_bias[:, f:f + 1]).then_inc(sem(f"{name}_hidden_free"), 1)
            act.wait_ge(sem(f"{name}_xT_psum"), 1)
            nc.scalar.activation(halves(core.xT[:, :], HALF), ps[:, 6:8, 0:HALF], ACT.Copy
                                 ).then_inc(sem(f"{name}_xT_ready"), 1)

        @block.vector
        def _(dve):
            link = chain(core, dve, f"{name}_vector_steps")
            dve.wait_ge(sem(f"{name}_out_psum"), 1)
            dve.wait_ge(sem("expert_rows_loaded"), 48)
            link(nc.vector.tensor_tensor(core.work[:, :, :], token_banks(core, 4), rows(bias), ALU.add))
            link(nc.vector.tensor_tensor(core.work[:, :, :], core.work[:, :, :], core.xn[:, :, :], ALU.add))
            layer_norm(core, link, core.xn, core.work, gain, shift)
            dve.wait_ge(sem("gates_ready"), 1)
            add_gated(core, link, gate, core.xn)
            layer_norm(core, link, core.xn, core.x)
            dve.sem_inc(sem(f"{name}_added"), 1)


def merge_weights_phase(core):
    nc, sem, ps, dram = core.nc, core.sem, core.ps, core.dram
    with ExitStack() as own, nc.Block() as block:
        raw = {n: core.sb(f"raw1_{n}", [D, H, E1], F32, own) for n in ("Wq", "Wk", "Wv")}
        turned = {n: core.sb(f"turned_{n}", [2 * E1, H // 2, D], F32, own) for n in ("Wq", "Wk", "Wv")}
        wo = core.sb("Wo", [2 * E1, H // 2, D], F32, own)

        @block.sync
        def _(sp):
            for n in raw:
                sp.dma_start(raw[n][:, :, :], dram[f"L1_xattn_{n}"].rearrange("h d e -> d h e")
                             ).then_inc(sem(f"{n}_loaded"), 16)
            sp.dma_start(wo[:, :, :], dram["L1_xattn_Wo"].rearrange("(a p) o -> p a o", p=2 * E1)
                         ).then_inc(sem("Wo_loaded"), 16)

        @block.tensor
        def _(pe):
            for k, n in enumerate(raw):
                pe.wait_ge(sem(f"{n}_loaded"), 16)
                for a in range(H // 2):
                    ins = nc.tensor.transpose(ps[:, 2 * k + a // 4, D * (a % 4):D * (a % 4 + 1)],
                                              raw[n][:, 2 * a:2 * a + 2, :].rearrange("d h e -> d (h e)"),
                                              core.ident[:, :])
                ins.then_inc(sem("turned_psum"), 1)
            pe.wait_ge(sem("Wo_loaded"), 16)
            for k, (left, right) in enumerate(((turned["Wq"], turned["Wk"]), (turned["Wv"], wo))):
                pe.wait_ge(sem("turned_ready"), 2 if k == 0 else 3)
                for quarter in range(2):
                    q = 2 * k + quarter
                    pe.wait_ge(sem("turned_ready"), 3)
                    if q >= 2:
                        pe.wait_ge(sem("merged_ready"), q - 1)
                    for h in range(8 * quarter, 8 * quarter + 8):
                        p, a = E1 * (h % 2), h // 2
                        ins = nc.tensor.matmul(ps[:, 2 * (q % 2) + h % 2, D * (a % 4):D * (a % 4 + 1)],
                                               left[p:p + E1, a, :], right[p:p + E1, a, :], start=True, stop=True)
                    ins.then_inc(sem("merged_psum"), 1)

        @block.scalar
        def _(act):
            for k, n in enumerate(raw):
                act.wait_ge(sem("turned_psum"), k + 1)
                nc.scalar.activation(turned[n][:, :, :].rearrange("p (c a) d -> p c (a d)", c=2),
                                     ps[:, 2 * k:2 * k + 2, :], ACT.Copy).then_inc(sem("turned_ready"), 1)

        @block.vector
        def _(dve):
            for q in range(4):
                dst = (core.merged_qk if q < 2 else core.merged_vo)[:, 8 * (q % 2):8 * (q % 2) + 8, :]
                dve.wait_ge(sem("merged_psum"), q + 1)
                nc.vector.tensor_copy(dst.rearrange("d (a r) o -> d r a o", r=2),
                                      ps[:, 2 * (q % 2):2 * (q % 2) + 2, :].rearrange("d r (a o) -> d r a o", a=4)
                                      ).then_inc(sem("merged_ready"), 1)


def side_order_1(first, last):
    order = []
    for s in range(STEPS):
        if s == LAG and not first:
            order += [(s, -1, "sum", 1, 0), (s, -1, "sum", 1, 1)]
        if s == TT + LAG:
            order += [(s, 0, "sum", 0, 0), (s, 0, "sum", 0, 1)]
        if not last:
            order += [(s, 1, *JOBS1[k]) for k in AT_STEP1[s]]
    return order + [(STEPS + LAG, 0, "sum", 1, 0), (STEPS + LAG, 0, "sum", 1, 1)] * last


def cross_attention_1_phase(core):
    nc, sem, ps = core.nc, core.sem, core.ps
    jobs, nj = JOBS1, len(JOBS1)
    with ExitStack() as own:
        def sb(name, shape, dt=F32):
            return core.sb(name, shape, dt, own)

        ctx = core.ctx
        chigh = sb("x1_context_high", [D, 2, T], F16)
        clow = sb("x1_context_low", [D, 2, T], F16)
        qhigh = sb("x1_queries_high", [D, 2, H * S], F16)
        qlow = sb("x1_queries_low", [D, 2, H * S], F16)
        mask_raw = sb("x1_mask_raw", [S, 2, T], U8)
        masked = sb("x1_masked", [S + SHIFT, 2, T], F16)
        select = sb("x1_select", [S + SHIFT, 2, H, S], F16)
        probs = sb("x1_probs", [128, RING, UNIT * S])
        sums = sb("x1_sums", [128, 2, UNIT * S])
        inverse = sb("x1_inverse", [128, 2, HALF])
        ones = sb("x1_ones", [128, 128])
        junk = sb("x1_junk", [S, 2, 512], F16)
        mx = sb("x1_max", [S, H, NC])
        negmax = sb("x1_negmax", [S, H])
        parts = sb("x1_shift_parts", [S, SHIFT, H], F16)
        rest = sb("x1_shift_rest", [S, H])
        shift = sb("x1_shift", [SHIFT * H, S], F16)
        averages = core.averages
        splits = count(jobs, ("q", "tr"))

        def base(b, first, sides=1):
            return (nj if first else nj + nj + 2 + (nj + 4) * (b - 1)) if sides == 1 else (
                nj // 2 if first else nj + 1 + (nj + 4) // 2 * (b - 1))

        with nc.Block() as block:
            @block.sync
            def _(sp):
                def load(b, u):
                    load_context_tiles(core, sp, b, u, sem("x1_context_loaded"))
                    sp.dma_start(mask_raw[:, u, :],
                                 core.dram["mask_BxSxS2_bf1"][bass.ds(b, 1), :, :].rearrange("o s t -> (o s) t")
                                 ).then_inc(sem("x1_mask_loaded"), 16)

                def shift_rows(n, u):
                    sp.wait_ge(sem("x1_shift_ready"), n + 1)
                    sp.dma_start(select[S:S + SHIFT, u, :, :].rearrange("r h s -> r (h s)"), shift[:, :]
                                 ).then_inc(sem("x1_shift_loaded"), 16)

                load(0, 0)
                sp.wait_ge(sem("x1_select_ready"), 1)
                shift_rows(0, 0)

                def sequence(b, u, first, last):
                    if not last:
                        sp.wait_ge(sem("x1_product_done"), STEPS * b + RING)
                        load(b + 1, 1 - u)
                        shift_rows(b + 1, 1 - u)

                run_sequences(sp, sequence)

            @block.gpsimd
            def _(pool):
                pool.memset(ones[:, :], 1.0)
                pool.memset(masked[:, :, :], 1.0).then_inc(sem("x1_ones_ready"), 1)
                for u in range(2):
                    ins = pool.tensor_copy(select[0:S, u, :, :],
                                           core.ident4[:, 0:1, :].broadcast_to([S, H, S]))
                ins.then_inc(sem("x1_select_ready"), 1)
                pool.sem_inc(sem("x1_sums_used"), 2)
                pool.wait_ge(sem("x1_ones_ready"), 1)

                def additive_mask(n, u):
                    pool.wait_ge(sem("x1_mask_loaded"), 16 * (n + 1))
                    wait_apart(pool, sem("pool_waits"))
                    pool.tensor_scalar(masked[0:S, u, :], mask_raw[:, u, :], -MASKED, MASKED, ALU.mult, ALU.add
                                       ).then_inc(sem("x1_mask_ready"), 1)

                additive_mask(0, 0)

                def sequence(b, u, first, last):
                    for s in range(STEPS):
                        unit, t = s // TT, s % TT
                        if s == 1 and not last:
                            additive_mask(b + 1, 1 - u)
                        pool.wait_ge(sem("x1_probs_ready"), STEPS * b + s + 1 + 2)
                        dst, src = sums[0:ROWS[t], unit, :], probs[0:ROWS[t], s % RING, :]
                        if t == 0:
                            pool.wait_ge(sem("x1_sums_used"), 2 * b + unit + 1)
                            wait_apart(pool, sem("pool_waits"))
                            ins = pool.tensor_copy(dst, src)
                        else:
                            pool.wait_ge(sem("x1_sums_done"), STEPS * b + s + RING)
                            ins = pool.tensor_tensor(dst, dst, src, ALU.add)
                        ins.then_inc(sem("x1_sums_done"), 1)

                run_sequences(pool, sequence)

            @block.tensor
            def _(pe):
                def job(kind, a, c, p, n, u, before, half_before):
                    pe.wait_ge(sem(f"x1_side_free{p % 2}"), half_before + p // 2 + 1)
                    bank = ps[:, SIDE1 + p % 2, :]
                    if kind == "q":
                        for h in range(HC * a, HC * a + HC):
                            ins = nc.tensor.matmul(bank[:, (h % HC) * S:(h % HC + 1) * S], core.merged_qk[:, h, :],
                                                   core.xT[:, bass.ds(n * S, S)], start=True, stop=True)
                    elif kind == "tr":
                        if a == 0:
                            pe.wait_ge(sem("x1_context_loaded"), 32 * n + 32)
                        for t in range(GT * a, GT * a + GT):
                            o = OFF[t] - CHUNKS[a][0]
                            ins = nc.tensor.transpose(bank[:, o:o + ROWS[t]], ctx[0:ROWS[t], u, t, :],
                                                      core.ident[0:ROWS[t], 0:ROWS[t]])
                    elif kind == "n":
                        if a == 0 and c == 0:
                            pe.wait_ge(sem("x1_high_ready"), splits * (n + 1))
                        o, w = CHUNKS[c]
                        ins = nc.tensor.matmul(bank[0:S, 0:w], qhigh[:, u, a * S:(a + 1) * S], chigh[:, u, o:o + w],
                                               start=True, stop=True)
                    elif kind == "m":
                        pe.wait_ge(sem("x1_parts_ready"), n + 1)
                        ins = nc.tensor.matmul(bank[0:SHIFT * H, 0:S], parts[:, :, :].rearrange("s r h -> s (r h)"),
                                               core.ident4[:, 0, :], start=True, stop=True)
                    else:
                        if c == 0:
                            pe.wait_ge(sem("x1_sums_done"), STEPS * n + TT * (a + 1) + RING)
                        ins = nc.tensor.matmul(bank[:, 0:HALF], ones[0:ROWS[0], :],
                                               sums[0:ROWS[0], a, c * HALF:(c + 1) * HALF], start=True, stop=True)
                        if c == 1:
                            ins.then_inc(sem("x1_side_ready"), 1)
                            return ins
                    ins.then_inc(sem("x1_side_ready"), 1)

                pe.wait_ge(sem("x1_ones_ready"), 1)
                pe.wait_ge(sem("x1_select_ready"), 1)
                for k in range(nj):
                    job(*jobs[k], k, 0, 0, 0, 0)

                def values_product(b, u, v, c):
                    unit, t = v // TT, v % TT
                    if t == 0:
                        pe.wait_ge(sem("x1_averages_ready"), 4 * b + 2 * unit + 1 + c)
                    if c == 0:
                        pe.wait_ge(sem("x1_probs_ready"), STEPS * b + v + 1 + 2)
                    ins = nc.tensor.matmul(ps[:, ACC + c, 0:HALF], ctx[0:ROWS[t], u, t, :],
                                           probs[0:ROWS[t], v % RING, c * HALF:(c + 1) * HALF],
                                           start=(t == 0), stop=(t == TT - 1))
                    if c == 1:
                        ins.then_inc(sem("x1_product_done"), 1)

                def sequence(b, u, first, last):
                    order = side_order_1(first, last)
                    for s in range(STEPS + (LAG + 1 if last else 0)):
                        mine = [(p, o) for p, o in enumerate(order) if o[0] == s]
                        for p, (_, ahead, kind, a, c) in mine:
                            if kind == "sum":
                                job(kind, a, c, p, b + ahead, u, None, base(b, first, 2))
                        if s < STEPS:
                            unit, t = s // TT, s % TT
                            if s == 0:
                                pe.wait_ge(sem("x1_shift_loaded"), 16 * (b + 1))
                                pe.wait_ge(sem("x1_low_ready"), splits * (b + 1))
                                pe.wait_ge(sem("x1_mask_ready"), b + 1)
                            pe.wait_ge(sem("x1_probs_ready"), STEPS * b + s + 1)
                            r, o = ROWS[t], OFF[t]
                            for k, (left, right) in enumerate(((chigh, qhigh), (chigh, qlow), (clow, qhigh))):
                                for c in range(2):
                                    q0 = (UNIT * unit + HC * c) * S
                                    nc.tensor.matmul(ps[0:r, 2 * (s % 2) + c, 0:HALF], left[:, u, o:o + r],
                                                     right[:, u, q0:q0 + HALF], start=(k == 0), stop=False)
                            for c in range(2):
                                h0 = UNIT * unit + HC * c
                                ins = nc.tensor.matmul(ps[0:r, 2 * (s % 2) + c, 0:HALF], masked[:, u, o:o + r],
                                                       select[:, u, h0:h0 + HC, :].rearrange("p h s -> p (h s)"),
                                                       start=False, stop=True)
                            ins.then_inc(sem("x1_scores_ready"), 1)
                        side = [o for o in mine if o[1][2] != "sum"]
                        v = s - LAG
                        for part in range(3):
                            for p, (_, ahead, kind, a, c) in share(side, part, 3):
                                job(kind, a, c, p, b + 1, 1 - u, None, base(b, first, 2))
                            if part < 2 and 0 <= v < STEPS:
                                values_product(b, u, v, part)
                            elif part < 2 and v < 0 and not first:
                                values_product(b - 1, 1 - u, v + STEPS, part)

                run_sequences(pe, sequence)

            @block.scalar
            def _(act):
                act.sem_inc(sem("x1_probs_ready"), 2)

                def job(kind, a, c, p, n, u, before):
                    if kind not in ("q", "tr"):
                        return
                    act.wait_ge(sem("x1_side_ready"), before + p + 1)
                    bank = ps[:, SIDE1 + p % 2, :]
                    if kind == "q":
                        dst, w = qhigh[:, u, HALF * a:HALF * (a + 1)], HALF
                    else:
                        o, w = CHUNKS[a]
                        dst = chigh[:, u, o:o + w]
                    nc.scalar.activation(dst, bank[:, 0:w], ACT.Copy).then_inc(sem("x1_high_ready"), 1)

                for k in range(nj):
                    job(*jobs[k], k, 0, 0, 0)

                def sequence(b, u, first, last):
                    order = side_order_1(first, last)
                    for s in range(STEPS):
                        if s < STEPS:
                            r = ROWS[s % TT]
                            act.wait_ge(sem("x1_scores_ready"), STEPS * b + s + 1)
                            act.wait_ge(sem("x1_product_done"), STEPS * b + s + 1)
                            act.wait_ge(sem("x1_sums_done"), STEPS * b + s + 1)
                            nc.scalar.activation(halves(probs[0:r, s % RING, :], HALF),
                                                 ps[0:r, 2 * (s % 2):2 * (s % 2) + 2, 0:HALF], ACT.Exp, scale=SCALE1
                                                 ).then_inc(sem("x1_probs_ready"), 1)
                        for p, (at, ahead, kind, a, c) in enumerate(order):
                            if at == s:
                                job(kind, a, c, p, b + 1, 1 - u, base(b, first))

                run_sequences(act, sequence)

            @block.vector
            def _(dve):
                dve.sem_inc(sem("x1_product_done"), RING)
                dve.sem_inc(sem("x1_sums_done"), RING)
                dve.sem_inc(sem("x1_averages_ready"), 2)
                dve.sem_inc(sem("x1_side_free0"), 1)
                dve.sem_inc(sem("x1_side_free1"), 1)
                last_n = [j for j in jobs if j[0] == "n"][-1]

                def job(kind, a, c, p, n, u, before, half_before, splits_before):
                    free = sem(f"x1_side_free{p % 2}")
                    dve.wait_ge(sem("x1_side_ready"), before + p + 1)
                    bank = ps[:, SIDE1 + p % 2, :]
                    if kind in ("q", "tr"):
                        dve.wait_ge(sem("x1_high_ready"), splits * n + splits_before + 1)
                        if kind == "q":
                            high, low, w = qhigh, qlow, HALF
                            o = HALF * a
                        else:
                            high, low, (o, w) = chigh, clow, CHUNKS[a]
                        nc.vector.tensor_tensor(low[:, u, o:o + w], bank[:, 0:w], high[:, u, o:o + w], ALU.subtract
                                                ).then_inc(sem("x1_low_ready"), 1)
                        dve.wait_ge(sem("x1_low_ready"), splits * n + splits_before + 1)
                        dve.sem_inc(free, 1)
                    elif kind == "n":
                        o, w = CHUNKS[c]
                        if a == 0 and c == 0:
                            dve.wait_ge(sem("x1_mask_ready"), n + 1)
                        wait_apart(dve, sem("vector_waits"))
                        nc.vector.tensor_tensor_reduce(junk[:, p % 2, 0:w], bank[0:S, 0:w], masked[0:S, u, o:o + w],
                                                       1.0, -3.0e38, ALU.add, ALU.max, mx[:, a, c:c + 1]
                                                       ).then_inc(free, 1)
                        if (kind, a, c) == last_n:
                            dve.wait_ge(free, half_before + p // 2 + 2)
                            float16_parts(core, dve, "x1", n, mx[:, :, :], negmax[:, :],
                                          [parts[:, r, :] for r in range(SHIFT)], rest[:, :], negmax[:, :]
                                          ).then_inc(sem("x1_parts_ready"), 1)
                    elif kind == "m":
                        if not isinstance(n, int) or n:
                            dve.wait_ge(sem("x1_shift_loaded"), 16 * n)
                        nc.vector.tensor_copy(shift[:, :], bank[0:SHIFT * H, 0:S]
                                              ).then_inc(sem("x1_shift_ready"), 1)
                        dve.wait_ge(sem("x1_shift_ready"), n + 1)
                        dve.sem_inc(free, 1)
                    else:
                        nc.vector.reciprocal(inverse[:, c, :], bank[:, 0:HALF]).then_inc(free, 1)
                        if c == 1:
                            dve.sem_inc(sem("x1_sums_used"), 1)
                        dve.wait_ge(free, half_before + p // 2 + 2)
                        dve.wait_ge(sem("x1_product_done"), STEPS * n + TT * (a + 1) + RING)
                        h0 = (UNIT * a + HC * c) * S
                        nc.vector.tensor_tensor(averages[:, bass.ds(n, 1), h0:h0 + HALF],
                                                ps[:, ACC + c, 0:HALF].unsqueeze(1), inverse[:, c, :].unsqueeze(1),
                                                ALU.mult).then_inc(sem("x1_averages_ready"), 1)

                for k in range(nj):
                    job(*jobs[k], k, 0, 0, 0, 0, count(jobs, ("q", "tr"), k))

                def sequence(b, u, first, last):
                    seen = 0
                    for p, (_, ahead, kind, a, c) in enumerate(side_order_1(first, last)):
                        job(kind, a, c, p, b + ahead, 1 - u, base(b, first), base(b, first, 2), seen)
                        if kind != "sum":
                            seen += kind in ("q", "tr")

                run_sequences(dve, sequence)


def project_averages_phase(core):
    nc, sem, ps = core.nc, core.sem, core.ps
    with nc.Block() as block:
        @block.tensor
        def _(pe):
            for b in range(NB):
                for h in range(H):
                    ins = nc.tensor.matmul(ps[0:S, 4 + b // 4, D * (b % 4):D * (b % 4 + 1)],
                                           core.averages[:, b, h * S:(h + 1) * S], core.merged_vo[:, h, :],
                                           start=(h == 0), stop=(h == H - 1))
            ins.then_inc(sem("projected_psum"), 1)
            pe.wait_ge(sem("projected_added"), 1)
            transpose_x(core, pe, core.xn, 6).then_inc(sem("projected_xT_psum"), 1)

        @block.scalar
        def _(act):
            act.wait_ge(sem("projected_xT_psum"), 1)
            nc.scalar.activation(halves(core.xT[:, :], HALF), ps[:, 6:8, 0:HALF], ACT.Copy
                                 ).then_inc(sem("projected_xT_ready"), 1)

        @block.vector
        def _(dve):
            link = chain(core, dve, "projected_vector_steps")
            dve.wait_ge(sem("projected_psum"), 1)
            link(nc.vector.tensor_copy(core.work[:, :, :], token_banks(core, 4)))
            add_gated(core, link, 1, core.work)
            layer_norm(core, link, core.xn, core.x)
            dve.sem_inc(sem("projected_added"), 1)


def experts_phase(core):
    nc, sem, ps, dram = core.nc, core.sem, core.ps, core.dram
    with ExitStack() as own:
        def sb(name, shape, dt=F32):
            return core.sb(name, shape, dt, own)

        gate_w = sb("gate_w", [D, NE])
        gate_b = sb("gate_b", [S, NE])
        up = sb("expert_up", [D, 2, FF])
        up_bias = sb("expert_up_bias", [D, 2, FT])
        down = sb("expert_down", [D, 2, FT, D])
        b2 = sb("expert_b2", [NE, D])
        hidden = sb("expert_hidden", [D, FT, NTOK])
        logits = sb("router_scores", [S, NB, NE])
        best = sb("router_best", [S, NB, NE])
        greater = sb("router_greater", [S, NB, NE, NE])
        equal = sb("router_equal", [S, NB, NE, NE])
        lower = sb("router_lower", [S, NE, NE])
        rank = sb("router_rank", [S, NB, NE])
        e2 = sb("router_second", [S, NB])
        w1 = sb("router_w1", [S, NB])
        w2 = sb("router_w2", [S, NB])
        comb = sb("router_weights", [S, NB, NE])
        second = sb("router_weights_second", [S, NB, NE])
        combT = sb("router_weightsT", [NE, NTOK])
        part = sb("expert_part", [S, NB, D])

        def over_features(ap):
            return ap.broadcast_to([S, NB, D])

        with nc.Block() as block:
            @block.sync
            def _(sp):
                sp.dma_start(gate_w[:, :], dram["L1_ffn_gate_w"]).then_inc(sem("router_loaded"), 16)
                sp.dma_start(gate_b[:, :], dram["L1_ffn_gate_b"].rearrange("(o e) -> o e", o=1).broadcast_to([S, NE])
                             ).then_inc(sem("router_loaded"), 16)
                sp.dma_start(b2[:, :], dram["L1_ffn_b2"]).then_inc(sem("router_loaded"), 16)

                with sp.Fori(0, NE // 2) as i:
                    for u in range(2):
                        e = 2 * i + u
                        sp.wait_ge(sem("expert_used"), e + 1)
                        sp.dma_start(up[:, u, :], dram["L1_ffn_w1"][bass.ds(e, 1), :, :].rearrange("o d f -> (o d) f")
                                     ).then_inc(sem(f"expert_weights_loaded{u}"), 16)
                        sp.dma_start(up_bias[:, u, :], dram["L1_ffn_b1"][bass.ds(e, 1), :].rearrange(
                            "o (f p) -> (o p) f", p=D), allow_slow_non_contiguous=True).then_inc(sem(f"expert_weights_loaded{u}"), 16)
                        sp.dma_start(down[:, u, :, :], dram["L1_ffn_w2"][bass.ds(e, 1), :, :].rearrange(
                            "o (f p) d -> (o p) f d", p=D)).then_inc(sem(f"expert_weights_loaded{u}"), 16)

            @block.gpsimd
            def _(pool):
                pool.memset(lower[:, :, :], 1.0).then_inc(sem("router_lower_ready"), 1)
                pool.wait_ge(sem("router_lower_ready"), 1)
                pool.affine_select(out=lower[:, :, :], in_=lower[:, :, :], compare_op=ALU.is_gt, fill=0.0, base=0,
                                   pattern=[[1, NE], [-1, NE]], channel_multiplier=0
                                   ).then_inc(sem("router_lower_ready"), 1)

            @block.tensor
            def _(pe):
                pe.wait_ge(sem("router_loaded"), 48)
                for b in range(NB):
                    ins = nc.tensor.matmul(ps[0:S, 6, NE * b:NE * (b + 1)], core.xT[:, b * S:(b + 1) * S], gate_w[:, :],
                                           start=True, stop=True)
                ins.then_inc(sem("router_psum"), 1)
                with pe.Fori(0, NE // 2) as i:
                    for u in range(2):
                        e = 2 * i + u
                        pe.wait_ge(sem(f"expert_weights_loaded{u}"), 48 * i + 48)
                        hidden_layer(core, pe, up[:, u, :], sem("expert_hidden_free"), sem("expert_hidden_psum"), FT * e)
                        pe.wait_ge(sem("expert_hidden_free"), FT * e + FT + 2)
                        pe.wait_ge(sem("expert_out_free"), e + 1)
                        output_layer(core, pe, down[:, u, :, :], hidden, 4).then_inc(sem("expert_out_psum"), 1)
                pe.wait_ge(sem("router_weights_ready"), 1)
                for b in range(NB):
                    ins = nc.tensor.transpose(ps[0:NE, 6 + b // 4, (b % 4) * S:(b % 4 + 1) * S], comb[:, b, :],
                                              core.ident[0:S, 0:S])
                ins.then_inc(sem("router_weightsT_psum"), 1)
                pe.wait_ge(sem("router_weightsT_ready"), 1)
                for b in range(NB):
                    ins = nc.tensor.matmul(ps[0:S, b // 4, D * (b % 4):D * (b % 4 + 1)], combT[:, b * S:(b + 1) * S],
                                           b2[:, :], start=True, stop=True)
                ins.then_inc(sem("expert_bias_psum"), 1)

            @block.scalar
            def _(act):
                act.sem_inc(sem("expert_hidden_free"), 2)
                act.wait_ge(sem("router_gap_ready"), 1)
                nc.scalar.activation(e2[:, :], e2[:, :], ACT.Exp).then_inc(sem("router_exp_ready"), 1)
                with act.Fori(0, NE // 2) as i:
                    for u in range(2):
                        e = 2 * i + u
                        act.wait_ge(sem("expert_out_psum"), e + 1)
                        act.wait_ge(sem(f"expert_weights_loaded{u}"), 48 * i + 48)
                        for f in range(FT):
                            act.wait_ge(sem("expert_hidden_psum"), FT * e + f + 1)
                            nc.scalar.activation(halves(hidden[:, f, :], HALF),
                                                 ps[:, 2 * (f % 2):2 * (f % 2) + 2, 0:HALF], ACT.Relu,
                                                 bias=up_bias[:, u, f:f + 1]).then_inc(sem("expert_hidden_free"), 1)
                act.wait_ge(sem("router_weightsT_psum"), 1)
                nc.scalar.activation(halves(combT[:, :], HALF), ps[0:NE, 6:8, 0:HALF], ACT.Copy
                                     ).then_inc(sem("router_weightsT_ready"), 1)

            @block.vector
            def _(dve):
                dve.sem_inc(sem("expert_used"), 2)
                dve.sem_inc(sem("expert_out_free"), 1)
                dve.sem_inc(sem("expert_out_psum"), 1)
                link = chain(core, dve, "router_steps")
                dve.wait_ge(sem("router_psum"), 1)
                link(nc.vector.tensor_tensor(logits[:, :, :], ps[0:S, 6, 0:NB * NE].rearrange("s (b e) -> s b e", e=NE),
                                             gate_b[:, :].unsqueeze(1).broadcast_to([S, NB, NE]), ALU.add))
                for b in range(NB):
                    ins = nc.vector.max(best[:, b, :], logits[:, b, :])
                link(ins)
                nc.vector.tensor_tensor(e2[:, :], best[:, :, 1], best[:, :, 0], ALU.subtract
                                        ).then_inc(sem("router_gap_ready"), 1)
                dve.wait_ge(sem("router_lower_ready"), 2)
                for b in range(NB):
                    other = logits[:, b, :].unsqueeze(1).broadcast_to([S, NE, NE])
                    mine = logits[:, b, :].unsqueeze(2).broadcast_to([S, NE, NE])
                    nc.vector.tensor_tensor(greater[:, b, :, :], other, mine, ALU.is_gt)
                    ins = nc.vector.tensor_tensor(equal[:, b, :, :], other, mine, ALU.is_equal)
                link(ins)
                link(nc.vector.tensor_tensor(
                    equal[:, :, :, :].rearrange("s b e f -> s b (e f)"), equal[:, :, :, :].rearrange("s b e f -> s b (e f)"),
                    lower[:, :, :].rearrange("s e f -> s (e f)").unsqueeze(1).broadcast_to([S, NB, NE * NE]), ALU.mult))
                link(nc.vector.tensor_tensor(greater[:, :, :, :].rearrange("s b e f -> s (b e f)"),
                                             greater[:, :, :, :].rearrange("s b e f -> s (b e f)"),
                                             equal[:, :, :, :].rearrange("s b e f -> s (b e f)"), ALU.add))
                link(nc.vector.tensor_reduce(rank[:, :, :], greater[:, :, :, :], AX_X, ALU.add))
                dve.wait_ge(sem("router_exp_ready"), 1)
                link(nc.vector.tensor_scalar(w1[:, :], e2[:, :], 1.0, None, ALU.add))
                link(nc.vector.reciprocal(w1[:, :], w1[:, :]))
                link(nc.vector.tensor_tensor(w2[:, :], e2[:, :], w1[:, :], ALU.mult))
                nc.vector.tensor_scalar(comb[:, :, :], rank[:, :, :], 0.0, None, ALU.is_equal)
                link(nc.vector.tensor_scalar(second[:, :, :], rank[:, :, :], 1.0, None, ALU.is_equal))
                link(nc.vector.tensor_tensor(comb[:, :, :], comb[:, :, :],
                                             w1[:, :].unsqueeze(2).broadcast_to([S, NB, NE]), ALU.mult))
                link(nc.vector.tensor_tensor(second[:, :, :], second[:, :, :],
                                             w2[:, :].unsqueeze(2).broadcast_to([S, NB, NE]), ALU.mult))
                link(nc.vector.tensor_tensor(comb[:, :, :], comb[:, :, :], second[:, :, :], ALU.add))
                dve.sem_inc(sem("router_weights_ready"), 1)
                link(nc.vector.memset(core.work[:, :, :], 0.0))

                with dve.Fori(0, NE // 2) as i:
                    for u in range(2):
                        e = 2 * i + u
                        dve.wait_ge(sem("expert_out_psum"), e + 2)
                        dve.sem_inc(sem("expert_used"), 1)
                        nc.vector.tensor_tensor(part[:, :, :], token_banks(core, 4), over_features(comb[:, :, bass.ds(e, 1)]),
                                                ALU.mult).then_inc(sem("expert_out_free"), 1)
                        dve.wait_ge(sem("expert_out_free"), e + 2)
                        nc.vector.tensor_tensor(core.work[:, :, :], core.work[:, :, :], part[:, :, :], ALU.add
                                                ).then_inc(sem("expert_added"), 1)
                        dve.wait_ge(sem("expert_added"), e + 1)
                dve.wait_ge(sem("expert_bias_psum"), 1)
                link(nc.vector.tensor_tensor(core.work[:, :, :], core.work[:, :, :], token_banks(core, 0), ALU.add))
                add_gated(core, link, 3, core.work)


INPUTS = ["x", "ctx_1024", "mask_BxSxS2_bf1", "g_xattn", "g_ffn"] + [
    f"L0_xattn_{n}" for n in ("Wq1", "Wk1", "Wv1", "bv1", "Wq2", "Wk2", "Wv2", "bv2", "g1", "be1", "g2", "be2", "g3",
                              "be3", "Wf1", "bf1", "Wf2", "bf2")] + [
    f"L0_ffn_{n}" for n in ("w1", "b1", "w2", "b2", "gamma", "beta")] + [
    f"L1_xattn_{n}" for n in ("Wq", "Wk", "Wv", "Wo")] + [
    f"L1_ffn_{n}" for n in ("gate_w", "gate_b", "w1", "b1", "w2", "b2")]


def store_phase(core, what):
    nc, sem = core.nc, core.sem
    with nc.Block() as block:
        @block.sync
        def _(sp):
            sp.dma_start(core.out.rearrange("b s d -> s b d"), what[:, :, :]).then_inc(sem("out_stored"), 16)
            sp.wait_ge(sem("out_stored"), 16)


def program(nc, dram, out):
    with ExitStack() as stack:
        core = Core(nc, stack, dram, out)
        core.oT = core.sb("oT", [128, NB, G * S])
        core.negmax = core.sb("negmax", [S, G * J * NB])
        core.row_sums = core.sb("row_sums", [S, NB, G, J])
        core.ctx = core.sb("context", [128, 2, TT, D])
        setup_phase(core)
        self_attention_phase(core)
        finish_attention_phase(core, "self")
        cross_attention_0_phase(core)
        finish_attention_phase(core, "cross")
        feed_forward_phase(core, "ffn", core.row["bf2"], core.row["g3"], core.row["be3"], 0)
        feed_forward_phase(core, "expert0", core.row_e["b2"], core.row_e["gamma"], core.row_e["beta"], 2)
        core.averages = core.sb("averages", [D, NB, H * S])
        core.merged_qk = core.sb("merged_qk", [D, H, D])
        core.merged_vo = core.sb("merged_vo", [D, H, D])
        merge_weights_phase(core)
        cross_attention_1_phase(core)
        project_averages_phase(core)
        experts_phase(core)
        store_phase(core, core.x)


def kernel(**inputs):
    import numpy as _np
    import concourse.bacc as _bacc
    from concourse import mybir as _mybir
    from concourse.bass_utils import run_bass_kernel_spmd as _run

    nc = _bacc.Bacc("TRN2", target_bir_lowering=False, num_devices=1)
    arrays, dram = {}, {}
    for name in INPUTS:
        a = _np.ascontiguousarray(inputs[name])
        if a.dtype == _np.bool_:
            a = a.view(_np.uint8)
        arrays[f"in_{name}"] = a
        dram[name] = nc.dram_tensor(f"in_{name}", a.shape, _mybir.dt.from_np(a.dtype), kind="ExternalInput").ap()
    out = nc.dram_tensor("out_x", (NB, S, D), _mybir.dt.float32, kind="ExternalOutput").ap()
    program(nc, dram, out)
    return _run(nc, [arrays], core_ids=[0]).results[0]["out_x"]
```

```python
from contextlib import ExitStack
from math import log

import concourse.bass as bass
from concourse import mybir

F32 = mybir.dt.float32
F16 = mybir.dt.float16
U8 = mybir.dt.uint8
I32 = mybir.dt.int32
ALU = mybir.AluOpType
ACT = mybir.ActivationFunctionType
AX_X = mybir.AxisListType.X

NB, S, D, T, H = 8, 100, 128, 1444, 16
NTOK = NB * S
HALF = NTOK // 2
G, J = 4, 4
E0 = D // H
STACK = 3 * E0
SHIFT = 3
E1 = 64
FF = 512
FT = FF // D
NE = 8
EPS = 1e-5

HC = 4
UNIT = H // 2
BOOST = 64.0
MASKED = -60000.0
TT = -(-T // 128)
ROWS = [T // TT + (t < T % TT) for t in range(TT)]
OFF = [sum(ROWS[:t]) for t in range(TT)]
NG = 3
GT = TT // NG
CHUNKS = [(OFF[GT * q], sum(ROWS[GT * q:GT * q + GT])) for q in range(NG)]
NC = NG
TALL = T % TT
assert TT == NG * GT and TALL == GT and max(w for _, w in CHUNKS) <= 512
SCALE0 = float(E0) ** -0.5
SCALE1 = float(S) ** -0.5
STEPS = 2 * TT
LAG = 2
RING = 4
HALF_RING = 3
JOB_STEPS0 = (0, 20.5, 21)
JOB_STEPS1 = (0, 21, 21)
WEIGHTS0 = {"q": 1.5, "tr": 1.5, "k": 1.2, "v": 1.0, "n": 2.0}
WEIGHTS1 = {"q": 1.0, "tr": 1.0, "n": 0.3}
ACC = 4
SIDE0, SIDES0 = 5, 3
SIDE1, SIDES1 = 6, 2
EARLY_BANKS = (0, 1, 2, 3, 6, 7)


MARKS = [(E0, 2 * E0, -1.0), (STACK, STACK + SHIFT, 1.0), (2 * E0, STACK, -1.0), (STACK, STACK + SHIFT, 1.0)]


def spread(jobs, weights, first, last, step_of_m):
    shares = [weights[job[0]] for job in jobs[:-1]]
    steps = [[] for _ in range(STEPS)]
    for k in range(len(shares)):
        steps[int(first + (last - first) * sum(shares[:k]) / sum(shares))].append(k)
    steps[step_of_m].append(len(jobs) - 1)
    return steps


def share(items, k, of):
    return items[len(items) * k // of:len(items) * (k + 1) // of]


JOBS0 = ([("q", p, 0) for p in range(2)] + [("tr", q, 0) for q in range(NG)]
         + [("k", c, j) for c in range(NC) for j in range(J)] + [("v", q, 0) for q in range(NG)]
         + [("n", h, c) for c in range(NC) for h in range(H)] + [("m", 0, 0)])
assert len(JOBS0) % SIDES0 == 0
JOBS1 = ([("q", q, 0) for q in range(H // HC)] + [("tr", q, 0) for q in range(NG)]
         + [("n", h, c) for h in range(H) for c in range(NC)] + [("m", 0, 0)])
assert len(JOBS1) % SIDES1 == 0
AT_STEP0, AT_STEP1 = spread(JOBS0, WEIGHTS0, *JOB_STEPS0), spread(JOBS1, WEIGHTS1, *JOB_STEPS1)


def count(jobs, kinds, k=None):
    return sum(job[0] in kinds for job in jobs[:k])


class Core:

    def __init__(self, nc, stack, dram, out):
        self.nc, self.stack, self.dram, self.out = nc, stack, dram, out
        self.sems, self.links = {}, {}

    def sem(self, name):
        if name not in self.sems:
            self.sems[name] = self.stack.enter_context(self.nc.semaphore(name))
        return self.sems[name]

    def sb(self, name, shape, dt=F32, stack=None):
        return (stack or self.stack).enter_context(self.nc.sbuf_tensor(name, shape, dt))


def chain(core, eng, name):
    done = core.sem(name)

    def link(ins):
        core.links[name] = core.links.get(name, 0) + 1
        ins.then_inc(done, 1)
        eng.wait_ge(done, core.links[name])

    return link


def inverse_root(core, link, root, var):
    nc, half, t = core.nc, core.ln_half[:, :], core.ln_t[:, :]
    link(nc.vector.tensor_scalar(root, var, EPS, None, ALU.add))
    link(nc.vector.tensor_scalar(half, root, -0.5, None, ALU.mult))
    link(nc.vector.tensor_scalar(root.bitcast(I32), root.bitcast(I32), -0.5, float(0x5F3759DF), ALU.mult, ALU.add))
    for _ in range(3):
        link(nc.vector.tensor_tensor(t, root, root, ALU.mult))
        link(nc.vector.tensor_tensor(t, t, half, ALU.mult))
        link(nc.vector.scalar_tensor_tensor(out=root, in0=t, scalar=1.5, in1=root, op0=ALU.add, op1=ALU.mult))


def layer_norm(core, link, dst, src, gain=None, shift=None):
    nc, st, mv, rstd = core.nc, core.ln_stats, core.ln_mv, core.ln_rstd
    for b in range(NB):
        ins = nc.vector.bn_stats(st[:, b, :], src[:, b, :])
    link(ins)
    for b in range(NB):
        ins = nc.vector.bn_aggr(mv[:, b, :], st[:, b, :])
    link(ins)
    inverse_root(core, link, rstd[:, :], mv[:, :, 1])
    for b in range(NB):
        ins = nc.vector.tensor_scalar(dst[:, b, :], src[:, b, :], mv[:, b, 0:1], rstd[:, b:b + 1],
                                      ALU.subtract, ALU.mult)
    link(ins)
    if gain is not None:
        link(nc.vector.tensor_tensor(dst[:, :, :], dst[:, :, :], rows(gain), ALU.mult))
        link(nc.vector.tensor_tensor(dst[:, :, :], dst[:, :, :], rows(shift), ALU.add))


def rows(row):
    return row[0:S, :].unsqueeze(1).broadcast_to([S, NB, D])


def transpose_x(core, pe, src, bank):
    for b in range(NB):
        ins = core.nc.tensor.transpose(core.ps[:, bank + b // 4, (b % 4) * S:(b % 4 + 1) * S],
                                       src[:, b, :], core.ident[0:S, 0:S])
    return ins


def split_stack(core, eng, dst, psum, high, signs):
    return core.nc.vector.scalar_tensor_tensor(out=dst, in0=high, scalar=signs, in1=psum,
                                               op0=ALU.mult, op1=ALU.add)


def shift_parts(core, link, parts, psum, rest):
    nc = core.nc
    link(nc.vector.tensor_copy(parts[:, 0, :], psum))
    link(nc.vector.tensor_tensor(rest, psum, parts[:, 0, :], ALU.subtract))
    link(nc.vector.tensor_copy(parts[:, 1, :], rest))
    link(nc.vector.tensor_tensor(rest, rest, parts[:, 1, :], ALU.subtract))
    return nc.vector.tensor_copy(parts[:, 2, :], rest)


def setup_phase(core, layer0):
    nc, dram, sem = core.nc, core.dram, core.sem
    core.ps = core.stack.enter_context(nc.psum_tensor("psum", [128, 8, 512], F32))
    core.x = core.sb("x", [S, NB, D])
    core.xn = core.sb("normalised", [S, NB, D])
    core.work = core.sb("work", [S, NB, D])
    core.xT = core.sb("xT", [D, NTOK])
    core.ident = core.sb("identity", [128, 128])
    core.ident4 = core.sb("identity_heads", [S, J, S], F16)
    core.ln_stats = core.sb("ln_stats", [S, NB, 6])
    core.ln_mv = core.sb("ln_mean_var", [S, NB, 2])
    core.ln_rstd = core.sb("ln_rstd", [S, NB])
    core.ln_half = core.sb("ln_half", [S, NB])
    core.ln_t = core.sb("ln_t", [S, NB])
    core.gates = core.sb("gates", [128, 4])
    core.ctx = core.sb("context", [128, 2, TT, D])

    def sb(name, shape, dt=F32):
        return core.sb(name, shape, dt, layer0)

    core.oT = sb("oT", [128, NB, G * S])
    core.negmax = sb("negmax", [S, 2, G * J * NB // 2])
    core.row_sums = sb("row_sums", [S, NB, G, J])
    core.causal4 = sb("causal_heads", [S, J, S], F16)
    core.signs_k = sb("signs_keys", [128, 1])
    core.signs_q = sb("signs_queries", [128, 1])
    core.ones_k = sb("ones_keys", [128, 1])
    core.wstack = {n: sb(f"stack_{n}", [D, J, 128]) for n in ("Wq1", "Wk1", "Wq2", "Wk2")}
    core.wraw = {n: sb(f"raw_{n}", [D, H, E0]) for n in ("Wq1", "Wk1", "Wv1", "Wq2", "Wk2", "Wv2")}
    names = {"bv1": H * E0, "bv2": H * E0, "g1": D, "be1": D, "g2": D, "be2": D, "g3": D, "be3": D,
             "bf2": D}
    core.row = {n: sb(f"row_{n}", [S, w]) for n, w in names.items()}
    core.row_e = {n: sb(f"row_{n}", [S, D]) for n in ("b2", "gamma", "beta")}
    core.dense = {n: (sb(f"{n}_up", [D, FF]), sb(f"{n}_up_bias", [D, FT]), sb(f"{n}_down", [D, FT, D]))
                  for n in ("ffn", "expert0")}
    row_marks = sb("row_marks", [128, len(MARKS), G])

    with nc.Block() as block:
        @block.sync
        def _(sp):
            sp.dma_start(core.x[:, :, :], dram["x"].rearrange("b s d -> s b d")).then_inc(sem("x_loaded"), 16)
            for n in ("Wq1", "Wk1", "Wv1"):
                sp.dma_start(core.wraw[n][:, :, :], dram[f"L0_xattn_{n}"].rearrange("h d e -> d h e")
                             ).then_inc(sem("self_weights_loaded"), 16)
            for n in ("Wq2", "Wk2", "Wv2"):
                sp.dma_start(core.wraw[n][:, :, :], dram[f"L0_xattn_{n}"].rearrange("h d e -> d h e")
                             ).then_inc(sem("cross_weights_loaded"), 16)
            for n, up, up_bias, down in (
                    ("ffn", dram["L0_xattn_Wf1"], dram["L0_xattn_bf1"], dram["L0_xattn_Wf2"]),
                    ("expert0", dram["L0_ffn_w1"][0], dram["L0_ffn_b1"][0], dram["L0_ffn_w2"][0])):
                for dst, src in zip(core.dense[n], (up, up_bias.rearrange("(f p) -> p f", p=D),
                                                    down.rearrange("(f p) d -> p f d", p=D))):
                    sp.dma_start(dst[tuple(slice(None) for _ in dst.shape)], src, allow_slow_non_contiguous=True
                                 ).then_inc(sem(f"{n}_loaded"), 16)

        @block.scalar
        def _(act):
            for n, w in names.items():
                src = dram[f"L0_xattn_{n}"]
                src = src.rearrange("h e -> (h e)") if len(src.shape) == 2 else src
                act.dma_start(core.row[n][:, :], src.rearrange("(o w) -> o w", o=1).broadcast_to([S, w])
                              ).then_inc(sem("rows_loaded"), 16)
            for k, n in enumerate(("g_xattn", "g_ffn")):
                act.dma_start(core.gates[:, 2 * k:2 * k + 2],
                              dram[n].rearrange("(o w) -> o w", o=1).broadcast_to([128, 2])
                              ).then_inc(sem("gates_loaded"), 16)
            for n, src in (("b2", dram["L0_ffn_b2"][0:1, :]),
                           ("gamma", dram["L0_ffn_gamma"].rearrange("(o w) -> o w", o=1)),
                           ("beta", dram["L0_ffn_beta"].rearrange("(o w) -> o w", o=1))):
                act.dma_start(core.row_e[n][:, :], src.broadcast_to([S, D])).then_inc(sem("expert_rows_loaded"), 16)
            act.wait_ge(sem("gates_loaded"), 32)
            nc.scalar.activation(core.gates[:, :], core.gates[:, :], ACT.Tanh).then_inc(sem("gates_ready"), 1)

        @block.gpsimd
        def _(pool):
            link = chain(core, pool, "pool_steps")
            link(nc.gpsimd.memset(core.ident[:, :], 0.0))
            link(nc.gpsimd.affine_select(out=core.ident[:, :], in_=core.ident[:, :], compare_op=ALU.not_equal,
                                         fill=1.0, base=0, pattern=[[-1, 128]], channel_multiplier=1))
            nc.gpsimd.tensor_copy(core.ident4[:, :, :],
                                  core.ident[0:S, 0:S].unsqueeze(1).broadcast_to([S, J, S])
                                  ).then_inc(sem("identity_ready"), 1)
            link(nc.gpsimd.memset(core.causal4[:, :, :], 0.0))
            nc.gpsimd.affine_select(out=core.causal4[:, :, :], in_=core.causal4[:, :, :], compare_op=ALU.is_ge,
                                    fill=MASKED, base=0, pattern=[[0, J], [-1, S]], channel_multiplier=1
                                    ).then_inc(sem("causal_ready"), 1)
            for k, (lo, hi, value) in enumerate(MARKS):
                marks = row_marks[:, k, :]
                link(nc.gpsimd.memset(marks, value))
                link(nc.gpsimd.affine_select(out=marks, in_=marks, compare_op=ALU.is_ge, fill=0.0, base=-lo,
                                             pattern=[[-32, G]], channel_multiplier=1))
                ins = nc.gpsimd.affine_select(out=marks, in_=marks, compare_op=ALU.is_ge, fill=0.0,
                                              base=hi - 1, pattern=[[32, G]], channel_multiplier=-1)
                if k + 1 < len(MARKS):
                    link(ins)
            ins.then_inc(sem("marks_ready"), 1)

        @block.vector
        def _(dve):
            link = chain(core, dve, "vector_steps")
            for n in core.wstack:
                link(nc.vector.memset(core.wstack[n][:, :, :], 0.0))
            dve.wait_ge(sem("x_loaded"), 16)
            layer_norm(core, link, core.xn, core.x)
            dve.sem_inc(sem("x_normalised"), 1)
            dve.wait_ge(sem("marks_ready"), 1)
            nc.vector.tensor_reduce(core.signs_k[:, :], row_marks[:, 0:2, :].rearrange("p a g -> p (a g)"),
                                    AX_X, ALU.add)
            nc.vector.tensor_reduce(core.signs_q[:, :], row_marks[:, 2, :], AX_X, ALU.add)
            nc.vector.tensor_reduce(core.ones_k[:, :], row_marks[:, 3, :], AX_X, ALU.add
                                    ).then_inc(sem("signs_ready"), 1)
            for n, loaded in {"Wq1": "self_weights_loaded", "Wk1": "self_weights_loaded",
                              "Wq2": "cross_weights_loaded", "Wk2": "cross_weights_loaded"}.items():
                dve.wait_ge(sem(loaded), 48)
                order = "d (g j) e -> d g j e" if n in ("Wq1", "Wk1") else "d (j g) e -> d g j e"
                for r in range(3):
                    ins = nc.vector.tensor_copy(
                        core.wstack[n][:, :, :].rearrange("d j (g r) -> d g j r", g=G)[:, :, :, E0 * r:E0 * r + E0],
                        core.wraw[n][:, :, :].rearrange(order, j=J))
                ins.then_inc(sem("stack_weights_ready"), 1)


def self_attention_phase(core):
    nc, sem, ps = core.nc, core.sem, core.ps
    with ExitStack() as own:
        def sb(name, shape, dt=F32):
            return core.sb(name, shape, dt, own)

        high = sb("self_high", [128, 2, 2, HALF], F16)
        qst = sb("self_queries", [128, 2, J, HALF], F16)
        kst = sb("self_keys", [128, J, NTOK], F16)
        values = sb("self_values", [S, NB, H, 32])
        probs = sb("self_probs", [S, RING, 2, J * S])
        mx = sb("self_max", [S, G, J, NB])
        shift = sb("self_shift", [G * J * NB // 2, 2, SHIFT, S], F16)
        rest = sb("self_shift_rest", [G * J * NB // 2, S])

        with nc.Block() as block:
            @block.sync
            def _(sp):
                for b in range(2):
                    load_context_tiles(core, sp, b, b, sem(f"x0_context_loaded{b}"))
                for c in range(2):
                    sp.wait_ge(sem("self_shift_ready"), c + 1)
                    for g in range(G):
                        for r in range(SHIFT):
                            row = 32 * g + STACK + r
                            sp.dma_start(qst[row:row + 1, c, :, :].rearrange("o j n -> o (j n)"),
                                         shift[J * NB // 2 * g:J * NB // 2 * (g + 1), c, r, :]
                                         ).then_inc(sem(f"self_shift_loaded{c}"), 16)

            @block.gpsimd
            def _(pool):
                link = chain(core, pool, "pool_steps")
                link(nc.gpsimd.memset(values[:, :, :, :], 0.0))
                nc.gpsimd.memset(values[:, :, :, E0:E0 + 1], 1.0).then_inc(sem("self_ones_ready"), 1)

            @block.tensor
            def _(pe):
                pe.wait_ge(sem("identity_ready"), 1)
                pe.wait_ge(sem("x_normalised"), 1)
                transpose_x(core, pe, core.xn, 6).then_inc(sem("input_xT_psum"), 1)
                pe.wait_ge(sem("input_xT_ready"), 1)
                pe.wait_ge(sem("stack_weights_ready"), 2)
                for k, n in enumerate(("Wq1", "Wk1")):
                    for j in range(J):
                        i = J * k + j
                        if i >= 2:
                            pe.wait_ge(sem("self_stack_ready"), i - 1)
                        for c in range(2):
                            ins = nc.tensor.matmul(ps[:, 2 * (i % 2) + c, 0:HALF], core.wstack[n][:, j, :],
                                                   core.xT[:, c * HALF:(c + 1) * HALF], start=True, stop=True)
                        ins.then_inc(sem("self_stack_psum"), 1)
                for b in range(NB):
                    ins = nc.tensor.matmul(ps[0:S, 4 + b // 4, 128 * (b % 4):128 * (b % 4 + 1)],
                                           core.xT[:, b * S:(b + 1) * S],
                                           core.wraw["Wv1"][:, :, :].rearrange("d h e -> d (h e)"),
                                           start=True, stop=True)
                ins.then_inc(sem("self_values_psum"), 1)
                pe.wait_ge(sem("self_stack_ready"), 2 * J)
                pe.wait_ge(sem("causal_ready"), 1)
                for b in range(NB):
                    for g in range(G):
                        if b:
                            pe.wait_ge(sem("self_max_ready"), G * (b - 1) + g + 1)
                        bank = ps[0:S, g, 0:HALF]
                        nc.tensor.matmul(bank, core.ident4[:, 0, :],
                                         core.causal4[:, :, :].rearrange("s j t -> s (j t)"),
                                         start=True, stop=False, skip_group_check=True)
                        for j in range(J):
                            ins = nc.tensor.matmul(
                                ps[0:S, g, j * S:(j + 1) * S], qst[32 * g:32 * g + STACK, b // 4, j, (b % 4) * S:(b % 4 + 1) * S],
                                kst[32 * g:32 * g + STACK, j, b * S:(b + 1) * S],
                                start=False, stop=True, skip_group_check=True)
                        ins.then_inc(sem("self_first_scores"), 1)
                    if b in (NB // 2, NB - 1):
                        c = b // (NB - 1)
                        pe.wait_ge(sem("self_negmax_ready"), c + 1)
                        nc.tensor.transpose(ps[0:G * J * NB // 2, 6 + c, 0:S], core.negmax[:, c, :],
                                            core.ident[0:S, 0:S]).then_inc(sem("self_negmax_psum"), 1)
                pe.wait_ge(sem("self_values_ready"), 2)

                def values_product(n):
                    b, half = n // 2, n % 2
                    pe.wait_ge(sem("self_probs_ready"), n + 1)
                    if half == 0 and b >= 2:
                        pe.wait_ge(sem("self_oT_ready"), b - 1)
                    for gg in range(2):
                        g = 2 * half + gg
                        for j in range(J):
                            ins = nc.tensor.matmul(
                                ps[32 * j:32 * j + 32, ACC + b % 2, g * S:(g + 1) * S], values[:, b, J * g + j, :],
                                probs[:, n % RING, gg, j * S:(j + 1) * S], start=(g == 0), stop=True,
                                skip_group_check=True)
                    ins.then_inc(sem("self_product_done"), 1)

                for n in range(2 * NB):
                    b, half = n // 2, n % 2
                    if n % NB == 0:
                        pe.wait_ge(sem(f"self_shift_loaded{n // NB}"), 16 * G * SHIFT)
                    if n >= 2:
                        pe.wait_ge(sem("self_probs_ready"), n - 1)
                    for gg in range(2):
                        g = 2 * half + gg
                        nc.tensor.matmul(ps[0:S, g, 0:HALF], core.causal4[:, 0, :],
                                         core.ident4[:, :, :].rearrange("s j t -> s (j t)"),
                                         start=True, stop=False, skip_group_check=True)
                        for j in range(J):
                            ins = nc.tensor.matmul(
                                ps[0:S, g, j * S:(j + 1) * S],
                                kst[32 * g:32 * g + STACK + SHIFT, j, b * S:(b + 1) * S],
                                qst[32 * g:32 * g + STACK + SHIFT, b // 4, j, (b % 4) * S:(b % 4 + 1) * S],
                                start=False, stop=True, skip_group_check=True)
                    ins.then_inc(sem("self_scores_psum"), 1)
                    if n >= 1:
                        values_product(n - 1)
                values_product(2 * NB - 1)

            @block.scalar
            def _(act):
                act.wait_ge(sem("input_xT_psum"), 1)
                nc.scalar.activation(core.xT[:, :].rearrange("d (c n) -> d c n", c=2), ps[:, 6:8, 0:HALF], ACT.Copy
                                     ).then_inc(sem("input_xT_ready"), 1)
                act.wait_ge(sem("signs_ready"), 1)
                for i in range(2 * J):
                    act.wait_ge(sem("self_stack_psum"), i + 1)
                    if i >= 2:
                        act.wait_ge(sem("self_stack_ready"), i - 1)
                    b = 2 * (i % 2)
                    nc.scalar.activation(high[:, i % 2, :, :], ps[:, b:b + 2, 0:HALF], ACT.Identity,
                                         bias=core.ones_k[:, 0:1] if i >= J else 0.0
                                         ).then_inc(sem("self_high_ready"), 1)
                act.wait_ge(sem("self_values_psum"), 1)
                act.wait_ge(sem("self_ones_ready"), 1)
                for c in range(2):
                    nc.scalar.activation(values[:, 4 * c:4 * c + 4, :, 0:E0],
                                         ps[0:S, 4 + c, :].rearrange("s (b h e) -> s b h e", b=4, h=H), ACT.Copy
                                         ).then_inc(sem("self_values_ready"), 1)
                for n in range(2 * NB):
                    half = n % 2
                    act.wait_ge(sem("self_scores_psum"), n + 1)
                    if n >= RING:
                        act.wait_ge(sem("self_product_done"), n - RING + 1)
                    nc.scalar.activation(probs[:, n % RING, :, :], ps[0:S, 2 * half:2 * half + 2, 0:HALF], ACT.Exp,
                                         scale=SCALE0).then_inc(sem("self_probs_ready"), 1)

            @block.vector
            def _(dve):
                link = chain(core, dve, "vector_steps")
                for i in range(2 * J):
                    dve.wait_ge(sem("self_high_ready"), i + 1)
                    b = 2 * (i % 2)
                    dst = qst[:, :, i, :] if i < J else halves(kst[:, i % J, :], HALF)
                    split_stack(core, dve, dst, ps[:, b:b + 2, 0:HALF], high[:, i % 2, :, :],
                                core.signs_q[:, 0:1] if i < J else core.signs_k[:, 0:1]
                                ).then_inc(sem("self_stack_ready"), 1)
                for b in range(NB):
                    for g in range(G):
                        dve.wait_ge(sem("self_first_scores"), G * b + g + 1)
                        nc.vector.tensor_reduce(mx[:, g, :, b], ps[0:S, g, 0:HALF].rearrange("s (j t) -> s j t", j=J),
                                                AX_X, ALU.max).then_inc(sem("self_max_ready"), 1)
                    if b in (NB // 2 - 1, NB - 1):
                        c = b // (NB - 1)
                        dve.wait_ge(sem("self_max_ready"), G * (b + 1))
                        nc.vector.tensor_scalar(core.negmax[:, c, :].rearrange("s (g j b) -> s g j b", g=G, j=J),
                                                mx[:, :, :, c * NB // 2:(c + 1) * NB // 2], -1.0, None, ALU.mult
                                                ).then_inc(sem("self_negmax_ready"), 1)
                    if b in (NB // 2 + 1, NB - 1):
                        c = b // (NB - 1)
                        dve.wait_ge(sem("self_negmax_psum"), c + 1)
                        shift_parts(core, link, shift[:, c, :, :], ps[0:G * J * NB // 2, 6 + c, 0:S], rest[:, :]
                                    ).then_inc(sem("self_shift_ready"), 1)
                for b in range(NB):
                    dve.wait_ge(sem("self_product_done"), 2 * b + 2)
                    nc.vector.tensor_copy(core.oT[:, b, :], ps[:, ACC + b % 2, 0:G * S]
                                          ).then_inc(sem("self_oT_ready"), 1)


def finish_attention_phase(core, name):
    nc, sem, ps = core.nc, core.sem, core.ps
    gain, shift, bias = {"self": ("g1", "be1", "bv1"), "cross": ("g2", "be2", "bv2")}[name]
    with nc.Block() as block:
        @block.tensor
        def _(pe):
            for b in range(NB):
                if b >= 4:
                    pe.wait_ge(sem(name + "_normalised"), b - 3)
                for g in range(G):
                    ins = nc.tensor.transpose(ps[0:S, b % 4, 128 * g:128 * (g + 1)], core.oT[:, b, g * S:(g + 1) * S],
                                              core.ident[:, :])
                ins.then_inc(sem(name + "_o_psum"), 1)
            pe.wait_ge(sem(name + "_added"), 1)
            transpose_x(core, pe, core.xn, 6).then_inc(sem(name + "_xT_psum"), 1)

        @block.vector
        def _(dve):
            link = chain(core, dve, "vector_steps")
            for b in range(NB):
                dve.wait_ge(sem(name + "_o_psum"), b + 1)
                o = ps[0:S, b % 4, :].rearrange("s (g j e) -> s g j e", g=G, j=J)
                link(nc.vector.reciprocal(core.row_sums[:, b, :, :], o[:, :, :, E0]))
                nc.vector.tensor_tensor(core.work[:, b, :].rearrange("s (g j e) -> s g j e", g=G, j=J),
                                        o[:, :, :, 0:E0],
                                        core.row_sums[:, b, :, :].unsqueeze(3).broadcast_to([S, G, J, E0]), ALU.mult
                                        ).then_inc(sem(name + "_normalised"), 1)
            dve.wait_ge(sem(name + "_normalised"), NB)
            dve.wait_ge(sem("rows_loaded"), 16 * len(core.row))
            link(nc.vector.tensor_tensor(core.work[:, :, :], core.work[:, :, :], rows(core.row[bias]), ALU.add))
            link(nc.vector.tensor_tensor(core.work[:, :, :], core.work[:, :, :], core.xn[:, :, :], ALU.add))
            layer_norm(core, link, core.xn, core.work, core.row[gain], core.row[shift])
            dve.sem_inc(sem(name + "_added"), 1)

        @block.scalar
        def _(act):
            act.wait_ge(sem(name + "_xT_psum"), 1)
            nc.scalar.activation(core.xT[:, :].rearrange("d (c n) -> d c n", c=2), ps[:, 6:8, 0:HALF], ACT.Copy
                                 ).then_inc(sem(name + "_xT_ready"), 1)


def run_sequences(eng, emit):
    emit(0, 0, True, False)
    with eng.Fori(0, NB // 2 - 1) as i:
        for k in range(2):
            emit(2 * i + k + 1, (k + 1) % 2, False, False)
    emit(NB - 1, 1, False, True)


def wait_apart(eng, turns):
    eng.sem_inc(turns, 1)


def load_context_tiles(core, eng, b, u, loaded):
    src = core.dram["ctx_1024"][bass.ds(b, 1), :, :].rearrange("o r d -> (o r) d")
    cut = OFF[TALL]
    eng.dma_start(core.ctx[0:ROWS[0], u, 0:TALL, :], src[0:cut, :].rearrange("(t p) d -> p t d", p=ROWS[0])
                  ).then_inc(loaded, 16)
    eng.dma_start(core.ctx[0:ROWS[-1], u, TALL:TT, :], src[cut:T, :].rearrange("(t p) d -> p t d", p=ROWS[-1])
                  ).then_inc(loaded, 16)


def float16_parts(core, dve, phase, n, mx, negmax, parts, rest, whole):
    nc, steps = core.nc, core.sem(phase + "_shift_steps")
    nc.vector.tensor_reduce(negmax, mx, AX_X, ALU.max, negate=True).then_inc(steps, 1)
    dve.wait_ge(steps, 5 * n + 1)
    nc.vector.tensor_copy(parts[0], whole).then_inc(steps, 1)
    dve.wait_ge(steps, 5 * n + 2)
    nc.vector.tensor_tensor(rest, whole, parts[0], ALU.subtract).then_inc(steps, 1)
    dve.wait_ge(steps, 5 * n + 3)
    nc.vector.tensor_copy(parts[1], rest).then_inc(steps, 1)
    dve.wait_ge(steps, 5 * n + 4)
    nc.vector.tensor_tensor(rest, rest, parts[1], ALU.subtract).then_inc(steps, 1)
    dve.wait_ge(steps, 5 * n + 5)
    return nc.vector.tensor_copy(parts[2], rest)


def cross_attention_0_phase(core):
    nc, sem, ps = core.nc, core.sem, core.ps
    jobs, nj = JOBS0, len(JOBS0)
    with ExitStack() as own:
        def sb(name, shape, dt=F32):
            return core.sb(name, shape, dt, own)

        ctx = core.ctx
        ctxT = sb("x0_contextT", [D, T])
        high = sb("x0_high", [128, len(EARLY_BANKS), 512], F16)
        qst = sb("x0_queries", [128, 2, J, G * S], F16)
        kst = sb("x0_keys", [128, 2, J, T], F16)
        values = sb("x0_values", [128, 2, TT, H, 32])
        probs = sb("x0_probs", [128, RING, 2, G * S])
        mx = sb("x0_max", [S, H, NC])
        negmax = sb("x0_negmax", [S, H])
        parts = sb("x0_shift_parts", [S, G, SHIFT, J], F16)
        rest = sb("x0_shift_rest", [S, G, J])
        shift = sb("x0_shift", [G * SHIFT * J, S], F16)

        def lane(k, n, early):
            if early:
                i = k % len(EARLY_BANKS)
                return ps[:, EARLY_BANKS[i], :], high[:, i, :], sem(f"early_free{i}"), k // len(EARLY_BANKS)
            i = k % SIDES0
            return ps[:, SIDE0 + i, :], high[:, i, :], sem(f"x0_side_free{i}"), nj // SIDES0 * (n - 1) + k // SIDES0

        stacks = count(jobs, "qk")

        with nc.Block() as block:
            @block.sync
            def _(sp):
                def load_context(b, u):
                    load_context_tiles(core, sp, b, u, sem(f"x0_context_loaded{u}"))

                def shift_rows(n, u):
                    sp.wait_ge(sem("x0_shift_ready"), n + 1)
                    for g in range(G):
                        row = 32 * g + STACK
                        sp.dma_start(qst[row:row + SHIFT, u, :, g * S:(g + 1) * S],
                                     shift[SHIFT * J * g:SHIFT * J * (g + 1), :]
                                     ).then_inc(sem("x0_shift_loaded"), 16)

                shift_rows(0, 0)
                load_context(2, 0)
                shift_rows(1, 1)
                with sp.Fori(0, NB // 2 - 2) as i:
                    for k in range(2):
                        load_context(2 * i + k + 3, (k + 1) % 2)
                        shift_rows(2 * i + k + 2, k % 2)
                load_context(NB - 1, 1)
                for n in (NB - 2, NB - 1):
                    shift_rows(n, n % 2)

            @block.gpsimd
            def _(pool):
                for u in range(2):
                    pool.memset(qst[:, u, :, :], 0.0).then_inc(sem("x0_zero_queries"), 1)
                for u in range(2):
                    pool.memset(values[:, u, :, :, :], 0.0).then_inc(sem("x0_zeros_ready"), 1)
                    pool.wait_ge(sem("x0_zeros_ready"), u + 1)
                    pool.memset(values[:, u, :, :, E0:E0 + 1], 1.0).then_inc(sem("x0_ones_ready"), 1)

            @block.tensor
            def _(pe):
                pe.wait_ge(sem("self_xT_ready"), 1)
                pe.wait_ge(sem("stack_weights_ready"), 4)

                def job(k, n, u, early=False):
                    kind, a, c = jobs[k]
                    bank, _, free, turn = lane(k, n, early)
                    pe.wait_ge(free, turn + 1)
                    if kind == "q":
                        for p in range(2):
                            ins = nc.tensor.matmul(bank[:, p * S:(p + 1) * S], core.wstack["Wq2"][:, 2 * a + p, :],
                                                   core.xT[:, bass.ds(n * S, S)], start=True, stop=True)
                    elif kind == "tr":
                        if a == 0:
                            pe.wait_ge(sem(f"x0_context_loaded{u}"), 16 * (n - u) + 32)
                        for t in range(GT * a, GT * a + GT):
                            o = OFF[t] - CHUNKS[a][0]
                            ins = nc.tensor.transpose(bank[:, o:o + ROWS[t]],
                                                      ctx[0:ROWS[t], u, t, :], core.ident[0:ROWS[t], 0:ROWS[t]])
                    elif kind == "k":
                        if a == 0 and c == 0:
                            pe.wait_ge(sem("x0_contextT_ready"), NG * (n + 1))
                        o, w = CHUNKS[a]
                        ins = nc.tensor.matmul(bank[:, 0:w], core.wstack["Wk2"][:, c, :], ctxT[:, o:o + w],
                                               start=True, stop=True)
                    elif kind == "v":
                        for t in range(GT * a, GT * a + GT):
                            ins = nc.tensor.matmul(bank[0:ROWS[t], D * (t % GT):D * (t % GT + 1)],
                                                   ctxT[:, OFF[t]:OFF[t] + ROWS[t]],
                                                   core.wraw["Wv2"][:, :, :].rearrange("d h e -> d (h e)"),
                                                   start=True, stop=True)
                    elif kind == "n":
                        if a == 0:
                            pe.wait_ge(sem("x0_stack_ready"), stacks * n + 2 + J * (c + 1))
                        g, j, (o, w) = a // J, a % J, CHUNKS[c]
                        ins = nc.tensor.matmul(bank[0:S, 0:w], qst[32 * g:32 * g + STACK, u, j, g * S:(g + 1) * S],
                                               kst[32 * g:32 * g + STACK, u, j, o:o + w], start=True, stop=True)
                    elif kind == "m":
                        pe.wait_ge(sem("x0_parts_ready"), n + 1)
                        ins = nc.tensor.matmul(bank[0:G * SHIFT * J, 0:S],
                                               parts[:, :, :, :].rearrange("s g r j -> s (g r j)"),
                                               core.ident4[:, 0, :], start=True, stop=True)
                    ins.then_inc(sem("x0_side_ready"), 1)

                for k in range(nj):
                    job(k, 0, 0, early=True)

                def values_product(b, u, v, j):
                    t = v // 2
                    if v == 0 and j == 0:
                        pe.wait_ge(sem("x0_values_ready"), NG * (b + 1))
                        pe.wait_ge(sem("x0_oT_ready"), b + 1)
                    if j % 2 == 0:
                        pe.wait_ge(sem("x0_probs_ready"), STEPS * b + v + 1 + 2)
                    for g in range(G):
                        ins = nc.tensor.matmul(
                            ps[32 * g:32 * g + 32, ACC, j * S:(j + 1) * S], values[0:ROWS[t], u, t, G * j + g, :],
                            probs[0:ROWS[t], v % RING, j % 2, g * S:(g + 1) * S],
                            start=(t == 0 and j == 0), stop=(t == TT - 1), skip_group_check=True)
                    if j % 2:
                        ins.then_inc(sem("x0_product_done"), 1)

                def sequence(b, u, first, last):
                    for s in range(STEPS + (LAG if last else 0)):
                        if s < STEPS:
                            t, half = s // 2, s % 2
                            if s == 0:
                                pe.wait_ge(sem("x0_shift_loaded"), 16 * G * (b + 1))
                            pe.wait_ge(sem("x0_probs_ready"), STEPS * b + s + 1)
                            for j in (2 * half, 2 * half + 1):
                                ins = nc.tensor.matmul(ps[0:ROWS[t], j, 0:G * S],
                                                       kst[:, u, j, OFF[t]:OFF[t] + ROWS[t]], qst[:, u, j, :],
                                                       start=True, stop=True)
                            ins.then_inc(sem("x0_scores_ready"), 1)
                        mine = [] if last else AT_STEP0[s]
                        v = s - LAG
                        for part in range(3):
                            for k in share(mine, part, 3):
                                job(k, b + 1, 1 - u)
                            if part < 2 and v >= 0:
                                values_product(b, u, v, 2 * (v % 2) + part)
                            elif part < 2 and not first:
                                values_product(b - 1, 1 - u, v + STEPS, 2 * (v % 2) + part)

                run_sequences(pe, sequence)

            @block.scalar
            def _(act):
                act.sem_inc(sem("x0_probs_ready"), 2)
                act.sem_inc(sem("x0_oT_ready"), 1)

                def job(k, n, u, early=False):
                    kind, a, c = jobs[k]
                    if kind in ("n", "m"):
                        return
                    act.wait_ge(sem("x0_side_ready"), nj * n + k + 1)
                    bank, high_k, free, _ = lane(k, n, early)
                    if kind == "q":
                        nc.scalar.activation(high_k[:, 0:2 * S], bank[:, 0:2 * S], ACT.Identity
                                             ).then_inc(sem("x0_high_ready"), 1)
                    elif kind == "k":
                        w = CHUNKS[a][1]
                        nc.scalar.activation(high_k[:, 0:w], bank[:, 0:w], ACT.Identity,
                                             bias=core.ones_k[:, 0:1]).then_inc(sem("x0_high_ready"), 1)
                    elif kind == "tr":
                        o, w = CHUNKS[a]
                        nc.scalar.activation(ctxT[:, o:o + w], bank[:, 0:w], ACT.Copy
                                             ).then_inc(sem("x0_contextT_ready"), 1)
                        act.wait_ge(sem("x0_contextT_ready"), NG * n + a + 1)
                        act.sem_inc(free, 1)
                    elif kind == "v":
                        if a == 0:
                            act.wait_ge(sem("x0_ones_ready"), 1 if early else 2)
                        r = ROWS[GT * a]
                        nc.scalar.activation(values[0:r, u, GT * a:GT * a + GT, :, 0:E0],
                                             bank[0:r, 0:GT * D].rearrange("p (t h e) -> p t h e", t=GT, h=H), ACT.Copy
                                             ).then_inc(sem("x0_values_ready"), 1)
                        act.wait_ge(sem("x0_values_ready"), NG * n + a + 1)
                        act.sem_inc(free, 1)

                def store_oT(b):
                    act.wait_ge(sem("x0_product_done"), STEPS * (b + 1) + RING)
                    nc.scalar.activation(core.oT[:, bass.ds(b, 1), :], ps[:, ACC, 0:J * S].unsqueeze(1), ACT.Copy
                                         ).then_inc(sem("x0_oT_ready"), 1)

                for k in range(nj):
                    job(k, 0, 0, early=True)

                def sequence(b, u, first, last):
                    for s in range(STEPS):
                        if s == LAG and not first:
                            store_oT(b - 1)
                        if s < STEPS:
                            t, half = s // 2, s % 2
                            act.wait_ge(sem("x0_scores_ready"), STEPS * b + s + 1)
                            act.wait_ge(sem("x0_product_done"), STEPS * b + s + 1)
                            nc.scalar.activation(probs[0:ROWS[t], s % RING, :, :],
                                                 ps[0:ROWS[t], 2 * half:2 * half + 2, 0:G * S], ACT.Exp,
                                                 scale=SCALE0).then_inc(sem("x0_probs_ready"), 1)
                        if not last:
                            for k in AT_STEP0[s]:
                                job(k, b + 1, 1 - u)
                    if last:
                        store_oT(b)

                run_sequences(act, sequence)

            @block.vector
            def _(dve):
                dve.sem_inc(sem("x0_product_done"), RING)
                for k in range(SIDES0):
                    dve.sem_inc(sem(f"x0_side_free{k}"), 1)
                for k in range(len(EARLY_BANKS)):
                    dve.sem_inc(sem(f"early_free{k}"), 1)
                last_n = max(k for k in range(nj) if jobs[k][0] == "n")

                def job(k, n, u, early=False):
                    kind, a, c = jobs[k]
                    if kind in ("tr", "v"):
                        return
                    bank, high_k, free, turn = lane(k, n, early)
                    dve.wait_ge(sem("x0_side_ready"), nj * n + k + 1)
                    if kind in ("q", "k"):
                        dve.wait_ge(sem("x0_high_ready"), stacks * n + count(jobs, "qk", k) + 1)
                        if kind == "q":
                            if k == 0:
                                dve.wait_ge(sem("x0_zero_queries"), 1 if early else 2)
                            for g in range(G):
                                rows_g = slice(32 * g, 32 * g + 32)
                                ins = split_stack(
                                    core, dve, qst[rows_g, u, 2 * a:2 * a + 2, g * S:(g + 1) * S],
                                    halves(bank[rows_g, 0:2 * S], S), halves(high_k[rows_g, 0:2 * S], S),
                                    core.signs_q[rows_g, 0:1])
                        else:
                            o, w = CHUNKS[a]
                            ins = split_stack(core, dve, kst[:, u, c, o:o + w], bank[:, 0:w],
                                              high_k[:, 0:w], core.signs_k[:, 0:1])
                        ins.then_inc(sem("x0_stack_ready"), 1)
                        dve.wait_ge(sem("x0_stack_ready"), stacks * n + count(jobs, "qk", k) + 1)
                        dve.sem_inc(free, 1)
                    elif kind == "n":
                        w = CHUNKS[c][1]
                        nc.vector.tensor_reduce(mx[:, a, c:c + 1], bank[0:S, 0:w], AX_X, ALU.max).then_inc(free, 1)
                        if k == last_n:
                            dve.wait_ge(free, turn + 2)
                            float16_parts(core, dve, "x0", n, mx[:, :, :], negmax[:, :],
                                          [parts[:, :, r, :] for r in range(SHIFT)], rest[:, :, :],
                                          negmax[:, :].rearrange("s (g j) -> s g j", g=G)
                                          ).then_inc(sem("x0_parts_ready"), 1)
                    elif kind == "m":
                        if not isinstance(n, int) or n:
                            dve.wait_ge(sem("x0_shift_loaded"), 16 * G * n)
                        nc.vector.tensor_copy(shift[:, :], bank[0:G * SHIFT * J, 0:S]
                                              ).then_inc(sem("x0_shift_ready"), 1)
                        dve.wait_ge(sem("x0_shift_ready"), n + 1)
                        dve.sem_inc(free, 1)

                for k in range(nj):
                    job(k, 0, 0, early=True)

                def sequence(b, u, first, last):
                    if not last:
                        for k in range(nj):
                            job(k, b + 1, 1 - u)

                run_sequences(dve, sequence)


def hidden_layer(core, pe, up, hidden_free, hidden_psum, base):
    nc, ps = core.nc, core.ps
    for f in range(FT):
        pe.wait_ge(hidden_free, base + f + 1)
        for c in range(2):
            ins = nc.tensor.matmul(ps[:, 2 * (f % 2) + c, 0:HALF], up[:, D * f:D * f + D],
                                   core.xT[:, c * HALF:(c + 1) * HALF], start=True, stop=True)
        ins.then_inc(hidden_psum, 1)


def output_layer(core, pe, down, hidden, bank):
    nc, ps = core.nc, core.ps
    for b in range(NB):
        for f in range(FT):
            ins = nc.tensor.matmul(ps[0:S, bank + b // 4, D * (b % 4):D * (b % 4 + 1)],
                                   hidden[:, f, b * S:(b + 1) * S], down[:, f, :], start=(f == 0), stop=(f == FT - 1))
    return ins


def halves(ap, w):
    return ap.rearrange("p (c n) -> p c n", n=w)


def token_banks(core, bank):
    return core.ps[0:S, bank:bank + 2, :].rearrange("s c (b d) -> s (c b) d", d=D)


def add_gated(core, link, gate, what):
    link(core.nc.vector.scalar_tensor_tensor(
        out=flat(core.x), in0=flat(what), scalar=core.gates[0:S, gate:gate + 1], in1=flat(core.x),
        op0=ALU.mult, op1=ALU.add))


def flat(t):
    return t[:, :, :].rearrange("s b d -> s (b d)")


def load_layer1_start(core, eng):
    load_context_tiles(core, eng, 0, 0, core.sem("x1_context_loaded"))
    load_mask(core, eng, 0, 0)


def load_mask(core, eng, b, u):
    eng.dma_start(core.mask_raw[:, u, :],
                  core.dram["mask_BxSxS2_bf1"][bass.ds(b, 1), :, :].rearrange("o s t -> (o s) t")
                  ).then_inc(core.sem("x1_mask_loaded"), 16)


def merged_weights(core, name):
    return {"ffn": (core.merged_qk, ("Wq", "Wk")), "expert0": (core.merged_vo, ("Wv",))}[name]


def feed_forward_phase(core, name, bias, gain, shift, gate):
    nc, sem, ps = core.nc, core.sem, core.ps
    up, up_bias, down = core.dense[name]
    merged, factors = merged_weights(core, name)
    with ExitStack() as own, nc.Block() as block:
        hidden = core.sb(f"{name}_hidden", [D, FT, NTOK], F32, own)
        raw = [core.sb(f"raw1_{n}", [D, H, E1], F32, own) for n in factors]
        turned = [core.sb(f"turned_{n}", [2 * E1, H // 2, D], F32, own) for n in factors]
        if name == "expert0":
            turned.append(core.sb("Wo", [2 * E1, H // 2, D], F32, own))

        @block.sync
        def _(sp):
            for k, n in enumerate(factors):
                sp.dma_start(raw[k][:, :, :], core.dram[f"L1_xattn_{n}"].rearrange("h d e -> d h e")
                             ).then_inc(sem(f"{n}_loaded"), 16)
            if name == "ffn":
                load_layer1_start(core, sp)
            else:
                sp.dma_start(turned[1][:, :, :], core.dram["L1_xattn_Wo"].rearrange("(a p) o -> p a o", p=2 * E1)
                             ).then_inc(sem("Wo_loaded"), 16)

        @block.gpsimd
        def _(pool):
            if name == "ffn":
                pool.memset(core.ones[:, :], 1.0)
                pool.memset(core.boost[:, :], log(BOOST))
                pool.memset(core.masked[:, :, :], 1.0).then_inc(sem("x1_ones_ready"), 1)
                for u in range(2):
                    ins = pool.tensor_copy(core.select[0:S, u, :, :], core.ident4[:, 0:1, :].broadcast_to([S, H, S]))
                ins.then_inc(sem("x1_select_ready"), 1)

        @block.tensor
        def _(pe):
            pe.wait_ge(sem(f"{name}_loaded"), 48)
            hidden_layer(core, pe, up, sem(f"{name}_hidden_free"), sem(f"{name}_hidden_psum"), 0)
            pe.wait_ge(sem(f"{name}_hidden_free"), 2 + FT)
            output_layer(core, pe, down, hidden, 4).then_inc(sem(f"{name}_out_psum"), 1)
            for k, n in enumerate(factors):
                pe.wait_ge(sem(f"{n}_loaded"), 16)
                for a in range(H // 2):
                    ins = nc.tensor.transpose(ps[:, 2 * k + a // 4, D * (a % 4):D * (a % 4 + 1)],
                                              raw[k][:, 2 * a:2 * a + 2, :].rearrange("d h e -> d (h e)"),
                                              core.ident[:, :])
                ins.then_inc(sem(f"{name}_turned_psum"), 1)
            if name == "expert0":
                pe.wait_ge(sem("Wo_loaded"), 16)
            pe.wait_ge(sem(f"{name}_turned_ready"), len(factors))
            for q in range(2):
                for h in range(8 * q, 8 * q + 8):
                    p, a = E1 * (h % 2), h // 2
                    ins = nc.tensor.matmul(ps[:, 2 * q + h % 2, D * (a % 4):D * (a % 4 + 1)],
                                           turned[0][p:p + E1, a, :], turned[1][p:p + E1, a, :], start=True, stop=True)
                ins.then_inc(sem(f"{name}_merged_psum"), 1)
            pe.wait_ge(sem(f"{name}_added"), 1)
            transpose_x(core, pe, core.xn, 6).then_inc(sem(f"{name}_xT_psum"), 1)

        @block.scalar
        def _(act):
            act.sem_inc(sem(f"{name}_hidden_free"), 2)
            for f in range(FT):
                act.wait_ge(sem(f"{name}_hidden_psum"), f + 1)
                nc.scalar.activation(halves(hidden[:, f, :], HALF), ps[:, 2 * (f % 2):2 * (f % 2) + 2, 0:HALF], ACT.Relu,
                                     bias=up_bias[:, f:f + 1]).then_inc(sem(f"{name}_hidden_free"), 1)
            for k in range(len(factors)):
                act.wait_ge(sem(f"{name}_turned_psum"), k + 1)
                nc.scalar.activation(turned[k][:, :, :].rearrange("p (c a) d -> p c (a d)", c=2),
                                     ps[:, 2 * k:2 * k + 2, :], ACT.Copy).then_inc(sem(f"{name}_turned_ready"), 1)
            for q in range(2):
                act.wait_ge(sem(f"{name}_merged_psum"), q + 1)
                heads = merged[:, 8 * q:8 * q + 8, :].rearrange("d (a r) o -> d r a o", r=2)
                for r in range(2):
                    ins = nc.scalar.activation(heads[:, r, :, :], ps[:, 2 * q + r, :].rearrange("d (a o) -> d a o", a=4),
                                               ACT.Copy)
                ins.then_inc(sem(f"{name}_merged_ready"), 1)
            act.wait_ge(sem(f"{name}_xT_psum"), 1)
            nc.scalar.activation(halves(core.xT[:, :], HALF), ps[:, 6:8, 0:HALF], ACT.Copy
                                 ).then_inc(sem(f"{name}_xT_ready"), 1)

        @block.vector
        def _(dve):
            link = chain(core, dve, "vector_steps")
            dve.wait_ge(sem(f"{name}_out_psum"), 1)
            dve.wait_ge(sem("expert_rows_loaded"), 48)
            link(nc.vector.tensor_tensor(core.work[:, :, :], token_banks(core, 4), rows(bias), ALU.add))
            link(nc.vector.tensor_tensor(core.work[:, :, :], core.work[:, :, :], core.xn[:, :, :], ALU.add))
            layer_norm(core, link, core.xn, core.work, gain, shift)
            dve.wait_ge(sem("gates_ready"), 1)
            add_gated(core, link, gate, core.xn)
            layer_norm(core, link, core.xn, core.x)
            dve.sem_inc(sem(f"{name}_added"), 1)


def side_order_1(first, last):
    order = []
    for s in range(STEPS):
        if s == LAG + 1 and not first:
            order += [(s, -1, "sum", 1, 0), (s, -1, "sum", 1, 1)]
        if s == TT + LAG + 1:
            order += [(s, 0, "sum", 0, 0), (s, 0, "sum", 0, 1)]
        if not last:
            order += [(s, 1, *JOBS1[k]) for k in AT_STEP1[s]]
    return order + [(STEPS + LAG, 0, "sum", 1, 0), (STEPS + LAG, 0, "sum", 1, 1)] * last


def cross_attention_1_phase(core):
    nc, sem, ps = core.nc, core.sem, core.ps
    jobs, nj = JOBS1, len(JOBS1)
    with ExitStack() as own:
        def sb(name, shape, dt=F32):
            return core.sb(name, shape, dt, own)

        ctx = core.ctx
        chigh = sb("x1_context_high", [D, 2, T], F16)
        clow = sb("x1_context_low", [D, 2, T], F16)
        qhigh = sb("x1_queries_high", [D, 2, H * S], F16)
        qlow = sb("x1_queries_low", [D, 2, H * S], F16)
        mask_raw, masked, select, ones, boost = core.mask_raw, core.masked, core.select, core.ones, core.boost
        vhigh = sb("x1_values_high", [128, 2, TT, D], F16)
        vlow = sb("x1_values_low", [128, 2, TT, D], F16)
        probs = sb("x1_probs", [128, RING, UNIT * S])
        phigh = sb("x1_probs_high", [128, HALF_RING, UNIT * S], F16)
        plow = sb("x1_probs_low", [128, HALF_RING, UNIT * S], F16)
        sums = sb("x1_sums", [128, 2, UNIT * S])
        junk = sb("x1_junk", [S, 2, 512], F16)
        mx = sb("x1_max", [S, H, NC])
        negmax = sb("x1_negmax", [S, H])
        parts = sb("x1_shift_parts", [S, SHIFT, H], F16)
        rest = sb("x1_shift_rest", [S, H])
        shift = sb("x1_shift", [SHIFT * H, S], F16)
        averages = core.averages
        splits = count(jobs, ("q", "tr"))

        def base(b, first, sides=1):
            return (nj if first else nj + nj + 2 + (nj + 4) * (b - 1)) if sides == 1 else (
                0 if first else nj // 2 + 1 + (nj + 4) // 2 * (b - 1))

        def lane(p, had):
            if had is None:
                k = p % len(EARLY_BANKS)
                in_layer_0 = len(range(k, len(JOBS0), len(EARLY_BANKS)))
                return ps[:, EARLY_BANKS[k], :], sem(f"early_free{k}"), in_layer_0 + p // len(EARLY_BANKS)
            return ps[:, SIDE1 + p % SIDES1, :], sem(f"x1_side_free{p % SIDES1}"), had + p // SIDES1

        with nc.Block() as block:
            @block.sync
            def _(sp):
                def load(b, u):
                    load_context_tiles(core, sp, b, u, sem("x1_context_loaded"))
                    load_mask(core, sp, b, u)

                def shift_rows(n, u):
                    sp.wait_ge(sem("x1_shift_ready"), n + 1)
                    sp.dma_start(select[S:S + SHIFT, u, :, :].rearrange("r h s -> r (h s)"), shift[:, :]
                                 ).then_inc(sem("x1_shift_loaded"), 16)

                sp.wait_ge(sem("x1_select_ready"), 1)
                shift_rows(0, 0)

                def sequence(b, u, first, last):
                    if not last:
                        sp.wait_ge(sem("x1_product_done"), STEPS * b + RING)
                        load(b + 1, 1 - u)
                        shift_rows(b + 1, 1 - u)

                run_sequences(sp, sequence)

            @block.gpsimd
            def _(pool):
                pool.sem_inc(sem("x1_sums_used"), 2)
                pool.wait_ge(sem("x1_ones_ready"), 1)

                def additive_mask(n, u):
                    pool.wait_ge(sem("x1_mask_loaded"), 16 * (n + 1))
                    wait_apart(pool, sem("pool_waits"))
                    pool.tensor_scalar(masked[0:S, u, :], mask_raw[:, u, :], -MASKED, MASKED, ALU.mult, ALU.add
                                       ).then_inc(sem("x1_mask_ready"), 1)

                additive_mask(0, 0)

                def sequence(b, u, first, last):
                    for s in range(STEPS):
                        unit, t = s // TT, s % TT
                        if s == 1 and not last:
                            additive_mask(b + 1, 1 - u)
                        pool.wait_ge(sem("x1_probs_ready"), STEPS * b + s + 1 + 2)
                        dst, src = sums[0:ROWS[t], unit, :], probs[0:ROWS[t], s % RING, :]
                        if t == 0:
                            pool.wait_ge(sem("x1_sums_used"), 2 * b + unit + 1)
                            wait_apart(pool, sem("pool_waits"))
                            ins = pool.tensor_copy(dst, src)
                        else:
                            pool.wait_ge(sem("x1_sums_done"), STEPS * b + s + RING)
                            ins = pool.tensor_tensor(dst, dst, src, ALU.add)
                        ins.then_inc(sem("x1_sums_done"), 1)

                run_sequences(pool, sequence)

            @block.tensor
            def _(pe):
                def job(kind, a, c, p, n, u, before, half_before):
                    bank, free, turn = lane(p, half_before)
                    pe.wait_ge(free, turn + 1)
                    if kind == "q":
                        for h in range(HC * a, HC * a + HC):
                            ins = nc.tensor.matmul(bank[:, (h % HC) * S:(h % HC + 1) * S], core.merged_qk[:, h, :],
                                                   core.xT[:, bass.ds(n * S, S)], start=True, stop=True)
                    elif kind == "tr":
                        if a == 0:
                            pe.wait_ge(sem("x1_context_loaded"), 32 * n + 32)
                        for t in range(GT * a, GT * a + GT):
                            o = OFF[t] - CHUNKS[a][0]
                            ins = nc.tensor.transpose(bank[:, o:o + ROWS[t]], ctx[0:ROWS[t], u, t, :],
                                                      core.ident[0:ROWS[t], 0:ROWS[t]])
                    elif kind == "n":
                        if a == 0 and c == 0:
                            pe.wait_ge(sem("x1_high_ready"), splits * (n + 1))
                        o, w = CHUNKS[c]
                        ins = nc.tensor.matmul(bank[0:S, 0:w], qhigh[:, u, a * S:(a + 1) * S], chigh[:, u, o:o + w],
                                               start=True, stop=True)
                    elif kind == "m":
                        pe.wait_ge(sem("x1_parts_ready"), n + 1)
                        ins = nc.tensor.matmul(bank[0:SHIFT * H, 0:S], parts[:, :, :].rearrange("s r h -> s (r h)"),
                                               core.ident4[:, 0, :], start=True, stop=True)
                    else:
                        if c == 0:
                            pe.wait_ge(sem("x1_sums_done"), STEPS * n + TT * (a + 1) + RING)
                        for h in range(HC * c, HC * c + HC):
                            ins = nc.tensor.matmul(bank[0:S, h % HC:h % HC + 1], sums[0:ROWS[0], a, h * S:(h + 1) * S],
                                                   ones[0:ROWS[0], :], start=True, stop=True)
                    ins.then_inc(sem("x1_side_ready"), 1)

                pe.wait_ge(sem("x1_ones_ready"), 1)
                pe.wait_ge(sem("x1_select_ready"), 1)
                for k in range(nj):
                    job(*jobs[k], k, 0, 0, 0, None)

                def values_product(b, u, v, c):
                    unit, t = v // TT, v % TT
                    if t == 0:
                        pe.wait_ge(sem("x1_averages_ready"), 4 * b + 2 * unit + 1 + c)
                    if c == 0 and v == 0:
                        pe.wait_ge(sem("x1_values_split"), b + 1)
                    if c == 0:
                        pe.wait_ge(sem("x1_probs_low_ready"), STEPS * b + v + 1)
                    for k, (left, right) in enumerate(((vhigh, phigh), (vhigh, plow), (vlow, phigh))):
                        ins = nc.tensor.matmul(ps[:, ACC + c, 0:HALF], left[0:ROWS[t], u, t, :],
                                               right[0:ROWS[t], v % HALF_RING, c * HALF:(c + 1) * HALF],
                                               start=(t == 0 and k == 0), stop=(t == TT - 1 and k == 2))
                    if c == 1:
                        ins.then_inc(sem("x1_product_done"), 1)

                def sequence(b, u, first, last):
                    order = side_order_1(first, last)
                    for s in range(STEPS + (LAG + 1 if last else 0)):
                        mine = [(p, o) for p, o in enumerate(order) if o[0] == s]
                        for p, (_, ahead, kind, a, c) in mine:
                            if kind == "sum":
                                job(kind, a, c, p, b + ahead, u, None, base(b, first, 2))
                        if s < STEPS:
                            unit, t = s // TT, s % TT
                            if s == 0:
                                pe.wait_ge(sem("x1_shift_loaded"), 16 * (b + 1))
                                pe.wait_ge(sem("x1_low_ready"), splits * (b + 1))
                                pe.wait_ge(sem("x1_mask_ready"), b + 1)
                            pe.wait_ge(sem("x1_probs_ready"), STEPS * b + s + 1)
                            r, o = ROWS[t], OFF[t]
                            for k, (left, right) in enumerate(((chigh, qhigh), (chigh, qlow), (clow, qhigh))):
                                for c in range(2):
                                    q0 = (UNIT * unit + HC * c) * S
                                    nc.tensor.matmul(ps[0:r, 2 * (s % 2) + c, 0:HALF], left[:, u, o:o + r],
                                                     right[:, u, q0:q0 + HALF], start=(k == 0), stop=False)
                            for c in range(2):
                                h0 = UNIT * unit + HC * c
                                ins = nc.tensor.matmul(ps[0:r, 2 * (s % 2) + c, 0:HALF], masked[:, u, o:o + r],
                                                       select[:, u, h0:h0 + HC, :].rearrange("p h s -> p (h s)"),
                                                       start=False, stop=True)
                            ins.then_inc(sem("x1_scores_ready"), 1)
                        side = [o for o in mine if o[1][2] != "sum"]
                        v = s - LAG
                        for part in range(3):
                            for p, (_, ahead, kind, a, c) in share(side, part, 3):
                                job(kind, a, c, p, b + 1, 1 - u, None, base(b, first, 2))
                            if part < 2 and 0 <= v < STEPS:
                                values_product(b, u, v, part)
                            elif part < 2 and v < 0 and not first:
                                values_product(b - 1, 1 - u, v + STEPS, part)

                run_sequences(pe, sequence)

            @block.scalar
            def _(act):
                act.sem_inc(sem("x1_probs_ready"), 2)
                act.sem_inc(sem("x1_averages_ready"), 2)

                def job(kind, a, c, p, n, u, before, half_before):
                    if kind not in ("q", "tr"):
                        return
                    act.wait_ge(sem("x1_side_ready"), before + p + 1)
                    bank, _, _ = lane(p, half_before)
                    if (kind, a) == ("tr", 0):
                        for tiles in (slice(0, TALL), slice(TALL, TT)):
                            r = ROWS[tiles.start]
                            ins = nc.scalar.activation(vhigh[0:r, u, tiles, :], ctx[0:r, u, tiles, :], ACT.Copy)
                        ins.then_inc(sem("x1_values_high_ready"), 1)
                    if kind == "q":
                        dst, w = qhigh[:, u, HALF * a:HALF * (a + 1)], HALF
                    else:
                        o, w = CHUNKS[a]
                        dst = chigh[:, u, o:o + w]
                    nc.scalar.activation(dst, bank[:, 0:w], ACT.Copy).then_inc(sem("x1_high_ready"), 1)

                for k in range(nj):
                    job(*jobs[k], k, 0, 0, 0, None)

                def store_averages(b, unit):
                    for c in range(2):
                        h0 = (UNIT * unit + HC * c) * S
                        act.wait_ge(sem("x1_product_done"), STEPS * b + TT * (unit + 1) + RING)
                        nc.scalar.activation(averages[:, bass.ds(b, 1), h0:h0 + HALF],
                                             ps[:, ACC + c, 0:HALF].unsqueeze(1), ACT.Copy
                                             ).then_inc(sem("x1_averages_ready"), 1)

                def sequence(b, u, first, last):
                    order = side_order_1(first, last)
                    for s in range(STEPS + (LAG if last else 0)):
                        if s == LAG and not first:
                            store_averages(b - 1, 1)
                        if s == TT + LAG:
                            store_averages(b, 0)
                        if s < STEPS:
                            r = ROWS[s % TT]
                            act.wait_ge(sem("x1_scores_ready"), STEPS * b + s + 1)
                            act.wait_ge(sem("x1_product_done"), STEPS * b + s + 1)
                            act.wait_ge(sem("x1_sums_done"), STEPS * b + s + 1)
                            nc.scalar.activation(halves(probs[0:r, s % RING, :], HALF),
                                                 ps[0:r, 2 * (s % 2):2 * (s % 2) + 2, 0:HALF], ACT.Exp,
                                                 bias=boost[0:r, 0:1], scale=SCALE1
                                                 ).then_inc(sem("x1_probs_ready"), 1)
                            act.wait_ge(sem("x1_probs_ready"), STEPS * b + s + 1 + 2)
                            act.wait_ge(sem("x1_product_done"), STEPS * b + s + 1 + RING - HALF_RING)
                            nc.scalar.activation(phigh[0:r, s % HALF_RING, :], probs[0:r, s % RING, :], ACT.Copy
                                                 ).then_inc(sem("x1_probs_high_ready"), 1)
                        for p, (at, ahead, kind, a, c) in enumerate(order):
                            if at == s:
                                job(kind, a, c, p, b + 1, 1 - u, base(b, first), base(b, first, 2))
                    if last:
                        store_averages(b, 1)

                run_sequences(act, sequence)

            @block.vector
            def _(dve):
                dve.sem_inc(sem("x1_product_done"), RING)
                dve.sem_inc(sem("x1_sums_done"), RING)
                for k in range(SIDES1):
                    dve.sem_inc(sem(f"x1_side_free{k}"), 1)
                last_n = [j for j in jobs if j[0] == "n"][-1]

                def job(kind, a, c, p, n, u, before, half_before, splits_before):
                    bank, free, turn = lane(p, half_before)
                    dve.wait_ge(sem("x1_side_ready"), before + p + 1)
                    if (kind, a) == ("tr", 0):
                        dve.wait_ge(sem("x1_values_high_ready"), n + 1)
                        for tiles in (slice(0, TALL), slice(TALL, TT)):
                            r = ROWS[tiles.start]
                            ins = nc.vector.tensor_tensor(vlow[0:r, u, tiles, :], ctx[0:r, u, tiles, :],
                                                          vhigh[0:r, u, tiles, :], ALU.subtract)
                        ins.then_inc(sem("x1_values_split"), 1)
                    if kind in ("q", "tr"):
                        dve.wait_ge(sem("x1_high_ready"), splits * n + splits_before + 1)
                        if kind == "q":
                            high, low, w = qhigh, qlow, HALF
                            o = HALF * a
                        else:
                            high, low, (o, w) = chigh, clow, CHUNKS[a]
                        nc.vector.tensor_tensor(low[:, u, o:o + w], bank[:, 0:w], high[:, u, o:o + w], ALU.subtract
                                                ).then_inc(sem("x1_low_ready"), 1)
                        dve.wait_ge(sem("x1_low_ready"), splits * n + splits_before + 1)
                        dve.sem_inc(free, 1)
                    elif kind == "n":
                        o, w = CHUNKS[c]
                        if a == 0 and c == 0:
                            dve.wait_ge(sem("x1_mask_ready"), n + 1)
                        if half_before is None:
                            _, free_before, turn_before = lane(p - 2, None)
                            dve.wait_ge(free_before, turn_before + 2)
                        wait_apart(dve, sem("vector_waits"))
                        nc.vector.tensor_tensor_reduce(junk[:, p % 2, 0:w], bank[0:S, 0:w], masked[0:S, u, o:o + w],
                                                       1.0, -3.0e38, ALU.add, ALU.max, mx[:, a, c:c + 1]
                                                       ).then_inc(free, 1)
                        if (kind, a, c) == last_n:
                            dve.wait_ge(free, turn + 2)
                            float16_parts(core, dve, "x1", n, mx[:, :, :], negmax[:, :],
                                          [parts[:, r, :] for r in range(SHIFT)], rest[:, :], negmax[:, :]
                                          ).then_inc(sem("x1_parts_ready"), 1)
                    elif kind == "m":
                        if not isinstance(n, int) or n:
                            dve.wait_ge(sem("x1_shift_loaded"), 16 * n)
                        nc.vector.tensor_copy(shift[:, :], bank[0:SHIFT * H, 0:S]
                                              ).then_inc(sem("x1_shift_ready"), 1)
                        dve.wait_ge(sem("x1_shift_ready"), n + 1)
                        dve.sem_inc(free, 1)
                    else:
                        h0 = UNIT * a + HC * c
                        nc.vector.reciprocal(core.inverse[:, bass.ds(n, 1), h0:h0 + HC], bank[0:S, 0:HC].unsqueeze(1)
                                             ).then_inc(free, 1)
                        if c == 1:
                            dve.sem_inc(sem("x1_sums_used"), 1)

                for k in range(nj):
                    job(*jobs[k], k, 0, 0, 0, None, count(jobs, ("q", "tr"), k))

                def low_probs(b, s):
                    r = ROWS[s % TT]
                    dve.wait_ge(sem("x1_probs_high_ready"), STEPS * b + s + 1)
                    nc.vector.tensor_tensor(plow[0:r, s % HALF_RING, :], probs[0:r, s % RING, :],
                                            phigh[0:r, s % HALF_RING, :],
                                            ALU.subtract).then_inc(sem("x1_probs_low_ready"), 1)

                def sequence(b, u, first, last):
                    order, seen = side_order_1(first, last), 0
                    for s in range(STEPS + (LAG + 1 if last else 0)):
                        if 1 <= s <= STEPS:
                            low_probs(b, s - 1)
                        elif s == 0 and not first:
                            low_probs(b - 1, STEPS - 1)
                        for p, (at, ahead, kind, a, c) in enumerate(order):
                            if at == s:
                                job(kind, a, c, p, b + ahead, 1 - u, base(b, first), base(b, first, 2), seen)
                                seen += kind in ("q", "tr")

                run_sequences(dve, sequence)


def project_tensor(core, pe):
    nc, sem, ps = core.nc, core.sem, core.ps
    for h in range(H):
        for c in range(2):
            i = 2 * h + c
            if i >= 8:
                pe.wait_ge(sem("projected_summed"), i - 7)
            for b in range(4 * c, 4 * c + 4):
                ins = nc.tensor.matmul(ps[0:S, i % 8, D * (b % 4):D * (b % 4 + 1)],
                                       core.averages[:, b, h * S:(h + 1) * S], core.merged_vo[:, h, :],
                                       start=True, stop=True)
            ins.then_inc(sem("projected_psum"), 1)
    pe.wait_ge(sem("projected_added"), 1)
    transpose_x(core, pe, core.xn, 6).then_inc(sem("projected_xT_psum"), 1)
    pe.wait_ge(sem("projected_xT_ready"), 1)


def project_scalar(core, act):
    nc, sem, ps = core.nc, core.sem, core.ps
    act.wait_ge(sem("projected_xT_psum"), 1)
    nc.scalar.activation(halves(core.xT[:, :], HALF), ps[:, 6:8, 0:HALF], ACT.Copy
                         ).then_inc(sem("projected_xT_ready"), 1)
    act.wait_ge(sem("projected_xT_ready"), 1)


def project_vector(core, dve):
    nc, sem, ps = core.nc, core.sem, core.ps
    link = chain(core, dve, "vector_steps")
    for h in range(H):
        for c in range(2):
            i = 2 * h + c
            dve.wait_ge(sem("projected_psum"), i + 1)
            if h:
                dve.wait_ge(sem("projected_summed"), i - 1)
            for b in range(4 * c, 4 * c + 4):
                product = ps[0:S, i % 8, D * (b % 4):D * (b % 4 + 1)]
                inverse = core.inverse[:, b, h:h + 1]
                if h == 0:
                    ins = nc.vector.tensor_scalar(core.work[:, b, :], product, inverse, None, ALU.mult)
                else:
                    ins = nc.vector.scalar_tensor_tensor(out=core.work[:, b, :], in0=product, scalar=inverse,
                                                         in1=core.work[:, b, :], op0=ALU.mult, op1=ALU.add)
            ins.then_inc(sem("projected_summed"), 1)
    dve.wait_ge(sem("projected_summed"), 2 * H)
    add_gated(core, link, 1, core.work)
    layer_norm(core, link, core.xn, core.x)
    dve.sem_inc(sem("projected_added"), 1)


def experts_phase(core):
    nc, sem, ps, dram = core.nc, core.sem, core.ps, core.dram
    with ExitStack() as own:
        def sb(name, shape, dt=F32):
            return core.sb(name, shape, dt, own)

        gate_w = sb("gate_w", [D, NE])
        gate_b = sb("gate_b", [S, NE])
        up = sb("expert_up", [D, 2, FF])
        up_bias = sb("expert_up_bias", [D, NE, FT])
        down = sb("expert_down", [D, 2, FT, D])
        b2 = sb("expert_b2", [NE, D])
        up_high, up_low = (sb(f"expert_up_{n}", [D, 2, FF], F16) for n in ("high", "low"))
        down_high, down_low = (sb(f"expert_down_{n}", [D, 2, FT, D], F16) for n in ("high", "low"))
        x_high, x_low = (sb(f"expert_x_{n}", [D, NTOK], F16) for n in ("high", "low"))
        hidden = sb("expert_hidden", [D, FT, NTOK])
        hidden_high, hidden_low = (sb(f"expert_hidden_{n}", [D, FT, NTOK], F16) for n in ("high", "low"))
        logits = sb("router_scores", [S, NB, NE])
        best = sb("router_best", [S, NB, NE])
        greater = sb("router_greater", [S, NB, NE, NE])
        equal = sb("router_equal", [S, NB, NE, NE])
        lower = sb("router_lower", [S, NE, NE])
        rank = sb("router_rank", [S, NB, NE])
        e2 = sb("router_second", [S, NB])
        w1 = sb("router_w1", [S, NB])
        w2 = sb("router_w2", [S, NB])
        comb = sb("router_weights", [S, NB, NE])
        second = sb("router_weights_second", [S, NB, NE])
        combT = sb("router_weightsT", [NE, NTOK])
        part = sb("expert_part", [S, NB, D])

        def load_expert(sp, e, u):
            loaded = sem(f"expert_weights_loaded{u}")
            sp.dma_start(up[:, u, :], dram["L1_ffn_w1"][bass.ds(e, 1), :, :].rearrange("o d f -> (o d) f")
                         ).then_inc(loaded, 16)
            sp.dma_start(down[:, u, :, :], dram["L1_ffn_w2"][bass.ds(e, 1), :, :].rearrange(
                "o (f p) d -> (o p) f d", p=D)).then_inc(loaded, 16)

        def over_features(ap):
            return ap.broadcast_to([S, NB, D])

        with nc.Block() as block:
            @block.sync
            def _(sp):
                sp.dma_start(gate_w[:, :], dram["L1_ffn_gate_w"]).then_inc(sem("router_loaded"), 16)
                sp.dma_start(gate_b[:, :], dram["L1_ffn_gate_b"].rearrange("(o e) -> o e", o=1).broadcast_to([S, NE])
                             ).then_inc(sem("router_loaded"), 16)
                sp.dma_start(b2[:, :], dram["L1_ffn_b2"]).then_inc(sem("router_loaded"), 16)
                for e in range(2):
                    load_expert(sp, e, e)
                sp.dma_start(up_bias[:, :, :], dram["L1_ffn_b1"].rearrange("e (f p) -> p e f", p=D),
                             allow_slow_non_contiguous=True).then_inc(sem("expert_bias_loaded"), 16)
                with sp.Fori(0, NE // 2 - 1) as i:
                    for u in range(2):
                        sp.wait_ge(sem("expert_split"), 2 * i + u + 1)
                        load_expert(sp, 2 * i + u + 2, u)

            @block.gpsimd
            def _(pool):
                pool.memset(lower[:, :, :], 1.0).then_inc(sem("router_lower_ready"), 1)
                pool.wait_ge(sem("router_lower_ready"), 1)
                pool.affine_select(out=lower[:, :, :], in_=lower[:, :, :], compare_op=ALU.is_gt, fill=0.0, base=0,
                                   pattern=[[1, NE], [-1, NE]], channel_multiplier=0
                                   ).then_inc(sem("router_lower_ready"), 1)
                with pool.Fori(0, NE // 2) as i:
                    for u in range(2):
                        e = 2 * i + u
                        pool.wait_ge(sem("expert_used"), e + 1)
                        pool.wait_ge(sem(f"expert_weights_loaded{u}"), 32 * i + 32)
                        wait_apart(pool, sem("pool_waits"))
                        pool.tensor_copy(up_high[:, u, :], up[:, u, :]).then_inc(sem("expert_highs"), 1)
                        pool.tensor_copy(down_high[:, u, :, :], down[:, u, :, :]).then_inc(sem("expert_highs"), 1)
                        pool.wait_ge(sem("expert_highs"), 2 * e + 2)
                        pool.tensor_tensor(up_low[:, u, :], up[:, u, :], up_high[:, u, :], ALU.subtract)
                        pool.tensor_tensor(down_low[:, u, :, :], down[:, u, :, :], down_high[:, u, :, :],
                                           ALU.subtract).then_inc(sem("expert_split"), 1)

            @block.tensor
            def _(pe):
                project_tensor(core, pe)
                pe.wait_ge(sem("router_loaded"), 48)
                for b in range(NB):
                    ins = nc.tensor.matmul(ps[0:S, 6, NE * b:NE * (b + 1)], core.xT[:, b * S:(b + 1) * S], gate_w[:, :],
                                           start=True, stop=True)
                ins.then_inc(sem("router_psum"), 1)
                pe.wait_ge(sem("expert_x_split"), 1)
                with pe.Fori(0, NE // 2) as i:
                    for u in range(2):
                        e = 2 * i + u
                        pe.wait_ge(sem("expert_split"), e + 1)
                        for f in range(FT):
                            pe.wait_ge(sem("expert_hidden_free"), FT * e + f + 1)
                            for k, (left, right) in enumerate(((up_high, x_high), (up_high, x_low), (up_low, x_high))):
                                for c in range(2):
                                    ins = nc.tensor.matmul(ps[:, 2 * (f % 2) + c, 0:HALF], left[:, u, D * f:D * f + D],
                                                           right[:, c * HALF:(c + 1) * HALF],
                                                           start=(k == 0), stop=(k == 2))
                            ins.then_inc(sem("expert_hidden_psum"), 1)
                        pe.wait_ge(sem("expert_out_free"), e + 1)
                        for f in range(FT):
                            pe.wait_ge(sem("expert_hidden_split"), FT * e + f + 1)
                            for b in range(NB):
                                out = ps[0:S, 4 + b // 4, D * (b % 4):D * (b % 4 + 1)]
                                for k, (left, right) in enumerate(((hidden_high, down_high), (hidden_low, down_high),
                                                                   (hidden_high, down_low))):
                                    ins = nc.tensor.matmul(out, left[:, f, b * S:(b + 1) * S], right[:, u, f, :],
                                                           start=(f == 0 and k == 0 and b % 4 == 0),
                                                           stop=(f == FT - 1 and k == 2), skip_group_check=True)
                        ins.then_inc(sem("expert_out_psum"), 1)
                pe.wait_ge(sem("router_weights_ready"), 1)
                for b in range(NB):
                    ins = nc.tensor.transpose(ps[0:NE, 6 + b // 4, (b % 4) * S:(b % 4 + 1) * S], comb[:, b, :],
                                              core.ident[0:S, 0:S])
                ins.then_inc(sem("router_weightsT_psum"), 1)
                pe.wait_ge(sem("router_weightsT_ready"), 1)
                for b in range(NB):
                    ins = nc.tensor.matmul(ps[0:S, b // 4, D * (b % 4):D * (b % 4 + 1)], combT[:, b * S:(b + 1) * S],
                                           b2[:, :], start=True, stop=True)
                ins.then_inc(sem("expert_bias_psum"), 1)

            @block.scalar
            def _(act):
                project_scalar(core, act)
                act.sem_inc(sem("expert_hidden_free"), 2)
                nc.scalar.activation(x_high[:, :], core.xT[:, :], ACT.Copy).then_inc(sem("expert_x_high_ready"), 1)
                act.wait_ge(sem("expert_bias_loaded"), 16)
                act.wait_ge(sem("router_gap_ready"), 1)
                nc.scalar.activation(e2[:, :], e2[:, :], ACT.Exp).then_inc(sem("router_exp_ready"), 1)
                with act.Fori(0, NE // 2) as i:
                    for u in range(2):
                        e = 2 * i + u
                        act.wait_ge(sem("expert_out_psum"), e + 1)
                        for f in range(FT):
                            act.wait_ge(sem("expert_hidden_psum"), FT * e + f + 1)
                            nc.scalar.activation(halves(hidden[:, f, :], HALF),
                                                 ps[:, 2 * (f % 2):2 * (f % 2) + 2, 0:HALF], ACT.Relu,
                                                 bias=up_bias[:, bass.ds(e, 1), f:f + 1].rearrange("d o f -> d (o f)")
                                                 ).then_inc(sem("expert_hidden_free"), 1)
                            act.wait_ge(sem("expert_hidden_free"), FT * e + f + 1 + 2)
                            nc.scalar.activation(hidden_high[:, f, :], hidden[:, f, :], ACT.Copy
                                                 ).then_inc(sem("expert_hidden_high"), 1)
                act.wait_ge(sem("router_weightsT_psum"), 1)
                nc.scalar.activation(halves(combT[:, :], HALF), ps[0:NE, 6:8, 0:HALF], ACT.Copy
                                     ).then_inc(sem("router_weightsT_ready"), 1)

            @block.vector
            def _(dve):
                dve.sem_inc(sem("expert_used"), 2)
                project_vector(core, dve)
                dve.sem_inc(sem("expert_out_free"), 1)
                dve.sem_inc(sem("expert_out_psum"), 1)
                link = chain(core, dve, "vector_steps")
                dve.wait_ge(sem("expert_x_high_ready"), 1)
                nc.vector.tensor_tensor(x_low[:, :], core.xT[:, :], x_high[:, :], ALU.subtract
                                        ).then_inc(sem("expert_x_split"), 1)
                dve.wait_ge(sem("router_psum"), 1)
                link(nc.vector.tensor_tensor(logits[:, :, :], ps[0:S, 6, 0:NB * NE].rearrange("s (b e) -> s b e", e=NE),
                                             gate_b[:, :].unsqueeze(1).broadcast_to([S, NB, NE]), ALU.add))
                for b in range(NB):
                    ins = nc.vector.max(best[:, b, :], logits[:, b, :])
                link(ins)
                nc.vector.tensor_tensor(e2[:, :], best[:, :, 1], best[:, :, 0], ALU.subtract
                                        ).then_inc(sem("router_gap_ready"), 1)
                dve.wait_ge(sem("router_lower_ready"), 2)
                for b in range(NB):
                    other = logits[:, b, :].unsqueeze(1).broadcast_to([S, NE, NE])
                    mine = logits[:, b, :].unsqueeze(2).broadcast_to([S, NE, NE])
                    nc.vector.tensor_tensor(greater[:, b, :, :], other, mine, ALU.is_gt)
                    ins = nc.vector.tensor_tensor(equal[:, b, :, :], other, mine, ALU.is_equal)
                link(ins)
                link(nc.vector.tensor_tensor(
                    equal[:, :, :, :].rearrange("s b e f -> s b (e f)"), equal[:, :, :, :].rearrange("s b e f -> s b (e f)"),
                    lower[:, :, :].rearrange("s e f -> s (e f)").unsqueeze(1).broadcast_to([S, NB, NE * NE]), ALU.mult))
                link(nc.vector.tensor_tensor(greater[:, :, :, :].rearrange("s b e f -> s (b e f)"),
                                             greater[:, :, :, :].rearrange("s b e f -> s (b e f)"),
                                             equal[:, :, :, :].rearrange("s b e f -> s (b e f)"), ALU.add))
                link(nc.vector.tensor_reduce(rank[:, :, :], greater[:, :, :, :], AX_X, ALU.add))
                dve.wait_ge(sem("router_exp_ready"), 1)
                link(nc.vector.tensor_scalar(w1[:, :], e2[:, :], 1.0, None, ALU.add))
                link(nc.vector.reciprocal(w1[:, :], w1[:, :]))
                link(nc.vector.tensor_tensor(w2[:, :], e2[:, :], w1[:, :], ALU.mult))
                nc.vector.tensor_scalar(comb[:, :, :], rank[:, :, :], 0.0, None, ALU.is_equal)
                link(nc.vector.tensor_scalar(second[:, :, :], rank[:, :, :], 1.0, None, ALU.is_equal))
                link(nc.vector.tensor_tensor(comb[:, :, :], comb[:, :, :],
                                             w1[:, :].unsqueeze(2).broadcast_to([S, NB, NE]), ALU.mult))
                link(nc.vector.tensor_tensor(second[:, :, :], second[:, :, :],
                                             w2[:, :].unsqueeze(2).broadcast_to([S, NB, NE]), ALU.mult))
                link(nc.vector.tensor_tensor(comb[:, :, :], comb[:, :, :], second[:, :, :], ALU.add))
                dve.sem_inc(sem("router_weights_ready"), 1)
                link(nc.vector.memset(core.work[:, :, :], 0.0))

                with dve.Fori(0, NE // 2) as i:
                    for u in range(2):
                        e = 2 * i + u
                        for f in range(FT):
                            dve.wait_ge(sem("expert_hidden_high"), FT * e + f + 1)
                            nc.vector.tensor_tensor(hidden_low[:, f, :], hidden[:, f, :], hidden_high[:, f, :],
                                                    ALU.subtract).then_inc(sem("expert_hidden_split"), 1)
                        dve.wait_ge(sem("expert_out_psum"), e + 2)
                        dve.sem_inc(sem("expert_used"), 1)
                        nc.vector.tensor_tensor(part[:, :, :], token_banks(core, 4), over_features(comb[:, :, bass.ds(e, 1)]),
                                                ALU.mult).then_inc(sem("expert_out_free"), 1)
                        dve.wait_ge(sem("expert_out_free"), e + 2)
                        nc.vector.tensor_tensor(core.work[:, :, :], core.work[:, :, :], part[:, :, :], ALU.add
                                                ).then_inc(sem("expert_added"), 1)
                        dve.wait_ge(sem("expert_added"), e + 1)
                dve.wait_ge(sem("expert_bias_psum"), 1)
                link(nc.vector.tensor_tensor(core.work[:, :, :], core.work[:, :, :], token_banks(core, 0), ALU.add))
                add_gated(core, link, 3, core.work)


INPUTS = ["x", "ctx_1024", "mask_BxSxS2_bf1", "g_xattn", "g_ffn"] + [
    f"L0_xattn_{n}" for n in ("Wq1", "Wk1", "Wv1", "bv1", "Wq2", "Wk2", "Wv2", "bv2", "g1", "be1", "g2", "be2", "g3",
                              "be3", "Wf1", "bf1", "Wf2", "bf2")] + [
    f"L0_ffn_{n}" for n in ("w1", "b1", "w2", "b2", "gamma", "beta")] + [
    f"L1_xattn_{n}" for n in ("Wq", "Wk", "Wv", "Wo")] + [
    f"L1_ffn_{n}" for n in ("gate_w", "gate_b", "w1", "b1", "w2", "b2")]


def store_phase(core, what):
    nc, sem = core.nc, core.sem
    with nc.Block() as block:
        @block.sync
        def _(sp):
            sp.dma_start(core.out.rearrange("b s d -> s b d"), what[:, :, :]).then_inc(sem("out_stored"), 16)
            sp.wait_ge(sem("out_stored"), 16)


def program(nc, dram, out):
    with ExitStack() as stack:
        core = Core(nc, stack, dram, out)
        core.merged_qk = core.sb("merged_qk", [D, H, D])
        core.merged_vo = core.sb("merged_vo", [D, H, D])
        core.mask_raw = core.sb("x1_mask_raw", [S, 2, T], U8)
        core.masked = core.sb("x1_masked", [S + SHIFT, 2, T], F16)
        core.select = core.sb("x1_select", [S + SHIFT, 2, H, S], F16)
        core.ones = core.sb("x1_ones", [128, 1])
        core.boost = core.sb("x1_boost", [128, 1])
        with ExitStack() as layer0:
            setup_phase(core, layer0)
            self_attention_phase(core)
            finish_attention_phase(core, "self")
            cross_attention_0_phase(core)
            finish_attention_phase(core, "cross")
            feed_forward_phase(core, "ffn", core.row["bf2"], core.row["g3"], core.row["be3"], 0)
            feed_forward_phase(core, "expert0", core.row_e["b2"], core.row_e["gamma"], core.row_e["beta"], 2)
        core.averages = core.sb("averages", [D, NB, H * S])
        core.inverse = core.sb("inverse_sums", [S, NB, H])
        cross_attention_1_phase(core)
        experts_phase(core)
        store_phase(core, core.x)


def kernel(**inputs):
    import numpy as _np
    import concourse.bacc as _bacc
    from concourse import mybir as _mybir
    from concourse.bass_utils import run_bass_kernel_spmd as _run

    nc = _bacc.Bacc("TRN2", target_bir_lowering=False, num_devices=1)
    arrays, dram = {}, {}
    for name in INPUTS:
        a = _np.ascontiguousarray(inputs[name])
        if a.dtype == _np.bool_:
            a = a.view(_np.uint8)
        arrays[f"in_{name}"] = a
        dram[name] = nc.dram_tensor(f"in_{name}", a.shape, _mybir.dt.from_np(a.dtype), kind="ExternalInput").ap()
    out = nc.dram_tensor("out_x", (NB, S, D), _mybir.dt.float32, kind="ExternalOutput").ap()
    program(nc, dram, out)
    return _run(nc, [arrays], core_ids=[0]).results[0]["out_x"]
```
